# Optimizing a Trainium2 kernel written in Bass

```python
import numpy as np
import jax
import jax.numpy as jnp

def _softmax(x, axis=-1):
    return jax.nn.softmax(x, axis=axis)

def _gelu(x):
    return jax.nn.gelu(x, approximate=True)

def _silu(x):
    return jax.nn.silu(x)

def _sigmoid(x):
    return jax.nn.sigmoid(x)

def _layernorm(x, axis=-1, eps=1e-05):
    m = jnp.mean(x, axis=axis, keepdims=True)
    v = jnp.var(x, axis=axis, keepdims=True)
    return (x - m) / jnp.sqrt(v + eps)

def _scatter_add(tgt, idx, src, axis=0):
    return tgt.at[idx].add(src)

def _segment_sum(src, seg, n):
    return jax.ops.segment_sum(src, seg, n)
kernel_name = 'mk_hybrid_d2_jaxref_r8_4de81f'

def setup_inputs(seed: int=0):
    np.random.seed(seed)
    _w = jnp.asarray

    def _L0_attn_a_setup():
        import jax, jax.numpy as jnp
        import numpy as np
        import math
        B, T, C = (8, 256, 128)
        H, D = (16, 64)

        def _l2norm(v, axis=-1, eps=1e-12):
            n = jnp.sqrt(jnp.sum(v * v, axis=axis, keepdims=True))
            return v / jnp.maximum(n, eps)

        def _reference_tuple_inner(x, W_r, b_r, W_k, b_k, W_v, b_v, W_g, b_g, W_o, b_o, decay, eta, time_mix_r, time_mix_k, time_mix_v, time_mix_g, gn_weight, gn_bias):
            Bx, Tx, Cx = x.shape
            Hh = decay.shape[0]
            Dd = Cx // Hh
            x_shift = jnp.concatenate([jnp.zeros_like(x[:, :1]), x[:, :-1]], axis=1)
            x_r = x * time_mix_r + x_shift * (1 - time_mix_r)
            x_k = x * time_mix_k + x_shift * (1 - time_mix_k)
            x_v = x * time_mix_v + x_shift * (1 - time_mix_v)
            x_g = x * time_mix_g + x_shift * (1 - time_mix_g)
            r = jax.nn.sigmoid(x_r @ W_r.T + b_r).reshape(Bx, Tx, Hh, Dd)
            k = (x_k @ W_k.T + b_k).reshape(Bx, Tx, Hh, Dd)
            v = (x_v @ W_v.T + b_v).reshape(Bx, Tx, Hh, Dd)
            g = jax.nn.silu(x_g @ W_g.T + b_g)
            k = _l2norm(k)
            v = _l2norm(v)
            dec = jax.nn.sigmoid(decay)
            et = jax.nn.sigmoid(eta)
            max_norm = math.sqrt(Dd) * 2.0
            rs = jnp.transpose(r, (1, 0, 2, 3))
            ks_ = jnp.transpose(k, (1, 0, 2, 3))
            vs = jnp.transpose(v, (1, 0, 2, 3))

            def step(state, rkv):
                r_t, k_t, v_t = rkv
                pred = jnp.einsum('bhij,bhj->bhi', state, k_t)
                err = pred - v_t
                state = dec * state - et * (err[..., :, None] * k_t[..., None, :])
                n = jnp.maximum(jnp.sqrt(jnp.sum(state * state, axis=(-2, -1), keepdims=True)), 1e-08)
                state = state * jnp.where(n > max_norm, max_norm / n, 1.0)
                wkv = jnp.einsum('bhij,bhj->bhi', state, r_t)
                return (state, wkv)
            state0 = jnp.zeros((Bx, Hh, Dd, Dd), jnp.float32)
            state, wkv = jax.lax.scan(step, state0, (rs, ks_, vs))
            wkv = jnp.transpose(wkv, (1, 0, 2, 3))
            mean = jnp.mean(wkv, axis=(1, 3), keepdims=True)
            var = jnp.mean(jnp.square(wkv - mean), axis=(1, 3), keepdims=True)
            wkv_n = ((wkv - mean) / jnp.sqrt(var + 1e-05)).reshape(Bx, Tx, Cx)
            wkv_n = wkv_n * gn_weight + gn_bias
            out = (wkv_n @ W_o.T + b_o) * g
            last_x = x[:, -1:, :]
            return (out, state, last_x)
        key = jax.random.key(seed)
        ks = jax.random.split(key, 20)
        s = 1.0 / math.sqrt(C)
        inp = {'x': jax.random.normal(ks[0], (B, T, C), dtype=jnp.float32), 'W_r': jax.random.normal(ks[1], (C, C), dtype=jnp.float32) * s, 'b_r': jnp.zeros((C,), jnp.float32), 'W_k': jax.random.normal(ks[2], (C, C), dtype=jnp.float32) * s, 'b_k': jnp.zeros((C,), jnp.float32), 'W_v': jax.random.normal(ks[3], (C, C), dtype=jnp.float32) * s, 'b_v': jnp.zeros((C,), jnp.float32), 'W_g': jax.random.normal(ks[4], (C, C), dtype=jnp.float32) * s, 'b_g': jnp.zeros((C,), jnp.float32), 'W_o': jax.random.normal(ks[5], (C, C), dtype=jnp.float32) * s, 'b_o': jnp.zeros((C,), jnp.float32), 'decay': jax.random.uniform(ks[6], (H, 1, 1), jnp.float32, 2.0, 4.0), 'eta': jax.random.uniform(ks[7], (H, 1, 1), jnp.float32, -3.0, -1.0), 'time_mix_r': jnp.full((1, 1, C), 0.5, jnp.float32), 'time_mix_k': jnp.full((1, 1, C), 0.5, jnp.float32), 'time_mix_v': jnp.full((1, 1, C), 0.5, jnp.float32), 'time_mix_g': jnp.full((1, 1, C), 0.5, jnp.float32), 'gn_weight': jnp.ones((C,), jnp.float32), 'gn_bias': jnp.zeros((C,), jnp.float32)}
        return inp
    _L0_attn_a_in = _L0_attn_a_setup()

    def _L0_attn_b_setup():
        import jax, jax.numpy as jnp
        import numpy as np
        D_MODEL = 128
        N_HEAD = 16
        N_BR = 4
        DH = D_MODEL // N_HEAD
        H_TOT = N_BR * N_HEAD
        SCALE = float(np.pi / np.sqrt(3.0))
        ATTN_SCALE = DH ** (-0.5)

        def _rope(x):
            B, H, T, Dh = x.shape
            inv_freq = 1.0 / 10000.0 ** (jnp.arange(0, Dh, 2, dtype=jnp.float32) / Dh)
            t = jnp.arange(T, dtype=jnp.float32)
            freqs = t[:, None] * inv_freq[None, :]
            cos = jnp.cos(freqs)[None, None]
            sin = jnp.sin(freqs)[None, None]
            x1 = x[..., 0::2]
            x2 = x[..., 1::2]
            return jnp.concatenate([-x2 * sin + x1 * cos, x1 * sin + x2 * cos], axis=-1)
        if __name__ == '__main__':
            out = reference(**setup_inputs())
            print(out.shape)
        key = jax.random.key(seed)
        ks = jax.random.split(key, 8)
        s = 0.02
        B, T = (1, 128)
        return {'X': jax.random.normal(ks[0], (B, T, D_MODEL), jnp.float32), 'Wq': jax.random.normal(ks[1], (D_MODEL, H_TOT * DH), jnp.float32) * s, 'bq': jnp.zeros((H_TOT * DH,), jnp.float32), 'Wk': jax.random.normal(ks[2], (D_MODEL, D_MODEL), jnp.float32) * s, 'bk': jnp.zeros((D_MODEL,), jnp.float32), 'Wv': jax.random.normal(ks[3], (D_MODEL, H_TOT * DH), jnp.float32) * s, 'bv': jnp.zeros((H_TOT * DH,), jnp.float32), 'sink_scalars': jax.random.normal(ks[4], (H_TOT, 1, 1), jnp.float32) * s, 'v_nulls': jax.random.normal(ks[5], (H_TOT, DH), jnp.float32) * s, 'Wo': jax.random.normal(ks[6], (D_MODEL, D_MODEL), jnp.float32) * s, 'bo': jnp.zeros((D_MODEL,), jnp.float32)}
    _L0_attn_b_in = _L0_attn_b_setup()

    def _L0_ffn_setup():
        import jax, jax.numpy as jnp
        import numpy as np
        DIM = 128
        DEPTH = 6
        HEADS = 16
        DIM_HEAD = 64
        WINDOW = 32
        INNER = HEADS * DIM_HEAD
        DIM_INNER = int(DIM * 4 * 2 / 3)
        QK_SCALE = 8.0

        def shift_tokens(t):
            a, s = jnp.split(t, 2, -1)
            s = jnp.pad(s, ((0, 0), (1, 0), (0, 0)))[:, :-1]
            return jnp.concatenate([a, s], -1)

        def l2norm(t):
            return t / jnp.maximum(jnp.linalg.norm(t, axis=-1, keepdims=True), 1e-12)

        def rotate_half(x):
            x1, x2 = jnp.split(x, 2, -1)
            return jnp.concatenate([-x2, x1], -1)

        def rotary_tables(n):
            half = jnp.arange(0, DIM_HEAD, 2, dtype=jnp.float32)
            inv_freq = 1.0 / 10000.0 ** (half / DIM_HEAD)
            t = jnp.arange(n, dtype=jnp.float32)
            freqs = t[:, None] * inv_freq[None, :]
            freqs = jnp.concatenate([freqs, freqs], -1)
            base_scale = (half + 0.4 * DIM_HEAD) / (1.4 * DIM_HEAD)
            power = (t - n // 2) / (WINDOW // 2)
            scale = base_scale[None, :] ** power[:, None]
            scale = jnp.concatenate([scale, scale], -1)
            return (freqs, scale)

        def local_attention(q, k, v):
            b, h, n, d = q.shape
            w = WINDOW
            nw = n // w
            bq = q.reshape(b, h, nw, w, d)
            bk = k.reshape(b, h, nw, w, d)
            bv = v.reshape(b, h, nw, w, d)

            def look(t):
                p = jnp.pad(t, ((0, 0), (0, 0), (1, 0), (0, 0), (0, 0)))
                return jnp.concatenate([p[:, :, :nw], p[:, :, 1:]], axis=3)
            bk2, bv2 = (look(bk), look(bv))
            seq = jnp.arange(n).reshape(nw, w)
            seq_p = jnp.pad(seq, ((1, 0), (0, 0)), constant_values=-1)
            jt = jnp.concatenate([seq_p[:nw], seq_p[1:]], axis=1)
            it = seq[:, :, None]
            jb = jt[:, None, :]
            mask = (it < jb) | (it > jb + w) | (jb == -1)
            sim = jnp.einsum('bhwie,bhwje->bhwij', bq, bk2) * QK_SCALE
            sim = jnp.where(mask, -jnp.finfo(sim.dtype).max, sim)
            attn = jax.nn.softmax(sim, -1)
            out = jnp.einsum('bhwij,bhwje->bhwie', attn, bv2)
            return out.reshape(b, h, n, d)

        def attn_layer(x, Wqkv, qs, ksc, Wo):
            b, n, _ = x.shape
            qkv = x @ Wqkv
            q, k, v = jnp.split(qkv, 3, -1)
            sh = lambda t: t.reshape(b, n, HEADS, DIM_HEAD).transpose(0, 2, 1, 3)
            q, k, v = (sh(q), sh(k), sh(v))
            q = l2norm(q) * qs
            k = l2norm(k) * ksc
            freqs, scale = rotary_tables(n)
            cos, sin = (jnp.cos(freqs), jnp.sin(freqs))
            q = q * cos * scale + rotate_half(q) * sin * scale
            inv = 1.0 / scale
            k = k * cos * inv + rotate_half(k) * sin * inv
            out = local_attention(q, k, v)
            out = out.transpose(0, 2, 1, 3).reshape(b, n, INNER)
            return out @ Wo

        def ffn_layer(x, g, bln, W1, b1, W2, b2):
            mu = x.mean(-1, keepdims=True)
            var = ((x - mu) ** 2).mean(-1, keepdims=True)
            xn = (x - mu) / jnp.sqrt(var + 1e-05) * g + bln
            hg = xn @ W1 + b1
            a, gate = jnp.split(hg, 2, -1)
            return a * jax.nn.gelu(gate, approximate=False) @ W2 + b2
        key = jax.random.key(seed)
        ks = jax.random.split(key, 8)
        B, N = (2, 256)
        init = lambda k, shape: jax.random.normal(k, shape, jnp.float32) * 0.02
        return {'x': jax.random.normal(ks[0], (B, N, DIM), jnp.float32), 'Wqkv': init(ks[1], (DEPTH, DIM, 3 * INNER)), 'q_scale': jnp.ones((DEPTH, DIM_HEAD), jnp.float32), 'k_scale': jnp.ones((DEPTH, DIM_HEAD), jnp.float32), 'Wo': init(ks[2], (DEPTH, INNER, DIM)), 'ln_g': jnp.ones((DEPTH, DIM), jnp.float32), 'ln_b': jnp.zeros((DEPTH, DIM), jnp.float32), 'W1': init(ks[3], (DEPTH, DIM, 2 * DIM_INNER)), 'b1': jnp.zeros((DEPTH, 2 * DIM_INNER), jnp.float32), 'W2': init(ks[4], (DEPTH, DIM_INNER, DIM)), 'b2': jnp.zeros((DEPTH, DIM), jnp.float32)}
    _L0_ffn_in = _L0_ffn_setup()

    def _L1_attn_a_setup():
        import jax, jax.numpy as jnp
        import numpy as np
        B, L, D = (4, 512, 128)
        EPS_NORM = 1e-06
        EPS_PHAZOR = 1e-05
        key = jax.random.key(seed)
        ks = jax.random.split(key, 8)
        gain = 0.01 * np.sqrt(2.0 / (D + D))
        inp = {'x': jax.random.normal(ks[0], (B, L, D), dtype=jnp.float32), 'Wz': jax.random.normal(ks[1], (D, D), dtype=jnp.float32) * gain, 'bz': jnp.zeros((D,), jnp.float32), 'Wza': jax.random.normal(ks[2], (D, D), dtype=jnp.float32) * gain, 'bza': jnp.zeros((D,), jnp.float32), 'Wy': jax.random.normal(ks[3], (D, D), dtype=jnp.float32) * gain, 'by': jnp.zeros((D,), jnp.float32), 'Wya': jax.random.normal(ks[4], (D, D), dtype=jnp.float32) * gain, 'bya': jnp.zeros((D,), jnp.float32), 'norm_w': jnp.ones((D,), jnp.float32), 'lc_re': jax.random.normal(ks[5], (D,), dtype=jnp.float32), 'lc_im': jax.random.normal(ks[6], (D,), dtype=jnp.float32)}
        return inp
    _L1_attn_a_in = _L1_attn_a_setup()

    def _L1_attn_b_setup():
        import jax, jax.numpy as jnp
        import numpy as np
        import math
        B, S, HID = (2, 256, 128)
        NH = 16
        HD = HID // NH
        key = jax.random.key(seed)
        ks = jax.random.split(key, 5)
        std = 1.0 / math.sqrt(HID)
        return {'x': jax.random.normal(ks[0], (B, S, HID), dtype=jnp.float32), 'wq': jax.random.normal(ks[1], (HID, HID), dtype=jnp.float32) * std, 'wk': jax.random.normal(ks[2], (HID, HID), dtype=jnp.float32) * std, 'wv': jax.random.normal(ks[3], (HID, HID), dtype=jnp.float32) * std, 'wo': jax.random.normal(ks[4], (HID, HID), dtype=jnp.float32) * std}
    _L1_attn_b_in = _L1_attn_b_setup()

    def _L1_ffn_setup():
        import jax, jax.numpy as jnp
        import numpy as np
        from functools import partial
        HEADS = 16
        EPS = 1e-12

        def _l2_normalize(z):
            n = jnp.linalg.norm(z, axis=-1, keepdims=True)
            return z / jnp.maximum(n, EPS)
        key = jax.random.key(seed)
        kx, kq, kk, kv, ko, kf = jax.random.split(key, 6)
        B, S, D, L = (2, 256, 128, 128)
        scale = 0.02
        return {'x': jax.random.normal(kx, (B, S, D), dtype=jnp.float32), 'Wq': jax.random.normal(kq, (D, L), dtype=jnp.float32) * scale, 'Wk': jax.random.normal(kk, (D, L), dtype=jnp.float32) * scale, 'Wv': jax.random.normal(kv, (D, L), dtype=jnp.float32) * scale, 'Wo': jax.random.normal(ko, (L, D), dtype=jnp.float32) * scale, 'Wff': jax.random.normal(kf, (D, D), dtype=jnp.float32) * scale}
    _L1_ffn_in = _L1_ffn_setup()
    _d = {'L0_attn_a_x': _L0_attn_a_in['x'], 'L0_attn_a_W_r': _L0_attn_a_in['W_r'], 'L0_attn_a_b_r': _L0_attn_a_in['b_r'], 'L0_attn_a_W_k': _L0_attn_a_in['W_k'], 'L0_attn_a_b_k': _L0_attn_a_in['b_k'], 'L0_attn_a_W_v': _L0_attn_a_in['W_v'], 'L0_attn_a_b_v': _L0_attn_a_in['b_v'], 'L0_attn_a_W_g': _L0_attn_a_in['W_g'], 'L0_attn_a_b_g': _L0_attn_a_in['b_g'], 'L0_attn_a_W_o': _L0_attn_a_in['W_o'], 'L0_attn_a_b_o': _L0_attn_a_in['b_o'], 'L0_attn_a_decay': _L0_attn_a_in['decay'], 'L0_attn_a_eta': _L0_attn_a_in['eta'], 'L0_attn_a_time_mix_r': _L0_attn_a_in['time_mix_r'], 'L0_attn_a_time_mix_k': _L0_attn_a_in['time_mix_k'], 'L0_attn_a_time_mix_v': _L0_attn_a_in['time_mix_v'], 'L0_attn_a_time_mix_g': _L0_attn_a_in['time_mix_g'], 'L0_attn_a_gn_weight': _L0_attn_a_in['gn_weight'], 'L0_attn_a_gn_bias': _L0_attn_a_in['gn_bias'], 'L0_attn_b_Wq': _L0_attn_b_in['Wq'], 'L0_attn_b_bq': _L0_attn_b_in['bq'], 'L0_attn_b_Wk': _L0_attn_b_in['Wk'], 'L0_attn_b_bk': _L0_attn_b_in['bk'], 'L0_attn_b_Wv': _L0_attn_b_in['Wv'], 'L0_attn_b_bv': _L0_attn_b_in['bv'], 'L0_attn_b_sink_scalars': _L0_attn_b_in['sink_scalars'], 'L0_attn_b_v_nulls': _L0_attn_b_in['v_nulls'], 'L0_attn_b_Wo': _L0_attn_b_in['Wo'], 'L0_attn_b_bo': _L0_attn_b_in['bo'], 'L0_ffn_Wqkv': _L0_ffn_in['Wqkv'], 'L0_ffn_q_scale': _L0_ffn_in['q_scale'], 'L0_ffn_k_scale': _L0_ffn_in['k_scale'], 'L0_ffn_Wo': _L0_ffn_in['Wo'], 'L0_ffn_ln_g': _L0_ffn_in['ln_g'], 'L0_ffn_ln_b': _L0_ffn_in['ln_b'], 'L0_ffn_W1': _L0_ffn_in['W1'], 'L0_ffn_b1': _L0_ffn_in['b1'], 'L0_ffn_W2': _L0_ffn_in['W2'], 'L0_ffn_b2': _L0_ffn_in['b2'], 'L1_attn_a_Wz': _L1_attn_a_in['Wz'], 'L1_attn_a_bz': _L1_attn_a_in['bz'], 'L1_attn_a_Wza': _L1_attn_a_in['Wza'], 'L1_attn_a_bza': _L1_attn_a_in['bza'], 'L1_attn_a_Wy': _L1_attn_a_in['Wy'], 'L1_attn_a_by': _L1_attn_a_in['by'], 'L1_attn_a_Wya': _L1_attn_a_in['Wya'], 'L1_attn_a_bya': _L1_attn_a_in['bya'], 'L1_attn_a_norm_w': _L1_attn_a_in['norm_w'], 'L1_attn_a_lc_re': _L1_attn_a_in['lc_re'], 'L1_attn_a_lc_im': _L1_attn_a_in['lc_im'], 'L1_attn_b_wq': _L1_attn_b_in['wq'], 'L1_attn_b_wk': _L1_attn_b_in['wk'], 'L1_attn_b_wv': _L1_attn_b_in['wv'], 'L1_attn_b_wo': _L1_attn_b_in['wo'], 'L1_ffn_Wq': _L1_ffn_in['Wq'], 'L1_ffn_Wk': _L1_ffn_in['Wk'], 'L1_ffn_Wv': _L1_ffn_in['Wv'], 'L1_ffn_Wo': _L1_ffn_in['Wo'], 'L1_ffn_Wff': _L1_ffn_in['Wff']}
    _x0 = _d['L0_attn_a_x']
    _d['L0_attn_a_x'] = jax.random.normal(jax.random.fold_in(jax.random.key(seed), 1), (8, 256, 128), dtype=_x0.dtype)
    del _x0
    return _d

def reference(L0_attn_a_x, L0_attn_a_W_r, L0_attn_a_b_r, L0_attn_a_W_k, L0_attn_a_b_k, L0_attn_a_W_v, L0_attn_a_b_v, L0_attn_a_W_g, L0_attn_a_b_g, L0_attn_a_W_o, L0_attn_a_b_o, L0_attn_a_decay, L0_attn_a_eta, L0_attn_a_time_mix_r, L0_attn_a_time_mix_k, L0_attn_a_time_mix_v, L0_attn_a_time_mix_g, L0_attn_a_gn_weight, L0_attn_a_gn_bias, L0_attn_b_Wq, L0_attn_b_bq, L0_attn_b_Wk, L0_attn_b_bk, L0_attn_b_Wv, L0_attn_b_bv, L0_attn_b_sink_scalars, L0_attn_b_v_nulls, L0_attn_b_Wo, L0_attn_b_bo, L0_ffn_Wqkv, L0_ffn_q_scale, L0_ffn_k_scale, L0_ffn_Wo, L0_ffn_ln_g, L0_ffn_ln_b, L0_ffn_W1, L0_ffn_b1, L0_ffn_W2, L0_ffn_b2, L1_attn_a_Wz, L1_attn_a_bz, L1_attn_a_Wza, L1_attn_a_bza, L1_attn_a_Wy, L1_attn_a_by, L1_attn_a_Wya, L1_attn_a_bya, L1_attn_a_norm_w, L1_attn_a_lc_re, L1_attn_a_lc_im, L1_attn_b_wq, L1_attn_b_wk, L1_attn_b_wv, L1_attn_b_wo, L1_ffn_Wq, L1_ffn_Wk, L1_ffn_Wv, L1_ffn_Wo, L1_ffn_Wff):

    def _L0_attn_a_ref(x, W_r, b_r, W_k, b_k, W_v, b_v, W_g, b_g, W_o, b_o, decay, eta, time_mix_r, time_mix_k, time_mix_v, time_mix_g, gn_weight, gn_bias):
        import jax, jax.numpy as jnp
        import numpy as np
        import math
        B, T, C = (8, 256, 128)
        H, D = (16, 64)

        def _l2norm(v, axis=-1, eps=1e-12):
            n = jnp.sqrt(jnp.sum(v * v, axis=axis, keepdims=True))
            return v / jnp.maximum(n, eps)

        def _reference_tuple_inner(x, W_r, b_r, W_k, b_k, W_v, b_v, W_g, b_g, W_o, b_o, decay, eta, time_mix_r, time_mix_k, time_mix_v, time_mix_g, gn_weight, gn_bias):
            Bx, Tx, Cx = x.shape
            Hh = decay.shape[0]
            Dd = Cx // Hh
            x_shift = jnp.concatenate([jnp.zeros_like(x[:, :1]), x[:, :-1]], axis=1)
            x_r = x * time_mix_r + x_shift * (1 - time_mix_r)
            x_k = x * time_mix_k + x_shift * (1 - time_mix_k)
            x_v = x * time_mix_v + x_shift * (1 - time_mix_v)
            x_g = x * time_mix_g + x_shift * (1 - time_mix_g)
            r = jax.nn.sigmoid(x_r @ W_r.T + b_r).reshape(Bx, Tx, Hh, Dd)
            k = (x_k @ W_k.T + b_k).reshape(Bx, Tx, Hh, Dd)
            v = (x_v @ W_v.T + b_v).reshape(Bx, Tx, Hh, Dd)
            g = jax.nn.silu(x_g @ W_g.T + b_g)
            k = _l2norm(k)
            v = _l2norm(v)
            dec = jax.nn.sigmoid(decay)
            et = jax.nn.sigmoid(eta)
            max_norm = math.sqrt(Dd) * 2.0
            rs = jnp.transpose(r, (1, 0, 2, 3))
            ks_ = jnp.transpose(k, (1, 0, 2, 3))
            vs = jnp.transpose(v, (1, 0, 2, 3))

            def step(state, rkv):
                r_t, k_t, v_t = rkv
                pred = jnp.einsum('bhij,bhj->bhi', state, k_t)
                err = pred - v_t
                state = dec * state - et * (err[..., :, None] * k_t[..., None, :])
                n = jnp.maximum(jnp.sqrt(jnp.sum(state * state, axis=(-2, -1), keepdims=True)), 1e-08)
                state = state * jnp.where(n > max_norm, max_norm / n, 1.0)
                wkv = jnp.einsum('bhij,bhj->bhi', state, r_t)
                return (state, wkv)
            state0 = jnp.zeros((Bx, Hh, Dd, Dd), jnp.float32)
            state, wkv = jax.lax.scan(step, state0, (rs, ks_, vs))
            wkv = jnp.transpose(wkv, (1, 0, 2, 3))
            mean = jnp.mean(wkv, axis=(1, 3), keepdims=True)
            var = jnp.mean(jnp.square(wkv - mean), axis=(1, 3), keepdims=True)
            wkv_n = ((wkv - mean) / jnp.sqrt(var + 1e-05)).reshape(Bx, Tx, Cx)
            wkv_n = wkv_n * gn_weight + gn_bias
            out = (wkv_n @ W_o.T + b_o) * g
            last_x = x[:, -1:, :]
            return (out, state, last_x)
        return _reference_tuple_inner(x, W_r, b_r, W_k, b_k, W_v, b_v, W_g, b_g, W_o, b_o, decay, eta, time_mix_r, time_mix_k, time_mix_v, time_mix_g, gn_weight, gn_bias)[0]

    def _L0_attn_b_ref(X, Wq, bq, Wk, bk, Wv, bv, sink_scalars, v_nulls, Wo, bo):
        import jax, jax.numpy as jnp
        import numpy as np
        D_MODEL = 128
        N_HEAD = 16
        N_BR = 4
        DH = D_MODEL // N_HEAD
        H_TOT = N_BR * N_HEAD
        SCALE = float(np.pi / np.sqrt(3.0))
        ATTN_SCALE = DH ** (-0.5)

        def _rope(x):
            B, H, T, Dh = x.shape
            inv_freq = 1.0 / 10000.0 ** (jnp.arange(0, Dh, 2, dtype=jnp.float32) / Dh)
            t = jnp.arange(T, dtype=jnp.float32)
            freqs = t[:, None] * inv_freq[None, :]
            cos = jnp.cos(freqs)[None, None]
            sin = jnp.sin(freqs)[None, None]
            x1 = x[..., 0::2]
            x2 = x[..., 1::2]
            return jnp.concatenate([-x2 * sin + x1 * cos, x1 * sin + x2 * cos], axis=-1)
        if __name__ == '__main__':
            out = reference(**setup_inputs())
            print(out.shape)
        B, T, C = X.shape
        q = (X @ Wq + bq).reshape(B, T, H_TOT, DH).transpose(0, 2, 1, 3)
        v = (X @ Wv + bv).reshape(B, T, H_TOT, DH).transpose(0, 2, 1, 3)
        k_base = (X @ Wk + bk).reshape(B, T, N_HEAD, DH).transpose(0, 2, 1, 3)
        k = jnp.tile(k_base, (1, N_BR, 1, 1))
        q = _rope(q)
        k = _rope(k)
        scores = jnp.einsum('bhtd,bhsd->bhts', q, k) * ATTN_SCALE
        key_self = jnp.clip(jnp.sum(k * k, axis=-1), 1e-06, None)
        denom = jnp.sqrt(key_self)[:, :, None, :]
        w = jax.nn.softplus(scores / denom)
        causal = jnp.tril(jnp.ones((T, T), dtype=bool))
        w = jnp.where(causal[None, None], w, 0.0)
        w = w * jax.nn.sigmoid(SCALE * w)
        sinks = jnp.tanh(sink_scalars).reshape(1, H_TOT, 1, 1) + 1e-06
        alpha = 1.0 / (jnp.sum(w, axis=-1, keepdims=True) + sinks + 1e-06)
        probs_tokens = w * alpha
        probs_sink = sinks * alpha
        out_tokens = jnp.einsum('bhts,bhsd->bhtd', probs_tokens, v)
        out_sinks = probs_sink * v_nulls[None, :, None, :]
        context = out_tokens + out_sinks
        context = context.reshape(B, N_BR, N_HEAD, T, DH)
        context = context.transpose(0, 1, 3, 2, 4).reshape(B, N_BR, T, C)
        y = context @ Wo + bo
        return jnp.mean(y, axis=1)

    def _L0_ffn_ref(x, Wqkv, q_scale, k_scale, Wo, ln_g, ln_b, W1, b1, W2, b2):
        import jax, jax.numpy as jnp
        import numpy as np
        DIM = 128
        DEPTH = 6
        HEADS = 16
        DIM_HEAD = 64
        WINDOW = 32
        INNER = HEADS * DIM_HEAD
        DIM_INNER = int(DIM * 4 * 2 / 3)
        QK_SCALE = 8.0

        def shift_tokens(t):
            a, s = jnp.split(t, 2, -1)
            s = jnp.pad(s, ((0, 0), (1, 0), (0, 0)))[:, :-1]
            return jnp.concatenate([a, s], -1)

        def l2norm(t):
            return t / jnp.maximum(jnp.linalg.norm(t, axis=-1, keepdims=True), 1e-12)

        def rotate_half(x):
            x1, x2 = jnp.split(x, 2, -1)
            return jnp.concatenate([-x2, x1], -1)

        def rotary_tables(n):
            half = jnp.arange(0, DIM_HEAD, 2, dtype=jnp.float32)
            inv_freq = 1.0 / 10000.0 ** (half / DIM_HEAD)
            t = jnp.arange(n, dtype=jnp.float32)
            freqs = t[:, None] * inv_freq[None, :]
            freqs = jnp.concatenate([freqs, freqs], -1)
            base_scale = (half + 0.4 * DIM_HEAD) / (1.4 * DIM_HEAD)
            power = (t - n // 2) / (WINDOW // 2)
            scale = base_scale[None, :] ** power[:, None]
            scale = jnp.concatenate([scale, scale], -1)
            return (freqs, scale)

        def local_attention(q, k, v):
            b, h, n, d = q.shape
            w = WINDOW
            nw = n // w
            bq = q.reshape(b, h, nw, w, d)
            bk = k.reshape(b, h, nw, w, d)
            bv = v.reshape(b, h, nw, w, d)

            def look(t):
                p = jnp.pad(t, ((0, 0), (0, 0), (1, 0), (0, 0), (0, 0)))
                return jnp.concatenate([p[:, :, :nw], p[:, :, 1:]], axis=3)
            bk2, bv2 = (look(bk), look(bv))
            seq = jnp.arange(n).reshape(nw, w)
            seq_p = jnp.pad(seq, ((1, 0), (0, 0)), constant_values=-1)
            jt = jnp.concatenate([seq_p[:nw], seq_p[1:]], axis=1)
            it = seq[:, :, None]
            jb = jt[:, None, :]
            mask = (it < jb) | (it > jb + w) | (jb == -1)
            sim = jnp.einsum('bhwie,bhwje->bhwij', bq, bk2) * QK_SCALE
            sim = jnp.where(mask, -jnp.finfo(sim.dtype).max, sim)
            attn = jax.nn.softmax(sim, -1)
            out = jnp.einsum('bhwij,bhwje->bhwie', attn, bv2)
            return out.reshape(b, h, n, d)

        def attn_layer(x, Wqkv, qs, ksc, Wo):
            b, n, _ = x.shape
            qkv = x @ Wqkv
            q, k, v = jnp.split(qkv, 3, -1)
            sh = lambda t: t.reshape(b, n, HEADS, DIM_HEAD).transpose(0, 2, 1, 3)
            q, k, v = (sh(q), sh(k), sh(v))
            q = l2norm(q) * qs
            k = l2norm(k) * ksc
            freqs, scale = rotary_tables(n)
            cos, sin = (jnp.cos(freqs), jnp.sin(freqs))
            q = q * cos * scale + rotate_half(q) * sin * scale
            inv = 1.0 / scale
            k = k * cos * inv + rotate_half(k) * sin * inv
            out = local_attention(q, k, v)
            out = out.transpose(0, 2, 1, 3).reshape(b, n, INNER)
            return out @ Wo

        def ffn_layer(x, g, bln, W1, b1, W2, b2):
            mu = x.mean(-1, keepdims=True)
            var = ((x - mu) ** 2).mean(-1, keepdims=True)
            xn = (x - mu) / jnp.sqrt(var + 1e-05) * g + bln
            hg = xn @ W1 + b1
            a, gate = jnp.split(hg, 2, -1)
            return a * jax.nn.gelu(gate, approximate=False) @ W2 + b2
        for i in range(DEPTH):
            x = attn_layer(shift_tokens(x), Wqkv[i], q_scale[i], k_scale[i], Wo[i]) + x
            x = ffn_layer(shift_tokens(x), ln_g[i], ln_b[i], W1[i], b1[i], W2[i], b2[i]) + x
        return x

    def _L1_attn_a_ref(x, Wz, bz, Wza, bza, Wy, by, Wya, bya, norm_w, lc_re, lc_im):
        import jax, jax.numpy as jnp
        import numpy as np
        B, L, D = (4, 512, 128)
        EPS_NORM = 1e-06
        EPS_PHAZOR = 1e-05
        b, l, d = x.shape
        scale = jnp.power(jnp.float32(0.001), jnp.linspace(0.0, 1.0, d, dtype=jnp.float32))
        ln_phazor = EPS_PHAZOR + 1j * scale.astype(jnp.complex64)
        z = (x @ Wz.T + bz) * jax.nn.silu(x @ Wza.T + bza)
        z = z.astype(jnp.complex64)
        t = jnp.arange(l, dtype=jnp.float32)
        phazor_prog = jnp.exp(t[:, None].astype(jnp.complex64) * ln_phazor[None, :])
        phazor_fft = jnp.fft.fft(phazor_prog, n=2 * l, axis=0)
        z_fft = jnp.fft.fft(z, n=2 * l, axis=1)
        h_inner = jnp.fft.ifft(z_fft * phazor_fft[None], axis=1)[:, :l]
        last_conv = (lc_re + 1j * lc_im).astype(jnp.complex64)
        h_cross = last_conv[None, None, :] * (phazor_prog * jnp.exp(ln_phazor)[None, :])[None]
        h = (h_inner + h_cross).real
        normed = h * jax.lax.rsqrt(jnp.mean(h * h, axis=-1, keepdims=True) + EPS_NORM) * norm_w
        y = (normed @ Wy.T + by) * jax.nn.silu(x @ Wya.T + bya)
        return y

    def _L1_attn_b_ref(x, wq, wk, wv, wo):
        import jax, jax.numpy as jnp
        import numpy as np
        import math
        B, S, HID = (2, 256, 128)
        NH = 16
        HD = HID // NH
        b, s, _ = x.shape
        scale = 1.0 / math.sqrt(HD)

        def heads(t):
            return t.reshape(b, s, NH, HD).transpose(0, 2, 1, 3)
        q = heads(x @ wq.T)
        k = heads(x @ wk.T)
        v = heads(x @ wv.T)
        scores = jnp.einsum('bhqd,bhkd->bhqk', q, k) * scale
        q_idx = jnp.arange(s)[:, None]
        k_idx = jnp.arange(s)[None, :]
        causal_mask = k_idx > q_idx
        scores = jnp.where(causal_mask, -jnp.inf, scores)
        local_max = jnp.max(scores, axis=-1, keepdims=True)
        exp_scores = jnp.exp(scores - local_max)
        local_sum = jnp.sum(exp_scores, axis=-1, keepdims=True)
        attn_num = jnp.einsum('bhqk,bhkd->bhqd', exp_scores, v)
        attn_out = attn_num / (local_sum + 1e-08)
        attn_out = attn_out.transpose(0, 2, 1, 3).reshape(b, s, HID)
        return attn_out @ wo.T

    def _L1_ffn_ref(x, Wq, Wk, Wv, Wo, Wff):
        import jax, jax.numpy as jnp
        import numpy as np
        from functools import partial
        HEADS = 16
        EPS = 1e-12

        def _l2_normalize(z):
            n = jnp.linalg.norm(z, axis=-1, keepdims=True)
            return z / jnp.maximum(n, EPS)
        B, S, D = x.shape
        H = HEADS
        L = Wq.shape[1]
        dh = L // H

        def split_heads(t):
            return t.reshape(B, S, H, dh).transpose(0, 2, 1, 3).reshape(B * H, S, dh)
        q = split_heads(x @ Wq)
        k = split_heads(x @ Wk)
        v = split_heads(x @ Wv)
        scores = jnp.einsum('bqd,bkd->bkq', q, k) / jnp.sqrt(jnp.asarray(D, x.dtype))
        attn = jax.nn.softmax(scores, axis=-1)
        out = jnp.einsum('bkq,bkv->bqv', attn, v)
        z = out.reshape(B, H, S, dh).transpose(0, 2, 1, 3).reshape(B, S, L)
        z = z @ Wo
        z = _l2_normalize(z)
        z = z @ Wff
        z = _l2_normalize(z)
        z = jax.nn.gelu(z, approximate=False)
        return z
    x = L0_attn_a_x
    x = x + _L0_attn_a_ref(_layernorm(x, axis=-1), L0_attn_a_W_r, L0_attn_a_b_r, L0_attn_a_W_k, L0_attn_a_b_k, L0_attn_a_W_v, L0_attn_a_b_v, L0_attn_a_W_g, L0_attn_a_b_g, L0_attn_a_W_o, L0_attn_a_b_o, L0_attn_a_decay, L0_attn_a_eta, L0_attn_a_time_mix_r, L0_attn_a_time_mix_k, L0_attn_a_time_mix_v, L0_attn_a_time_mix_g, L0_attn_a_gn_weight, L0_attn_a_gn_bias)
    x = x + _L0_ffn_ref(_layernorm(x, axis=-1), L0_ffn_Wqkv, L0_ffn_q_scale, L0_ffn_k_scale, L0_ffn_Wo, L0_ffn_ln_g, L0_ffn_ln_b, L0_ffn_W1, L0_ffn_b1, L0_ffn_W2, L0_ffn_b2)
    x = x + _L0_attn_b_ref(_layernorm(x, axis=-1), L0_attn_b_Wq, L0_attn_b_bq, L0_attn_b_Wk, L0_attn_b_bk, L0_attn_b_Wv, L0_attn_b_bv, L0_attn_b_sink_scalars, L0_attn_b_v_nulls, L0_attn_b_Wo, L0_attn_b_bo)
    x = x + _L0_ffn_ref(_layernorm(x, axis=-1), L0_ffn_Wqkv, L0_ffn_q_scale, L0_ffn_k_scale, L0_ffn_Wo, L0_ffn_ln_g, L0_ffn_ln_b, L0_ffn_W1, L0_ffn_b1, L0_ffn_W2, L0_ffn_b2)
    x = x + _L1_attn_a_ref(_layernorm(x, axis=-1), L1_attn_a_Wz, L1_attn_a_bz, L1_attn_a_Wza, L1_attn_a_bza, L1_attn_a_Wy, L1_attn_a_by, L1_attn_a_Wya, L1_attn_a_bya, L1_attn_a_norm_w, L1_attn_a_lc_re, L1_attn_a_lc_im)
    x = x + _L1_ffn_ref(_layernorm(x, axis=-1), L1_ffn_Wq, L1_ffn_Wk, L1_ffn_Wv, L1_ffn_Wo, L1_ffn_Wff)
    x = x + _L1_attn_b_ref(_layernorm(x, axis=-1), L1_attn_b_wq, L1_attn_b_wk, L1_attn_b_wv, L1_attn_b_wo)
    x = x + _L1_ffn_ref(_layernorm(x, axis=-1), L1_ffn_Wq, L1_ffn_Wk, L1_ffn_Wv, L1_ffn_Wo, L1_ffn_Wff)
    return x

_drawn_inputs = setup_inputs


def setup_inputs(seed=0):
    import zlib

    import numpy as np

    out = dict(_drawn_inputs(seed))
    spreads = {'L0_attn_a_b_r': (0.0, 0.494),
     'L0_attn_a_b_k': (0.0, 0.1),
     'L0_attn_a_b_v': (0.0, 0.1),
     'L0_attn_a_b_g': (0.0, 0.1),
     'L0_attn_a_b_o': (0.0, 0.1),
     'L0_attn_a_time_mix_r': (0.5, 0.593),
     'L0_attn_a_time_mix_k': (0.5, 0.2),
     'L0_attn_a_time_mix_v': (0.5, 0.2),
     'L0_attn_a_time_mix_g': (0.5, 0.2),
     'L0_attn_a_gn_weight': (1.0, 0.2),
     'L0_attn_a_gn_bias': (0.0, 0.1),
     'L0_attn_b_bq': (0.0, 0.8),
     'L0_attn_b_bk': (0.0, 0.8),
     'L0_attn_b_bv': (0.0, 0.8),
     'L0_attn_b_bo': (0.0, 0.1),
     'L0_ffn_q_scale': (1.0, 0.6),
     'L0_ffn_k_scale': (1.0, 0.6),
     'L0_ffn_ln_g': (1.0, 0.6),
     'L0_ffn_ln_b': (0.0, 0.8),
     'L0_ffn_b1': (0.0, 0.593),
     'L0_ffn_b2': (0.0, 0.1),
     'L1_attn_a_bz': (0.0, 2.0),
     'L1_attn_a_bza': (0.0, 2.0),
     'L1_attn_a_by': (0.0, 0.8),
     'L1_attn_a_bya': (0.0, 0.8),
     'L1_attn_a_norm_w': (1.0, 0.6)}
    factors = {'L0_attn_b_Wq': 8.0,
     'L0_attn_b_Wk': 8.0,
     'L0_attn_b_Wv': 8.0,
     'L0_attn_b_sink_scalars': 8.0,
     'L0_attn_b_v_nulls': 8.0,
     'L0_attn_b_Wo': 8.0,
     'L1_attn_a_Wz': 200.0,
     'L1_attn_a_Wza': 200.0,
     'L1_attn_a_Wy': 29.887,
     'L1_attn_a_Wya': 40.155,
     'L1_attn_a_lc_re': 56.522,
     'L1_attn_a_lc_im': 64.0,
     'L1_ffn_Wq': 47.365,
     'L1_ffn_Wk': 140.016}
    for name, (base, spread) in spreads.items():
        noise = np.random.default_rng([zlib.crc32(name.encode()), seed]).standard_normal(out[name].shape)
        drawn = base * np.exp(spread * noise) if base else spread * noise
        out[name] = jnp.asarray(drawn.astype(out[name].dtype))
    for name, factor in factors.items():
        out[name] = (out[name] * factor).astype(out[name].dtype)
    return out
```

```python
from contextlib import ExitStack

import numpy as np

import concourse.bass as bass
from concourse import mybir

F32 = mybir.dt.float32
ALU = mybir.AluOpType
ACT = mybir.ActivationFunctionType
AX_X = mybir.AxisListType.X
ds = bass.ds

P = 128
B, T, C = 8, 256, 128
N = B * T
CH = 512
NCH = N // CH

DEPTH, FH, FD = 6, 16, 64
WIN = 32
INNER = FH * FD
PAIRS = FH // 2
DI = int(C * 4 * 2 / 3)
DIM = [min(P, DI - P * m) for m in range(-(-DI // P))]
UNITS_IN_BODY = 2
TILES = 2 * UNITS_IN_BODY
BODIES = B // UNITS_IN_BODY
NEG = -1.0e30

INPUTS = {}


def nth(turn, per_turn, j):
    return turn * per_turn + j + 1


def rotary_constants():
    half = np.arange(0, FD, 2, dtype=np.float32)
    inv_freq = (np.float32(1.0) / np.float32(10000.0) ** (half / np.float32(FD))).astype(np.float32)
    t = np.arange(T, dtype=np.float32)
    freqs = (t[:, None] * inv_freq[None, :]).astype(np.float32).astype(np.float64)
    freqs = np.concatenate([freqs, freqs], -1)
    base = ((half + np.float32(0.4 * FD)) / np.float32(1.4 * FD)).astype(np.float64)
    power = (t.astype(np.float64) - T // 2) / (WIN // 2)
    scale = base[None, :] ** power[:, None]
    scale = np.concatenate([scale, scale], -1)
    sign = np.where(np.arange(FD) < FD // 2, -1.0, 1.0)
    qk_scale = 8.0
    kinds = [qk_scale * np.cos(freqs) * scale, np.cos(freqs) / scale,
             qk_scale * sign * np.sin(freqs) * scale, sign * np.sin(freqs) / scale]
    a = np.stack(kinds).reshape(4, 2, P, FD).transpose(2, 0, 1, 3)
    return np.ascontiguousarray(a, dtype=np.float32).reshape(P, 4 * 2 * FD)


def window_masks():
    i = np.arange(WIN)[:, None]
    previous = np.where(np.arange(WIN)[None, :] >= i, 0.0, NEG)
    own = np.where(np.arange(WIN)[None, :] <= i, 0.0, NEG)
    m = np.tile(np.concatenate([previous, own], 1), (4, 1))
    first = m.copy()
    first[:WIN, :WIN] = NEG
    return np.ascontiguousarray(np.concatenate([first, m], 1), dtype=np.float32)


def phazor_tables():
    w = np.power(np.float32(0.001), np.linspace(0.0, 1.0, C, dtype=np.float32)).astype(np.float64)[:, None]
    t = np.arange(T, dtype=np.float64)[None, :]
    a = 1e-5
    kinds = [np.exp(-a * t) * np.cos(w * t), np.exp(-a * t) * np.sin(w * t),
             np.exp(a * t) * np.cos(w * t), np.exp(a * t) * np.sin(w * t),
             np.exp(a * (t + 1)) * np.cos(w * (t + 1)), -np.exp(a * (t + 1)) * np.sin(w * (t + 1))]
    return np.stack(kinds, 1).reshape(P, 6 * T).astype(np.float32)


def rope_tables():
    inv_freq = np.float32(1.0) / np.float32(10000.0) ** (np.arange(0, 8, 2, dtype=np.float32) / np.float32(8))
    freqs = (np.arange(T, dtype=np.float32)[:, None] * inv_freq[None, :].astype(np.float32)).astype(np.float64).T
    cos = np.tile(np.cos(freqs), (P // 4, 1))
    sin = np.tile(np.concatenate([-np.sin(freqs), np.sin(freqs)]), (P // 8, 1))
    return np.concatenate([cos, sin], 1).astype(np.float32)


def shape_constants():
    ones = np.ones((P, P), np.float32)
    return {
        "c_identity": np.eye(P, dtype=np.float32),
        "c_mean": ones / np.float32(C),
        "c_rotary": rotary_constants(),
        "c_masks": window_masks(),
        "c_phazor": phazor_tables(),
        "c_rope": rope_tables(),
        "c_only16": (np.arange(P)[:, None] // 8 == np.arange(16)[None, :]).astype(np.float32),
        "c_ones8": np.kron(np.eye(16), np.ones((8, 8))).astype(np.float32),
        "c_tri": np.triu(np.ones((P, P), np.float32)),
        "c_causal": np.tile(np.triu(np.full((P, P), NEG, np.float32), 1), (1, 2)),
        "c_only": ((np.arange(P)[:, None] % 32) // 8 == np.arange(4)[None, :]).astype(np.float32),
        "c_eps": np.tile(np.array([[1e-5, 12 * np.log(2.0), 1e-6, 1e-12]], np.float32), (P, 1)),
    }


ALL = ("attn_a0", "ffn0", "attn_b0", "ffn1", "attn_a1", "mix0", "attn_b1", "mix1")


def program(nc, d, out, parts=ALL):
    ctx = ExitStack()
    with ctx:
        def sem(name):
            return ctx.enter_context(nc.semaphore(name))

        def sb(name, cols):
            return ctx.enter_context(nc.sbuf_tensor(name, [P, cols], F32))

        arena_cols = 44400
        arena = sb("arena", arena_cols)

        class Space:
            def __init__(self, start):
                self.at = start

            def take(self, cols):
                got = arena[:, self.at:self.at + cols]
                self.at += cols
                assert self.at <= arena_cols, self.at
                return got

        XO = sb("XO", N)
        XN = sb("XN", N)
        ident = sb("ident", P)
        mean_w = sb("mean_w", P)
        eps = sb("eps", 4)
        PS = ctx.enter_context(nc.psum_tensor("PS", [P, 8, CH], F32))
        lnc = sb("lnc", 2 * CH)
        lns = sb("lns", 2 * CH)

        ffn = Space(0)
        XT = ffn.take(N)
        Wqkv = ffn.take(3 * INNER)
        Wo = ffn.take(PAIRS * C).rearrange("p (m n) -> p m n", m=PAIRS)
        W1 = ffn.take(2 * DI)
        W2 = ffn.take(len(DIM) * C).rearrange("p (m n) -> p m n", m=len(DIM))
        fvec = ffn.take(16)
        qks = ffn.take(4 * FD).rearrange("p (k e) -> p k e", k=4)
        rotary = ffn.take(8 * FD).rearrange("p (k t e) -> p k t e", k=4, t=2)
        table = ffn.take(8 * FD).rearrange("p (k t e) -> p k t e", k=4, t=2)
        masks = ffn.take(2 * 2 * WIN).rearrange("p (t j) -> p t j", t=2)
        attn = Space(ffn.at)
        xs = [attn.take(T) for _ in range(UNITS_IN_BODY)]
        raw_at = attn.at
        raw = attn.take(2 * INNER)
        sq = attn.take(2 * INNER)
        t1 = attn.take(2 * INNER)
        t2 = attn.take(2 * INNER)
        nrm = attn.take(4 * 2 * FH).rearrange("p (a h) -> p a h", a=4)
        qT = attn.take(PAIRS * P).rearrange("p (m t) -> p m t", m=PAIRS)
        KT = [attn.take(PAIRS * (WIN + T)).rearrange("p (m t) -> p m t", m=PAIRS) for _ in range(UNITS_IN_BODY)]
        V = [attn.take(INNER) for _ in range(TILES)]
        sm = attn.take(INNER)
        E = attn.take(INNER)
        sst = attn.take(4 * FH).rearrange("p (a h) -> p a h", a=4)
        EP = attn.take(FH * P).rearrange("p (h j) -> p h j", h=FH)
        EPv = attn.take(FH * P).rearrange("p (h j) -> p h j", h=FH)
        PT = attn.take(FH * P).rearrange("p (h i) -> p h i", h=FH)
        PTv = attn.take(FH * WIN).rearrange("p (h i) -> p h i", h=FH)
        AT = [attn.take(PAIRS * T).rearrange("p (m t) -> p m t", m=PAIRS) for _ in range(UNITS_IN_BODY)]
        ysb = attn.take(T)
        mlp = Space(raw_at)
        gl = mlp.take(2 * len(DIM) * CH).rearrange("p (r m n) -> p r m n", r=2, m=len(DIM))
        hh = mlp.take(2 * len(DIM) * CH).rearrange("p (r m n) -> p r m n", r=2, m=len(DIM))
        assert mlp.at - raw_at <= 8 * INNER

        phase_end = sem("phase_end")
        const_loaded = sem("const_loaded")
        x_loaded = sem("x_loaded")
        x_turned = sem("x_turned")
        x_copied = sem("x_copied")
        out_turned = sem("out_turned")
        out_copied = sem("out_copied")
        out_stored = sem("out_stored")
        ln_mean = sem("ln_mean")
        ln_centred = sem("ln_centred")
        ln_squared = sem("ln_squared")
        ln_var = sem("ln_var")
        ln_log = sem("ln_log")
        ln_rstd = sem("ln_rstd")
        ln_scaled = sem("ln_scaled")
        ln_out = sem("ln_out")
        attn_w_loaded = sem("attn_w_loaded")
        mlp_w_loaded = sem("mlp_w_loaded")
        tables_ready = sem("tables_ready")
        xs_ready = sem("xs_ready")
        qkv_ready = sem("qkv_ready")
        qkv_copied = sem("qkv_copied")
        norm2_ready = sem("norm2_ready")
        norm2_own = sem("norm2_own")
        rnorm_log = sem("rnorm_log")
        rnorm_ready = sem("rnorm_ready")
        u_ready = sem("u_ready")
        t1_ready = sem("t1_ready")
        t2_ready = sem("t2_ready")
        turned = sem("turned")
        turned_copied = sem("turned_copied")
        scores_ready = sem("scores_ready")
        scores_read = sem("scores_read")
        max_ready = sem("max_ready")
        shifted_ready = sem("shifted_ready")
        exp_ready = sem("exp_ready")
        sum_ready = sem("sum_ready")
        recip_ready = sem("recip_ready")
        probs_ready = sem("probs_ready")
        padded_ready = sem("padded_ready")
        o_ready = sem("o_ready")
        o_copied = sem("o_copied")
        stream_added = sem("stream_added")
        up_ready = sem("up_ready")
        gelu_ready = sem("gelu_ready")
        h_ready = sem("h_ready")
        down_ready = sem("down_ready")
        down_added = sem("down_added")
        low_shifted = sem("low_shifted")
        high_shifted = sem("high_shifted")
        edge_zeroed = sem("edge_zeroed")
        ffn_const_loaded = sem("ffn_const_loaded")

        consts = [(ident, "c_identity"), (mean_w, "c_mean"), (eps, "c_eps")]

        def wait_alone(eng, semaphore, count):
            if not isinstance(count, int):
                count = eng.compute_val(count)
            eng.wait_ge(phase_end, 0)
            eng.wait_ge(semaphore, count)

        def meet(eng, n):
            eng.drain().then_inc(phase_end, 1)
            wait_alone(eng, phase_end, n * 4)

        def chunk(a, c):
            return a[:, c * CH:(c + 1) * CH]

        x_dram = d["L0_attn_a_x"].rearrange("b (u p) c -> p (b u) c", p=P)
        out_dram = out.rearrange("b (u p) c -> p (b u) c", p=P)
        xtok = arena[:, 0:N].rearrange("p (t c) -> p t c", c=C)
        otok = arena[:, 0:N].rearrange("p (t c) -> p t c", c=C)

        def load_sync(sp):
            for tile, name in consts:
                sp.dma_start(tile[:], d[name]).then_inc(const_loaded, 16)
            sp.dma_start(xtok, x_dram).then_inc(x_loaded, 16)

        def load_tensor(pe):
            pe.wait_ge(const_loaded, 16 * len(consts))
            pe.wait_ge(x_loaded, 16)
            for c in range(NCH):
                for j in range(4):
                    last = pe.transpose(PS[:, c, j * P:(j + 1) * P], xtok[:, 4 * c + j, :], ident[:])
                last.then_inc(x_turned, 1)

        def load_scalar(act):
            for c in range(NCH):
                act.wait_ge(x_turned, c + 1)
                act.activation(chunk(XO, c), PS[:, c, :], ACT.Copy).then_inc(x_copied, 1)

        def store_tensor(pe):
            for c in range(NCH):
                for j in range(4):
                    last = pe.transpose(PS[:, c, j * P:(j + 1) * P], XO[:, (4 * c + j) * P:(4 * c + j + 1) * P], ident[:])
                last.then_inc(out_turned, 1)

        def store_scalar(act):
            for c in range(NCH):
                act.wait_ge(out_turned, c + 1)
                act.activation(otok[:, 4 * c:4 * c + 4, :], PS[:, c, :], ACT.Copy).then_inc(out_copied, 1)

        def store_sync(sp):
            for c in range(NCH):
                sp.wait_ge(out_copied, c + 1)
                sp.dma_start(out_dram[:, 4 * c:4 * c + 4, :], otok[:, 4 * c:4 * c + 4, :]).then_inc(out_stored, 16)
            sp.wait_ge(out_stored, 16 * NCH)

        def ln_tensor(pe, n, src):
            def var(c):
                pe.wait_ge(ln_squared, nth(n, NCH, c))
                pe.matmul(PS[:, 4 + c, :], mean_w[:], lns[:, (c % 2) * CH:(c % 2 + 1) * CH],
                          start=True, stop=True).then_inc(ln_var, 1)
            for c in range(NCH):
                pe.matmul(PS[:, c, :], mean_w[:], chunk(src, c), start=True, stop=True).then_inc(ln_mean, 1)
            for c in range(NCH):
                var(c)

        def log_exp_tables(act):
            act.preload_act_table_set("natural_log_exp_and_others")

        def ln_scalar(act, n):
            log_exp_tables(act)
            for c in range(NCH):
                half = slice((c % 2) * CH, (c % 2 + 1) * CH)
                act.wait_ge(ln_centred, nth(n, NCH, c))
                if c >= 2:
                    act.wait_ge(ln_scaled, nth(n, NCH, c - 2))
                act.activation(lns[:, half], lnc[:, half], ACT.Square).then_inc(ln_squared, 1)
                act.wait_ge(ln_var, nth(n, NCH, c))
                act.activation(lns[:, half], PS[:, 4 + c, :], ACT.Ln, bias=eps[:, 0:1]).then_inc(ln_log, 1)
                act.wait_ge(ln_log, nth(n, NCH, c))
                act.activation(lns[:, half], lns[:, half], ACT.Exp, scale=-0.5).then_inc(ln_rstd, 1)

        def ln_vector(dve, n, src, dst, gain=None):
            def centre(c):
                half = slice((c % 2) * CH, (c % 2 + 1) * CH)
                dve.wait_ge(ln_mean, nth(n, NCH, c))
                dve.tensor_tensor(lnc[:, half], chunk(src, c), PS[:, c, :], ALU.subtract).then_inc(ln_centred, 1)

            def scale(c):
                half = slice((c % 2) * CH, (c % 2 + 1) * CH)
                dve.wait_ge(ln_rstd, nth(n, NCH, c))
                dve.tensor_tensor(chunk(dst, c), lnc[:, half], lns[:, half], ALU.mult).then_inc(ln_scaled, 1)
                dve.wait_ge(ln_scaled, nth(n, NCH, c))
                if gain is not None:
                    dve.tensor_scalar(chunk(dst, c), chunk(dst, c), gain[0], gain[1], ALU.mult, ALU.add)\
                       .then_inc(ln_out, 1)
            centre(0)
            centre(1)
            for c in range(NCH):
                scale(c)
                if c + 2 < NCH:
                    centre(c + 2)

        QKV, TURN, SCORE, HEAD = 0, 2, 4, 6
        QKV_PER, TURN_PER, SCORE_PER, HEAD_PER = 6 * TILES, 17 * UNITS_IN_BODY, 2 * TILES, 5 * UNITS_IN_BODY

        def turn_index(tt, kind, j):
            uu, par = divmod(tt, 2)
            return uu * 17 + par * 8 + (0 if kind == "qk" else 4) + j

        def head_index(tt, j):
            uu, par = divmod(tt, 2)
            return uu * 5 + par * 2 + j

        def fa_tensor(pe, run):
            wait_alone(pe, attn_w_loaded, (run + 1) * ATTN_LOADS)
            with pe.Fori(0, BODIES) as it:
                g = run * BODIES + it

                def qkv(tt):
                    uu, par = divmod(tt, 2)
                    if par == 0:
                        pe.wait_ge(xs_ready, nth(g, UNITS_IN_BODY, uu))
                    for c in range(6):
                        n = 6 * tt + c
                        pe.wait_ge(qkv_copied, nth(g, QKV_PER, n))
                        pe.matmul(PS[:, QKV + n % 2, :], xs[uu][:, par * P:(par + 1) * P], chunk(Wqkv, c),
                                  start=True, stop=True).then_inc(qkv_ready, 1)

                def turn_qk(tt):
                    for c in range(4):
                        n = turn_index(tt, "qk", c)
                        pe.wait_ge(turned_copied, nth(g, TURN_PER, n))
                        if c % 2 == 0:
                            pe.wait_ge(t1_ready, nth(g, 2 * TILES, 2 * tt + c // 2) + 1)
                            pe.wait_ge(t2_ready, nth(g, 2 * TILES, 2 * tt + c // 2) + 1)
                        for j in range(4):
                            o = PS[:, TURN + n % 2, j * P:(j + 1) * P]
                            cols = slice((4 * c + j) * P, (4 * c + j + 1) * P)
                            pe.matmul(o, t1[:, cols], ident[:], start=True, stop=False, is_transpose=True)
                            last = pe.matmul(o, t2[:, cols], ident[:], start=False, stop=True, is_transpose=True)
                        last.then_inc(turned, 1)

                def scores(tt):
                    uu, par = divmod(tt, 2)
                    wait_alone(pe, turned_copied, nth(g, TURN_PER, turn_index(tt, "qk", 3)) + 2)
                    for s in range(2):
                        wait_alone(pe, scores_read, nth(g, SCORE_PER, 2 * tt + s))
                        for m in range(PAIRS):
                            for w in range(4):
                                at = par * P + w * WIN
                                last = pe.matmul(PS[w * WIN:(w + 1) * WIN, SCORE + s, m * FD:(m + 1) * FD],
                                                 qT[s * FD:(s + 1) * FD, m, w * WIN:(w + 1) * WIN],
                                                 KT[uu][s * FD:(s + 1) * FD, m, at:at + 2 * WIN],
                                                 start=True, stop=True)
                        last.then_inc(scores_ready, 1)

                def turn_probs(tt):
                    pe.wait_ge(padded_ready, nth(g, TILES, tt))
                    for c in range(4):
                        n = turn_index(tt, "p", c)
                        pe.wait_ge(turned_copied, nth(g, TURN_PER, n))
                        for j in range(4):
                            last = pe.transpose(PS[:, TURN + n % 2, j * P:(j + 1) * P], EP[:, 4 * c + j, :], ident[:])
                        last.then_inc(turned, 1)
                    if tt % 2 == 1:
                        n = turn_index(tt, "p", 4)
                        wait_alone(pe, turned_copied, nth(g, TURN_PER, n))
                        for h in range(FH):
                            last = pe.transpose(PS[:, TURN + n % 2, h * WIN:(h + 1) * WIN], EPv[0:WIN, h, :],
                                                ident[0:WIN, 0:WIN])
                        last.then_inc(turned, 1)

                def heads(tt):
                    par = tt % 2
                    pe.wait_ge(turned_copied, nth(g, TURN_PER, turn_index(tt, "p", 3 + par)) + 2)
                    for j in range(2):
                        n = head_index(tt, j)
                        pe.wait_ge(o_copied, nth(g, HEAD_PER, n))
                        for m in range(4):
                            for s in range(2):
                                slot = s * PAIRS + 4 * j + m
                                h = 2 * (4 * j + m) + s
                                rows = slice(s * FD, (s + 1) * FD)
                                last = pe.matmul(PS[rows, HEAD + n % 2, m * P:(m + 1) * P],
                                                 V[tt][:, h * FD:(h + 1) * FD], PT[:, slot, :],
                                                 start=True, stop=True)
                                if par == 1:
                                    last = pe.matmul(PS[rows, HEAD + n % 2, m * P:m * P + WIN],
                                                     V[tt - 1][:, h * FD:(h + 1) * FD], PTv[:, slot, :],
                                                     start=False, stop=True, skip_group_check=True)
                        last.then_inc(o_ready, 1)

                def project(uu):
                    n = 5 * uu + 4
                    pe.wait_ge(o_copied, nth(g, HEAD_PER, n))
                    pe.wait_ge(o_copied, nth(g, HEAD_PER, n - 1) + 2)
                    for m in range(PAIRS):
                        last = pe.matmul(PS[:, HEAD + n % 2, 0:T], Wo[:, m, :], AT[uu][:, m, :],
                                         start=(m == 0), stop=(m == PAIRS - 1))
                    last.then_inc(o_ready, 1)

                qkv(0)
                for tt in range(TILES):
                    turn_qk(tt)
                    scores(tt)
                    if tt + 1 < TILES:
                        qkv(tt + 1)
                    turn_probs(tt)
                    heads(tt)
                    if tt % 2 == 1:
                        project(tt // 2)

        def fa_scalar(act, run):
            with act.Fori(0, BODIES) as it:
                g = run * BODIES + it

                def copy_qkv(tt):
                    act.wait_ge(t1_ready, g * 2 * TILES + 2 * tt + 1)
                    act.wait_ge(t2_ready, g * 2 * TILES + 2 * tt + 1)
                    for c in range(6):
                        n = 6 * tt + c
                        act.wait_ge(qkv_ready, nth(g, QKV_PER, n))
                        bank = PS[:, QKV + n % 2, :]
                        if c < 4:
                            act.activation(chunk(raw, c), bank, ACT.Copy)
                            act.activation(chunk(sq, c), bank, ACT.Square).then_inc(qkv_copied, 1)
                        else:
                            act.activation(V[tt][:, (c - 4) * CH:(c - 3) * CH], bank, ACT.Copy)\
                               .then_inc(qkv_copied, 1)

                def rnorm(tt):
                    act.wait_ge(norm2_ready, nth(g, TILES, tt))
                    act.activation(nrm[:, 1, :], nrm[:, 0, :], ACT.Ln, scale=float(2 ** 24)).then_inc(rnorm_log, 1)
                    act.wait_ge(rnorm_log, nth(g, TILES, tt))
                    act.activation(nrm[:, 2, :], nrm[:, 1, :], ACT.Exp, bias=eps[:, 1:2], scale=-0.5)\
                       .then_inc(rnorm_ready, 1)

                def copy_turned(tt):
                    uu, par = divmod(tt, 2)
                    for c in range(4):
                        n = turn_index(tt, "qk", c)
                        act.wait_ge(turned, nth(g, TURN_PER, n))
                        m = slice(4 * (c % 2), 4 * (c % 2) + 4)
                        to = qT[:, m, :] if c < 2 else KT[uu][:, m, WIN + par * P:WIN + (par + 1) * P]
                        act.activation(to, PS[:, TURN + n % 2, :].rearrange("p (m t) -> p m t", m=4), ACT.Copy)\
                           .then_inc(turned_copied, 1)

                def exps(tt):
                    act.wait_ge(shifted_ready, nth(g, TILES, tt))
                    act.activation(E, sm, ACT.Exp).then_inc(exp_ready, 1)

                def pad(tt):
                    act.wait_ge(probs_ready, nth(g, TILES, tt))
                    p3 = E.rearrange("p (h j) -> p h j", h=FH)
                    if tt % 2 == 1:
                        act.activation(EPv[0:WIN, :, 3 * WIN:4 * WIN], p3[0:WIN, :, 0:WIN], ACT.Copy)
                    act.activation(EP[0:WIN, :, 0:WIN], p3[0:WIN, :, WIN:2 * WIN], ACT.Copy)
                    for w in range(1, 4):
                        rows = slice(w * WIN, (w + 1) * WIN)
                        last = act.activation(EP[rows, :, (w - 1) * WIN:(w + 1) * WIN], p3[rows, :, :], ACT.Copy)
                    last.then_inc(padded_ready, 1)

                def copy_probs(tt):
                    for c in range(4):
                        n = turn_index(tt, "p", c)
                        act.wait_ge(turned, nth(g, TURN_PER, n))
                        act.activation(PT[:, 4 * c:4 * c + 4, :],
                                       PS[:, TURN + n % 2, :].rearrange("p (m t) -> p m t", m=4), ACT.Copy)\
                           .then_inc(turned_copied, 1)
                    if tt % 2 == 1:
                        n = turn_index(tt, "p", 4)
                        act.wait_ge(turned, nth(g, TURN_PER, n))
                        act.activation(PTv, PS[:, TURN + n % 2, :].rearrange("p (m t) -> p m t", m=FH), ACT.Copy)\
                           .then_inc(turned_copied, 1)

                def copy_heads(tt):
                    uu, par = divmod(tt, 2)
                    for j in range(2):
                        n = head_index(tt, j)
                        act.wait_ge(o_ready, nth(g, HEAD_PER, n))
                        act.activation(AT[uu][:, 4 * j:4 * j + 4, par * P:(par + 1) * P],
                                       PS[:, HEAD + n % 2, :].rearrange("p (m t) -> p m t", m=4), ACT.Copy)\
                           .then_inc(o_copied, 1)

                def copy_projected(uu):
                    n = 5 * uu + 4
                    act.wait_ge(o_ready, nth(g, HEAD_PER, n))
                    act.wait_ge(stream_added, nth(g, UNITS_IN_BODY, uu))
                    act.activation(ysb, PS[:, HEAD + n % 2, 0:T], ACT.Copy).then_inc(o_copied, 1)

                act.wait_ge(qkv_copied, g * QKV_PER + 2)
                for uu in range(UNITS_IN_BODY):
                    at = (it * UNITS_IN_BODY + uu) * T
                    act.activation(xs[uu][0:64, :], XT[0:64, ds(at, T)], ACT.Copy)
                    act.activation(xs[uu][64:128, 1:T], XT[64:128, ds(at, T - 1)], ACT.Copy).then_inc(xs_ready, 1)
                copy_qkv(0)
                rnorm(0)
                for tt in range(TILES):
                    copy_turned(tt)
                    if tt + 1 < TILES:
                        copy_qkv(tt + 1)
                    exps(tt)
                    pad(tt)
                    if tt + 1 < TILES:
                        rnorm(tt + 1)
                    copy_probs(tt)
                    copy_heads(tt)
                    if tt % 2 == 1:
                        copy_projected(tt // 2)

        def fa_vector(dve, run):
            h3 = lambda a: a.rearrange("p (h e) -> p h e", e=FD)
            wait_alone(dve, tables_ready, run + 1)
            with dve.Fori(0, BODIES) as it:
                g = run * BODIES + it

                def softmax_shift(tt):
                    mask = masks[:, tt % 2:tt % 2 + 1, :].broadcast_to([P, PAIRS, 2 * WIN])
                    for s in range(2):
                        dve.wait_ge(scores_ready, nth(g, SCORE_PER, 2 * tt + s))
                        last = dve.tensor_tensor(h3(chunk(sm, s)), h3(PS[:, SCORE + s, :]), mask, ALU.add)
                        last.then_inc(scores_read, 1)
                    dve.wait_ge(scores_read, nth(g, SCORE_PER, 2 * tt + 1) + 2)
                    dve.tensor_reduce(sst[:, 0, :], h3(sm), AX_X, ALU.max).then_inc(max_ready, 1)
                    dve.wait_ge(max_ready, nth(g, TILES, tt))
                    mx = sst[:, 0, :].rearrange("p (h o) -> p h o", o=1).broadcast_to([P, FH, FD])
                    dve.tensor_tensor(h3(sm), h3(sm), mx, ALU.subtract).then_inc(shifted_ready, 1)

                def softmax_norm(tt):
                    dve.wait_ge(exp_ready, nth(g, TILES, tt))
                    dve.tensor_reduce(sst[:, 1, :], h3(E), AX_X, ALU.add).then_inc(sum_ready, 1)
                    dve.wait_ge(sum_ready, nth(g, TILES, tt))
                    dve.reciprocal(sst[:, 2, :], sst[:, 1, :]).then_inc(recip_ready, 1)
                    dve.wait_ge(recip_ready, nth(g, TILES, tt))
                    rc = sst[:, 2, :].rearrange("p (h o) -> p h o", o=1).broadcast_to([P, FH, FD])
                    dve.tensor_tensor(h3(E), h3(E), rc, ALU.mult).then_inc(probs_ready, 1)

                def norms(tt):
                    dve.wait_ge(qkv_copied, nth(g, QKV_PER, 6 * tt + 3) + 2)
                    dve.tensor_reduce(nrm[:, 3, :], h3(sq), AX_X, ALU.add).then_inc(norm2_own, 1)
                    dve.wait_ge(norm2_own, nth(g, TILES, tt))
                    dve.tensor_scalar(nrm[:, 0, :], nrm[:, 3, :], 1e-24, None, ALU.max).then_inc(norm2_ready, 1)

                def rotate(tt):
                    uu, par = divmod(tt, 2)
                    dve.wait_ge(rnorm_ready, nth(g, TILES, tt))
                    for k in range(2):
                        part = slice(k * INNER, (k + 1) * INNER)
                        rn = nrm[:, 2, k * FH:(k + 1) * FH].rearrange("p (h o) -> p h o", o=1)\
                            .broadcast_to([P, FH, FD])
                        dve.tensor_tensor(h3(raw[:, part]), h3(raw[:, part]), rn, ALU.mult).then_inc(u_ready, 1)
                    for k in range(2):
                        part = slice(k * INNER, (k + 1) * INNER)
                        cosine = table[:, k, par:par + 1, :].broadcast_to([P, FH, FD])
                        dve.wait_ge(u_ready, nth(g, 2 * TILES, 2 * tt + k))
                        dve.tensor_tensor(h3(t1[:, part]), h3(raw[:, part]), cosine, ALU.mult).then_inc(t1_ready, 1)

                def add_stream(uu):
                    at = ds((it * UNITS_IN_BODY + uu) * T, T)
                    dve.wait_ge(o_copied, nth(g, HEAD_PER, 5 * uu + 4) + 2)
                    dve.tensor_tensor(XT[:, at], XT[:, at], ysb, ALU.add).then_inc(stream_added, 1)

                norms(0)
                rotate(0)
                for tt in range(TILES):
                    softmax_shift(tt)
                    softmax_norm(tt)
                    if tt + 1 < TILES:
                        norms(tt + 1)
                        rotate(tt + 1)
                    if tt % 2 == 1:
                        add_stream(tt // 2)

        def fa_gpsimd(pool, run):
            pool.wait_ge(attn_w_loaded, (run + 1) * ATTN_LOADS)
            for k in range(4):
                last = pool.tensor_tensor(table[:, k, :, :], rotary[:, k, :, :],
                                          qks[:, k:k + 1, :].broadcast_to([P, 2, FD]), ALU.mult)
            last.then_inc(tables_ready, 1)
            wait_alone(pool, tables_ready, run + 1)
            with pool.Fori(0, BODIES) as it:
                g = run * BODIES + it
                for tt in range(TILES):
                    par = tt % 2
                    for k in range(2):
                        u3 = raw[:, k * INNER:(k + 1) * INNER].rearrange("p (h e) -> p h e", e=FD)
                        o3 = t2[:, k * INNER:(k + 1) * INNER].rearrange("p (h e) -> p h e", e=FD)
                        pool.wait_ge(u_ready, nth(g, 2 * TILES, 2 * tt + k))
                        for half in range(2):
                            a, b = half * 32, 32 - half * 32
                            sine = table[:, 2 + k, par:par + 1, a:a + 32].broadcast_to([P, FH, 32])
                            last = pool.tensor_tensor(o3[:, :, a:a + 32], u3[:, :, b:b + 32], sine, ALU.mult)
                        last.then_inc(t2_ready, 1)

        ATTN_LOADS, MLP_LOADS = 16 * 3, 16 * 4

        def ff_shift_vector(dve, run):
            dve.memset(XN[64:128, :].rearrange("p (b t) -> p b t", t=T)[:, :, 0:1], 0.0).then_inc(edge_zeroed, 1)
            for c in range(NCH):
                dve.tensor_copy(XN[0:64, c * CH:(c + 1) * CH], XT[0:64, c * CH:(c + 1) * CH]).then_inc(low_shifted, 1)

        def ff_shift_scalar(act, run):
            for c in range(NCH):
                to = XN[64:128, c * CH:(c + 1) * CH].rearrange("p (b t) -> p b t", t=T)
                fr = XT[64:128, c * CH:(c + 1) * CH].rearrange("p (b t) -> p b t", t=T)
                act.activation(to[:, :, 1:T], fr[:, :, 0:T - 1], ACT.Copy).then_inc(high_shifted, 1)

        def ff_tensor(pe, run, n):
            pe.wait_ge(edge_zeroed, run + 1)
            pe.wait_ge(low_shifted, nth(run, NCH, NCH - 1))
            pe.wait_ge(high_shifted, nth(run, NCH, NCH - 1))
            ln_tensor(pe, n, XN)
            M = len(DIM)

            def up(c):
                if c == 0:
                    pe.wait_ge(mlp_w_loaded, (run + 1) * MLP_LOADS)
                pe.wait_ge(ln_out, nth(run, NCH, NCH - 1))
                for m in range(M):
                    if c > 0:
                        pe.wait_ge(h_ready, nth(run, M * NCH, M * (c - 1) + m))
                    for k, first in ((0, DI), (1, 0)):
                        pe.matmul(PS[0:DIM[m], 2 * m + k, :], W1[:, first + P * m:first + P * m + DIM[m]],
                                  chunk(XN, c), start=True, stop=True).then_inc(up_ready, 1)

            def down(c):
                if c >= 2:
                    pe.wait_ge(down_added, nth(run, NCH, c - 2))
                for m in range(M):
                    pe.wait_ge(h_ready, nth(run, M * NCH, M * c + m))
                    last = pe.matmul(PS[:, 6 + c % 2, :], W2[0:DIM[m], m, :], hh[0:DIM[m], c % 2, m, :],
                                     start=(m == 0), stop=(m == M - 1))
                last.then_inc(down_ready, 1)
            up(0)
            for c in range(NCH):
                if c + 1 < NCH:
                    up(c + 1)
                down(c)

        def ff_scalar(act, run, n):
            M = len(DIM)
            ff_shift_scalar(act, run)
            ln_scalar(act, n)
            for c in range(NCH):
                for m in range(M):
                    act.wait_ge(up_ready, nth(run, 2 * M * NCH, 2 * (M * c + m)))
                    act.activation(gl[0:DIM[m], c % 2, m, :], PS[0:DIM[m], 2 * m, :], ACT.Gelu,
                                   bias=fvec[0:DIM[m], 3 + m:4 + m]).then_inc(gelu_ready, 1)

        def ff_vector(dve, run, n):
            M = len(DIM)
            ff_shift_vector(dve, run)
            dve.wait_ge(edge_zeroed, run + 1)
            dve.wait_ge(low_shifted, nth(run, NCH, NCH - 1))
            dve.wait_ge(high_shifted, nth(run, NCH, NCH - 1))
            dve.wait_ge(mlp_w_loaded, (run + 1) * MLP_LOADS)
            ln_vector(dve, n, XN, XN, gain=(fvec[:, 0:1], fvec[:, 1:2]))

            def gated(c):
                for m in range(M):
                    dve.wait_ge(gelu_ready, nth(run, M * NCH, M * c + m))
                    dve.wait_ge(up_ready, nth(run, 2 * M * NCH, 2 * (M * c + m) + 1))
                    rows = slice(0, DIM[m])
                    dve.scalar_tensor_tensor(hh[rows, c % 2, m, :], PS[rows, 2 * m + 1, :], fvec[rows, 6 + m:7 + m],
                                             gl[rows, c % 2, m, :], ALU.add, ALU.mult).then_inc(h_ready, 1)
            gated(0)
            for c in range(NCH):
                if c + 1 < NCH:
                    gated(c + 1)
                dve.wait_ge(down_ready, nth(run, NCH, c))
                dve.scalar_tensor_tensor(chunk(XT, c), PS[:, 6 + c % 2, :], fvec[:, 2:3], chunk(XT, c),
                                         ALU.add, ALU.add).then_inc(down_added, 1)

        def ffn_tensor(pe, call, K, n0):
            ln_tensor(pe, n0, XO)
            meet(pe, K + 1)
            with pe.Fori(0, DEPTH) as l:
                fa_tensor(pe, l + call * DEPTH)
                meet(pe, l * 2 + K + 2)
                ff_tensor(pe, l + call * DEPTH, l + n0 + 1)
                meet(pe, l * 2 + K + 3)

        def ffn_scalar(act, call, K, n0):
            ln_scalar(act, n0)
            meet(act, K + 1)
            with act.Fori(0, DEPTH) as l:
                log_exp_tables(act)
                fa_scalar(act, l + call * DEPTH)
                meet(act, l * 2 + K + 2)
                ff_scalar(act, l + call * DEPTH, l + n0 + 1)
                meet(act, l * 2 + K + 3)

        def ffn_vector(dve, call, K, n0):
            ln_vector(dve, n0, XO, XT)
            meet(dve, K + 1)
            with dve.Fori(0, DEPTH) as l:
                fa_vector(dve, l + call * DEPTH)
                meet(dve, l * 2 + K + 2)
                ff_vector(dve, l + call * DEPTH, l + n0 + 1)
                meet(dve, l * 2 + K + 3)
            for c in range(NCH):
                last = dve.tensor_tensor(chunk(XO, c), chunk(XO, c), chunk(XT, c), ALU.add)

        def ffn_gpsimd(pool, call, K, n0):
            for uu in range(UNITS_IN_BODY):
                pool.memset(xs[uu][:, 0:1], 0.0)
                pool.memset(KT[uu][:, :, 0:WIN], 0.0)
            pool.memset(EP, 0.0)
            pool.memset(EPv, 0.0)
            meet(pool, K + 1)
            wait_alone(pool, ffn_const_loaded, 32 * (call + 1))
            with pool.Fori(0, DEPTH) as l:
                fa_gpsimd(pool, l + call * DEPTH)
                meet(pool, l * 2 + K + 2)
                meet(pool, l * 2 + K + 3)

        def ffn_sync(sp, call, K):
            def attention(layer):
                sp.dma_start(Wqkv, d["L0_ffn_Wqkv"][layer, :, :].rearrange("o p n -> (o p) n")).then_inc(attn_w_loaded, 16)
                sp.dma_start(Wo, d["L0_ffn_Wo"][layer, :, :].rearrange("o (m p) n -> p (o m) n", p=P)).then_inc(attn_w_loaded, 16)
                sp.dma_start(qks, d["ffn_scales"][layer, :].rearrange("o (k e) -> o k e", k=4)
                             .broadcast_to([P, 4, FD])).then_inc(attn_w_loaded, 16)

            def feed_forward(layer):
                sp.dma_start(W1, d["L0_ffn_W1"][layer, :, :].rearrange("o p n -> (o p) n")).then_inc(mlp_w_loaded, 16)
                full = 2 * P
                w2 = d["L0_ffn_W2"]
                sp.dma_start(W2[:, 0:2, :], w2[layer, 0:full, :].rearrange("o (m p) n -> p (o m) n", p=P)).then_inc(mlp_w_loaded, 16)
                sp.dma_start(W2[0:DIM[2], 2, :], w2[layer, full:DI, :].rearrange("o p n -> (o p) n")).then_inc(mlp_w_loaded, 16)
                sp.dma_start(fvec[:, 0:9], d["ffn_vectors"][layer, :, :].rearrange("o p n -> (o p) n")).then_inc(mlp_w_loaded, 16)
            if K > 0:
                sp.wait_ge(phase_end, 4 * K)
            attention(slice(0, 1))
            feed_forward(slice(0, 1))
            sp.dma_start(rotary, d["c_rotary"].rearrange("p (k t e) -> p k t e", k=4, t=2)).then_inc(ffn_const_loaded, 16)
            sp.dma_start(masks, d["c_masks"].rearrange("p (t j) -> p t j", t=2)).then_inc(ffn_const_loaded, 16)
            with sp.Fori(0, DEPTH - 1) as l:
                sp.wait_ge(phase_end, (l * 2 + K + 2) * 4)
                attention(ds(l + 1, 1))
                sp.wait_ge(phase_end, (l * 2 + K + 3) * 4)
                feed_forward(ds(l + 1, 1))

        HD8 = 8
        MAX_NORM2 = float(HD8) * 4.0
        a0 = Space(0)
        a0_w = [a0.take(C) for _ in range(5)]
        a0_vec = a0.take(16)
        a0_rest = a0.take(4)
        a0_head = a0.take(8)
        a0_G = a0.take(N)
        a0_sh = a0.take(N)
        a0_R = a0.take(N)
        a0_K = a0.take(N)
        a0_V = a0.take(N)
        a0_F = a0.take(T + 1)
        a0_DF = a0.take(T + 1)
        a0_small = a0.take(64)
        a0_rn = a0.take(2 * T)
        a0_step = a0.take(256)
        a0_H = a0.take((T + 1) * HD8 * HD8)
        a0_mix = a0_H[:, 0:4 * N]
        a0_out = a0_H[:, 4 * N:7 * N]
        a0_tmp = a0_sh
        scratch = nc.dram_tensor("scratch", (4, B, C, T), F32, kind="Internal").ap()
        s_mix = sem("s_mix")
        s_sh = sem("s_sh")
        s_rest = sem("s_rest")
        s_part = sem("s_part")
        s_proj = sem("s_proj")
        s_act = sem("s_act")
        s_gate = sem("s_gate")
        s_a0w = sem("s_a0w")
        s_out = [sem(f"s_out{i}") for i in range(3)]
        s_in = sem("s_in")
        s_sq = sem("s_sq")
        s_n2 = sem("s_n2")
        s_rn = sem("s_rn")
        s_unit = sem("s_unit")
        scan_step = sem("scan_step")
        scan_norm = sem("scan_norm")
        s_wkv = sem("s_wkv")
        s_stat = sem("s_stat")
        s_rstd = sem("s_rstd")
        s_back = sem("s_back")
        s_backed = sem("s_backed")
        s_gn = sem("s_gn")
        s_o = sem("s_o")
        s_x = sem("s_x")
        r3 = lambda a: a.rearrange("p (d t) -> p d t", t=T)
        H3 = a0_H.rearrange("p (t e) -> p t e", e=HD8 * HD8)
        STEPS = 4

        def a0_sync(sp):
            for k, name in enumerate(("r", "k", "v", "g", "o")):
                sp.dma_start(a0_w[k], d[f"a0_W_{name}"]).then_inc(s_a0w, 16)
            sp.dma_start(a0_vec, d["a0_vectors"]).then_inc(s_a0w, 16)
            sp.dma_start(a0_head[:, 0:2], d["a0_heads"]).then_inc(s_a0w, 16)
            for k in range(3):
                sp.wait_ge(s_act, (k + 1) * NCH)
                sp.dma_start(scratch[k].rearrange("b c t -> c b t"),
                             a0_out[:, k * N:(k + 1) * N].rearrange("p (b t) -> p b t", b=B)).then_inc(s_out[k], 16)
            for k, to in enumerate((a0_R, a0_K, a0_V)):
                sp.wait_ge(s_out[k], 16)
                sp.dma_start(to, scratch[k].rearrange("b (h d) t -> (b h) (d t)", d=HD8)).then_inc(s_in, 16)
            sp.wait_ge(s_wkv, 7)
            sp.dma_start(scratch[3].rearrange("b (h d) t -> (b h) (d t)", d=HD8), a0_tmp).then_inc(s_back, 16)
            sp.wait_ge(s_back, 16)
            sp.dma_start(a0_R.rearrange("p (b t) -> p b t", b=B), scratch[3].rearrange("b c t -> c b t"))\
              .then_inc(s_backed, 16)

        def a0_vector(dve, n0):
            ln_vector(dve, n0, XO, XN)
            dve.memset(a0_sh.rearrange("p (b t) -> p b t", t=T)[:, :, 0:1], 0.0).then_inc(s_rest, 1)
            dve.wait_ge(s_a0w, 16 * 7)
            dve.tensor_scalar(a0_rest, a0_vec[:, 0:4], -1.0, 1.0, ALU.mult, ALU.add).then_inc(s_rest, 1)
            dve.wait_ge(s_rest, 2)
            dve.wait_ge(ln_scaled, (n0 + 1) * NCH)
            dve.tensor_copy(a0_sh.rearrange("p (b t) -> p b t", t=T)[:, :, 1:T],
                            XN[:].rearrange("p (b t) -> p b t", t=T)[:, :, 0:T - 1]).then_inc(s_sh, 1)
            dve.wait_ge(s_sh, 1)
            for k in range(4):
                dve.wait_ge(s_part, k + 1)
                m = a0_mix[:, k * N:(k + 1) * N]
                dve.scalar_tensor_tensor(m, a0_sh, a0_rest[:, k:k + 1], m, ALU.mult, ALU.add).then_inc(s_mix, 1)
            for c in range(NCH):
                dve.wait_ge(s_act, 4 * NCH - NCH + c + 1)
                dve.scalar_tensor_tensor(chunk(a0_G, c), PS[:, 4 + c, :], a0_vec[:, 7:8], chunk(a0_G, c),
                                         ALU.add, ALU.mult).then_inc(s_gate, 1)
            dve.wait_ge(s_unit, 1)
            dve.tensor_scalar(a0_head[:, 3:4], a0_head[:, 3:4], -1.0, None, ALU.mult).then_inc(s_unit, 1)
            dve.wait_ge(s_in, 48)
            for k, a in enumerate((a0_K, a0_V)):
                if k:
                    dve.wait_ge(s_n2, 1)
                dve.tensor_tensor(a0_tmp, a, a, ALU.mult).then_inc(s_sq, 1)
                dve.wait_ge(s_sq, k + 1)
                rn = a0_rn[:, k * T:(k + 1) * T]
                dve.tensor_reduce(rn, a0_tmp.rearrange("p (d t) -> p t d", t=T), AX_X, ALU.add).then_inc(s_n2, 1)
            dve.wait_ge(s_n2, 2)
            dve.tensor_scalar(a0_rn, a0_rn, 1e-24, None, ALU.max).then_inc(s_n2, 1)
            dve.wait_ge(s_rn, 2)
            for k, a in enumerate((a0_K, a0_V)):
                rn = a0_rn[:, k * T:(k + 1) * T].rearrange("p (o t) -> p o t", o=1).broadcast_to([P, HD8, T])
                dve.tensor_tensor(r3(a), r3(a), rn, ALU.mult).then_inc(s_sq, 1)
            dve.wait_ge(s_sq, 4)
            dve.tensor_scalar(a0_KEs, a0_K, a0_head[:, 3:4], None, ALU.mult).then_inc(s_unit, 1)
            dve.memset(a0_H[:, 0:HD8 * HD8], 0.0).then_inc(s_unit, 1)
            dve.memset(a0_small[:, 2:3], 1.0).then_inc(s_unit, 1)
            dve.wait_ge(s_unit, 5)
            prod = a0_step[:, 0:64].rearrange("p (i j) -> p i j", j=HD8)
            outer = a0_step[:, 64:128].rearrange("p (i j) -> p i j", j=HD8)
            pred = a0_step[:, 128:136]
            err = a0_step[:, 136:144]
            with dve.Fori(0, T // STEPS) as turn:
                for q in range(STEPS):
                    g = turn * STEPS + q
                    n = turn * STEPS * 7 + 7 * q
                    col = ds(g, 1)
                    kj = r3(a0_K)[:, :, col].rearrange("p j o -> p o j").broadcast_to([P, HD8, HD8])
                    ke = r3(a0_KEs)[:, :, col].rearrange("p j o -> p o j").broadcast_to([P, HD8, HD8])
                    before = a0_H[:, ds(g * 64, 64)]
                    after = a0_H[:, ds(g * 64 + 64, 64)]
                    dve.tensor_tensor(prod, before.rearrange("p (i j) -> p i j", j=HD8), kj, ALU.mult)\
                       .then_inc(scan_step, 1)
                    dve.wait_ge(scan_step, n + 1)
                    dve.tensor_reduce(pred, prod, AX_X, ALU.add).then_inc(scan_step, 1)
                    dve.wait_ge(scan_norm, turn * STEPS * 3 + 3 * q + 3)
                    x = a0_small[:, 2:3]
                    dve.tensor_scalar(a0_F[:, col], x, 1.0, None, ALU.min).then_inc(scan_step, 1)
                    dve.tensor_scalar(a0_DF[:, col], x, 1.0, a0_head[:, 2:3], ALU.min, ALU.mult)\
                       .then_inc(scan_step, 1)
                    dve.wait_ge(scan_step, n + 4)
                    dve.scalar_tensor_tensor(err, pred, a0_F[:, col], r3(a0_V)[:, :, col].rearrange("p i o -> p (i o)"),
                                             ALU.mult, ALU.subtract).then_inc(scan_step, 1)
                    dve.wait_ge(scan_step, n + 5)
                    dve.tensor_tensor(outer, err.rearrange("p (i o) -> p i o", o=1).broadcast_to([P, HD8, HD8]),
                                      ke, ALU.mult).then_inc(scan_step, 1)
                    dve.wait_ge(scan_step, n + 6)
                    dve.scalar_tensor_tensor(after, before, a0_DF[:, col], a0_step[:, 64:128],
                                             ALU.mult, ALU.add).then_inc(scan_step, 1)
                    dve.wait_ge(scan_step, n + 7)
            dve.wait_ge(scan_norm, 3 * T + 3)
            dve.tensor_scalar(a0_F[:, T:T + 1], a0_small[:, 2:3], 1.0, None, ALU.min).then_inc(s_wkv, 1)
            W3 = r3(a0_tmp)
            part = T // 4
            prod4 = a0_big.rearrange("p (t i j) -> p t i j", i=HD8, j=HD8)
            for c in range(4):
                dve.tensor_tensor(
                    a0_big.rearrange("p (t i j) -> p t i j", i=HD8, j=HD8),
                    H3[:, 1 + c * part:1 + (c + 1) * part, :].rearrange("p t (i j) -> p t i j", j=HD8),
                    a0_R.rearrange("p (j o t) -> p t o j", t=T, o=1)[:, c * part:(c + 1) * part, :, :]
                    .broadcast_to([P, part, HD8, HD8]), ALU.mult).then_inc(s_stat, 1)
                dve.wait_ge(s_stat, 2 * c + 1)
                dve.tensor_reduce(W3.rearrange("p i t -> p t i")[:, c * part:(c + 1) * part, :], prod4, AX_X,
                                  ALU.add).then_inc(s_stat, 1)
                dve.wait_ge(s_stat, 2 * c + 2)
            dve.wait_ge(s_wkv, 1)
            fb = a0_F[:, 1:T + 1].rearrange("p (o t) -> p o t", o=1).broadcast_to([P, HD8, T])
            dve.tensor_tensor(W3, W3, fb, ALU.mult).then_inc(s_wkv, 1)
            dve.wait_ge(s_wkv, 2)
            for c in range(NCH):
                dve.bn_stats(a0_small[:, 8 + 6 * c:14 + 6 * c], chunk(a0_tmp, c)).then_inc(s_wkv, 1)
            dve.wait_ge(s_wkv, 6)
            dve.bn_aggr(a0_small[:, 40:42], a0_small[:, 8:8 + 6 * NCH].rearrange("p (c s) -> p c s", s=6))\
               .then_inc(s_stat, 1)
            dve.wait_ge(s_rstd, 2)
            dve.tensor_scalar(a0_tmp, a0_tmp, a0_small[:, 40:41], a0_small[:, 43:44], ALU.subtract, ALU.mult)\
               .then_inc(s_wkv, 1)
            dve.wait_ge(s_backed, 16)
            dve.tensor_scalar(a0_R, a0_R, a0_vec[:, 9:10], a0_vec[:, 10:11], ALU.mult, ALU.add).then_inc(s_gn, 1)
            for c in range(NCH):
                dve.wait_ge(s_o, c + 1)
                dve.scalar_tensor_tensor(chunk(a0_G, c), PS[:, c, :], a0_vec[:, 8:9], chunk(a0_G, c),
                                         ALU.add, ALU.mult).then_inc(s_x, 1)
                dve.wait_ge(s_x, c + 1)
                dve.tensor_tensor(chunk(XO, c), chunk(XO, c), chunk(a0_G, c), ALU.add)

        a0_KEs = a0.take(N)
        a0_big = arena[:, a0.at:a0.at + (T // 4) * 64]
        a0.take((T // 4) * 64)

        def a0_scalar(act, n0):
            ln_scalar(act, n0)
            act.wait_ge(s_a0w, 16 * 7)
            act.wait_ge(ln_scaled, (n0 + 1) * NCH)
            for k in range(4):
                act.activation(a0_mix[:, k * N:(k + 1) * N], XN[:], ACT.Identity, scale=a0_vec[:, k:k + 1])\
                   .then_inc(s_part, 1)
            act.activation(a0_head[:, 2:4], a0_head[:, 0:2], ACT.Sigmoid).then_inc(s_unit, 1)
            for k in range(4):
                for c in range(NCH):
                    act.wait_ge(s_proj, k * NCH + c + 1)
                    bank = PS[:, (k % 2) * 4 + c, :]
                    to = chunk(a0_out[:, k * N:(k + 1) * N], c) if k < 3 else chunk(a0_G, c)
                    act.activation(to, bank, ACT.Sigmoid if k in (0, 3) else ACT.Identity,
                                   bias=a0_vec[:, 4 + k:5 + k]).then_inc(s_act, 1)
            log_exp_tables(act)
            act.wait_ge(s_n2, 3)
            act.activation(a0_rn, a0_rn, ACT.Ln, scale=float(2 ** 24)).then_inc(s_rn, 1)
            act.wait_ge(s_rn, 1)
            act.activation(a0_rn, a0_rn, ACT.Exp, bias=eps[:, 1:2], scale=-0.5).then_inc(s_rn, 1)
            act.wait_ge(s_unit, 5)
            with act.Fori(0, T // STEPS) as turn:
                for q in range(STEPS):
                    g = turn * STEPS + q
                    n = turn * STEPS * 3 + 3 * q
                    act.wait_ge(scan_step, turn * STEPS * 7 + 7 * q + 7)
                    after = a0_H[:, ds(g * 64 + 64, 64)]
                    act.activation(a0_step[:, 192:256], after, ACT.Square, accum_out=a0_small[:, 0:1])\
                       .then_inc(scan_norm, 1)
                    act.wait_ge(scan_norm, n + 4)
                    act.activation(a0_small[:, 1:2], a0_small[:, 0:1], ACT.Ln, bias=eps[:, 3:4],
                                   scale=1.0 / MAX_NORM2).then_inc(scan_norm, 1)
                    act.wait_ge(scan_norm, n + 5)
                    act.activation(a0_small[:, 2:3], a0_small[:, 1:2], ACT.Exp, scale=-0.5).then_inc(scan_norm, 1)
            act.wait_ge(s_stat, 9)
            act.activation(a0_small[:, 42:43], a0_small[:, 41:42], ACT.Ln, bias=eps[:, 0:1]).then_inc(s_rstd, 1)
            act.wait_ge(s_rstd, 1)
            act.activation(a0_small[:, 43:44], a0_small[:, 42:43], ACT.Exp, scale=-0.5).then_inc(s_rstd, 1)

        def a0_tensor(pe, n0):
            ln_tensor(pe, n0, XO)
            for k in range(4):
                pe.wait_ge(s_mix, k + 1)
                for c in range(NCH):
                    if k >= 2:
                        pe.wait_ge(s_act, (k - 2) * NCH + c + 1)
                    if k == 0 and c == 0:
                        pe.wait_ge(ln_scaled, (n0 + 1) * NCH)
                    pe.matmul(PS[:, (k % 2) * 4 + c, :], a0_w[k], chunk(a0_mix[:, k * N:(k + 1) * N], c),
                              start=True, stop=True).then_inc(s_proj, 1)
            pe.wait_ge(s_gn, 1)
            for c in range(NCH):
                pe.matmul(PS[:, c, :], a0_w[4], chunk(a0_R, c), start=True, stop=True).then_inc(s_o, 1)

        a1 = Space(0)
        a1_w = [a1.take(C) for _ in range(4)]
        a1_vec = a1.take(8)
        a1_tab = a1.take(6 * T).rearrange("p (k t) -> p k t", k=6)
        a1_cross = a1.take(T)
        a1_keep = a1.take(N)
        a1_S = a1.take(N)
        a1_Z = a1.take(N)
        a1_D = [a1.take(N) for _ in range(2)]
        a1_GY = a1.take(N)
        a1_sq = a1.take(N)
        a1_loaded = sem("a1_loaded")
        a1_proj = sem("a1_proj")
        a1_sigmoid = sem("a1_sigmoid")
        a1_gate = sem("a1_gate")
        a1_z = sem("a1_z")
        a1_keep_ready = sem("a1_keep_ready")
        a1_down = sem("a1_down")
        a1_run = sem("a1_run")
        a1_up = sem("a1_up")
        a1_cross_ready = sem("a1_cross_ready")
        a1_h = sem("a1_h")
        a1_squared = sem("a1_squared")
        a1_mean = sem("a1_mean")
        a1_log = sem("a1_log")
        a1_rms = sem("a1_rms")
        a1_normed = sem("a1_normed")
        a1_y = sem("a1_y")
        bt = lambda a: a.rearrange("p (b t) -> p b t", t=T)

        def a1_sync(sp):
            for k, name in enumerate(("za", "z", "ya", "y")):
                sp.dma_start(a1_w[k], d[f"a1_W_{name}"]).then_inc(a1_loaded, 16)
            sp.dma_start(a1_vec, d["a1_vectors"]).then_inc(a1_loaded, 16)
            sp.dma_start(a1_tab, d["c_phazor"].rearrange("p (k t) -> p k t", k=6)).then_inc(a1_loaded, 16)

        def a1_tensor(pe, n0):
            ln_tensor(pe, n0, XO)
            pe.wait_ge(a1_loaded, 16 * 6)
            pe.wait_ge(ln_scaled, (n0 + 1) * NCH)
            for k in range(3):
                for c in range(NCH):
                    if k == 2:
                        pe.wait_ge(a1_gate, c + 1)
                    pe.matmul(PS[:, (k % 2) * 4 + c, :], a1_w[k], chunk(XN, c), start=True, stop=True)\
                      .then_inc(a1_proj, 1)
            for c in range(NCH):
                pe.wait_ge(a1_squared, c + 1)
                pe.matmul(PS[:, 4 + c, :], mean_w[:], chunk(a1_sq, c), start=True, stop=True).then_inc(a1_mean, 1)
            for c in range(NCH):
                pe.wait_ge(a1_normed, c + 1)
                pe.matmul(PS[:, c, :], a1_w[3], chunk(a1_Z, c), start=True, stop=True).then_inc(a1_proj, 1)

        def a1_scalar(act, n0):
            ln_scalar(act, n0)
            for k, of in ((0, 0), (1, 2)):
                for c in range(NCH):
                    act.wait_ge(a1_proj, of * NCH + c + 1)
                    if k == 1:
                        act.wait_ge(a1_gate, c + 1)
                    act.activation(chunk(a1_S, c), PS[:, c, :], ACT.Sigmoid, bias=a1_vec[:, of:of + 1])\
                       .then_inc(a1_sigmoid, 1)
            log_exp_tables(act)
            for c in range(NCH):
                act.wait_ge(a1_h, c + 1)
                act.activation(chunk(a1_sq, c), chunk(a1_D[0], c), ACT.Square).then_inc(a1_squared, 1)
                act.wait_ge(a1_mean, c + 1)
                act.wait_ge(a1_gate, NCH + c + 1)
                act.activation(chunk(a1_S, c), PS[:, 4 + c, :], ACT.Ln, bias=eps[:, 2:3]).then_inc(a1_log, 1)
                act.wait_ge(a1_log, c + 1)
                act.activation(chunk(a1_S, c), chunk(a1_S, c), ACT.Exp, scale=-0.5).then_inc(a1_rms, 1)

        def a1_vector(dve, n0):
            ln_vector(dve, n0, XO, XN)
            dve.memset(a1_keep, 1.0).then_inc(a1_keep_ready, 1)
            dve.wait_ge(a1_keep_ready, 1)
            dve.memset(bt(a1_keep)[:, :, 0:1], 0.0).then_inc(a1_keep_ready, 1)
            dve.wait_ge(a1_loaded, 16 * 6)
            dve.tensor_scalar(a1_cross, a1_tab[:, 4, :], a1_vec[:, 5:6], None, ALU.mult).then_inc(a1_cross_ready, 1)
            dve.wait_ge(a1_cross_ready, 1)
            dve.scalar_tensor_tensor(a1_cross, a1_tab[:, 5, :], a1_vec[:, 6:7], a1_cross, ALU.mult, ALU.add)\
               .then_inc(a1_cross_ready, 1)
            for c in range(NCH):
                dve.wait_ge(a1_sigmoid, c + 1)
                dve.scalar_tensor_tensor(chunk(a1_Z, c), PS[:, c, :], a1_vec[:, 0:1], chunk(a1_S, c),
                                         ALU.add, ALU.mult).then_inc(a1_gate, 1)
                dve.wait_ge(a1_gate, c + 1)
                dve.wait_ge(a1_proj, NCH + c + 1)
                dve.scalar_tensor_tensor(chunk(a1_Z, c), PS[:, 4 + c, :], a1_vec[:, 1:2], chunk(a1_Z, c),
                                         ALU.add, ALU.mult).then_inc(a1_z, 1)
            dve.wait_ge(a1_z, NCH)
            dve.wait_ge(a1_keep_ready, 2)
            for k in range(2):
                table_of = lambda j: a1_tab[:, j:j + 1, :].broadcast_to([P, B, T])
                D = a1_D[k]
                dve.tensor_tensor(bt(D), bt(a1_Z), table_of(k), ALU.mult).then_inc(a1_down, 1)
                dve.wait_ge(a1_down, k + 1)
                dve.tensor_tensor_scan(D, a1_keep, D, 0.0, ALU.mult, ALU.add).then_inc(a1_run, 1)
                dve.wait_ge(a1_run, k + 1)
                dve.tensor_tensor(bt(D), bt(D), table_of(2 + k), ALU.mult).then_inc(a1_up, 1)
                dve.wait_ge(a1_up, k + 1)
            dve.wait_ge(a1_cross_ready, 2)
            cross = a1_cross.rearrange("p (o t) -> p o t", o=1).broadcast_to([P, CH // T, T])
            for c in range(NCH):
                dve.tensor_tensor(bt(chunk(a1_D[1], c)), bt(chunk(a1_D[1], c)), cross, ALU.add).then_inc(a1_up, 1)
                dve.wait_ge(a1_up, 3 + c)
                dve.tensor_tensor(chunk(a1_D[0], c), chunk(a1_D[0], c), chunk(a1_D[1], c), ALU.add).then_inc(a1_h, 1)
            for c in range(NCH):
                dve.wait_ge(a1_sigmoid, NCH + c + 1)
                dve.scalar_tensor_tensor(chunk(a1_GY, c), PS[:, c, :], a1_vec[:, 2:3], chunk(a1_S, c),
                                         ALU.add, ALU.mult).then_inc(a1_gate, 1)
            for c in range(NCH):
                dve.wait_ge(a1_rms, c + 1)
                dve.scalar_tensor_tensor(chunk(a1_Z, c), chunk(a1_D[0], c), a1_vec[:, 4:5], chunk(a1_S, c),
                                         ALU.mult, ALU.mult).then_inc(a1_normed, 1)
            for c in range(NCH):
                dve.wait_ge(a1_proj, 3 * NCH + c + 1)
                dve.scalar_tensor_tensor(chunk(a1_GY, c), PS[:, c, :], a1_vec[:, 3:4], chunk(a1_GY, c),
                                         ALU.add, ALU.mult).then_inc(a1_y, 1)
                dve.wait_ge(a1_y, c + 1)
                dve.tensor_tensor(chunk(XO, c), chunk(XO, c), chunk(a1_GY, c), ALU.add)

        SMALL = 16
        GROUPS, HEADS_IN_GROUP, GROUP = 4, 4, 32
        PAIRS8 = SMALL // 2
        hd = Space(0)
        hd_w = [hd.take(C) for _ in range(5)]
        hd_only = hd.take(HEADS_IN_GROUP)
        hd_x = hd.take(T)
        hd_q = hd.take(T)
        hd_k = hd.take(T)
        hd_m = [hd.take(T) for _ in range(HEADS_IN_GROUP)]
        hd_v = hd.take(2 * C).rearrange("p (t n) -> p t n", t=2)
        VGROUP = HEADS_IN_GROUP * 40
        hd_vm = hd.take(2 * GROUPS * VGROUP).rearrange("p (t n) -> p t n", t=2)
        hd_e = [hd.take(4 * T).rearrange("p (h t q) -> p h t q", h=2, t=2) for _ in range(2)]
        hd_st = [hd.take(16) for _ in range(2)]
        hd_Z = hd.take(N)
        hd_sq = hd.take(N)
        hd_rn = hd.take(N)
        hd_y = hd.take(N)
        hd_loaded = sem("hd_loaded")
        hd_zeroed = sem("hd_zeroed")
        hd_entered = sem("hd_entered")
        hd_proj = sem("hd_proj")
        hd_projected = sem("hd_projected")
        hd_masked = sem("hd_masked")
        hd_scores = sem("hd_scores")
        hd_max = sem("hd_max")
        hd_bias = sem("hd_bias")
        hd_exp = sem("hd_exp")
        hd_recip = sem("hd_recip")
        hd_v_ready = sem("hd_v_ready")
        hd_out = sem("hd_out")
        hd_copied = sem("hd_copied")
        tail_lin = sem("tail_lin")
        tail_sq = sem("tail_sq")
        tail_sum = sem("tail_sum")
        tail_floor = sem("tail_floor")
        tail_log = sem("tail_log")
        tail_rn = sem("tail_rn")
        tail_z = sem("tail_z")
        tail_gelu = sem("tail_gelu")
        MIX_SCALE = float(1.0 / np.sqrt(np.float32(C)))

        def mix_sync(sp):
            for k, name in enumerate(("Wq", "Wk", "Wv", "Wo", "Wff")):
                sp.dma_start(hd_w[k], d[f"L1_ffn_{name}"]).then_inc(hd_loaded, 16)
            sp.dma_start(hd_only, d["c_only"]).then_inc(hd_loaded, 16)

        def project_tensor(pe, g):
            pe.wait_ge(hd_entered, g + 1)
            for k in range(2):
                last = pe.matmul(PS[:, 5, k * T:(k + 1) * T], hd_w[k], hd_x, start=True, stop=True)
            last.then_inc(hd_proj, 1)
            for t in range(2):
                last = pe.matmul(PS[:, 6, t * C:(t + 1) * C], hd_x[:, t * P:(t + 1) * P], hd_w[2], start=True, stop=True)
            last.then_inc(hd_proj, 1)

        def mix_tensor(pe, run, call, n0):
            ln_tensor(pe, n0, XO)
            wait_alone(pe, hd_loaded, 16 * 6 * (run + 1))
            with pe.Fori(0, B) as b:
                g = run * B + b + 1
                project_tensor(pe, g)

                def scores(u):
                    if u >= 2:
                        wait_alone(pe, hd_exp, nth(g, PAIRS8, u - 2))
                    for s in range(2):
                        grp, v = divmod(2 * u + s, HEADS_IN_GROUP)
                        rows = slice(grp * GROUP, (grp + 1) * GROUP)
                        for t in range(2):
                            last = pe.matmul(PS[:, (u % 2) * 2 + s, t * T:(t + 1) * T],
                                             hd_m[v][rows, t * P:(t + 1) * P], hd_q[rows, :], start=True, stop=True)
                    last.then_inc(hd_scores, 1)

                def heads(u):
                    pe.wait_ge(hd_v_ready, nth(g, PAIRS8, u))
                    for s in range(2):
                        grp, v = divmod(2 * u + s, HEADS_IN_GROUP)
                        at = grp * VGROUP + v * GROUP
                        for t in range(2):
                            last = pe.matmul(PS[grp * GROUP:(grp + 1) * GROUP, 4, 0:T], hd_vm[:, t, at:at + GROUP],
                                             hd_e[u % 2][:, s, t, :], start=(v == 0 and t == 0),
                                             stop=(v == HEADS_IN_GROUP - 1 and t == 1), skip_group_check=True)
                    last.then_inc(hd_out, 1)
                wait_alone(pe, hd_masked, (g + 1) * HEADS_IN_GROUP)
                wait_alone(pe, hd_projected, (g + 1) * 3)
                scores(0)
                scores(1)
                for u in range(PAIRS8):
                    heads(u)
                    if u + 2 < PAIRS8:
                        scores(u + 2)
            for k in range(2):
                n = 2 * call + k
                for c in range(NCH):
                    if k == 0 and c == 0:
                        pe.wait_ge(hd_copied, (run + 1) * B + 1)
                    if k == 1:
                        pe.wait_ge(tail_z, nth(n - 1, NCH, c))
                    pe.matmul(PS[:, c, :], hd_w[3 + k], chunk(hd_Z, c), start=True, stop=True).then_inc(tail_lin, 1)
                for c in range(NCH):
                    pe.wait_ge(tail_sq, nth(n, NCH, c))
                    pe.matmul(PS[:, 4 + c, :], mean_w[:], chunk(hd_sq, c), start=True, stop=True).then_inc(tail_sum, 1)

        def project_scalar(act, g, b):
            act.wait_ge(hd_proj, g * 2)
            act.activation(hd_x, XN[:, ds(b * T, T)], ACT.Copy).then_inc(hd_entered, 1)

        def mix_scalar(act, run, call, n0):
            ln_scalar(act, n0)
            wait_alone(act, ln_scaled, (n0 + 1) * NCH)
            with act.Fori(0, B) as b:
                g = run * B + b + 1
                project_scalar(act, g, b)
                act.wait_ge(hd_proj, g * 2 + 1)
                act.wait_ge(hd_scores, g * PAIRS8)
                act.activation(hd_q, PS[:, 5, 0:T], ACT.Copy).then_inc(hd_projected, 1)
                act.wait_ge(hd_masked, g * HEADS_IN_GROUP)
                act.activation(hd_k, PS[:, 5, T:2 * T], ACT.Copy).then_inc(hd_projected, 1)
                act.wait_ge(hd_proj, g * 2 + 2)
                act.wait_ge(hd_v_ready, g * PAIRS8)
                act.activation(hd_v, PS[:, 6, 0:2 * C].rearrange("p (t n) -> p t n", t=2), ACT.Copy)\
                   .then_inc(hd_projected, 1)
                for u in range(PAIRS8):
                    act.wait_ge(hd_bias, nth(g, PAIRS8, u))
                    if u >= 2:
                        act.wait_ge(hd_out, nth(g, PAIRS8, u - 2))
                    for s in range(2):
                        for t in range(2):
                            st = hd_st[u % 2]
                            last = act.activation(hd_e[u % 2][:, s, t, :], PS[:, (u % 2) * 2 + s, t * T:(t + 1) * T],
                                                  ACT.Exp, bias=st[:, 4 + 2 * s + t:5 + 2 * s + t], scale=MIX_SCALE,
                                                  accum_out=st[:, 8 + 2 * s + t:9 + 2 * s + t])
                    last.then_inc(hd_exp, 1)
                act.wait_ge(hd_out, (g + 1) * PAIRS8)
                act.activation(hd_Z[:, ds(b * T, T)], PS[:, 4, 0:T], ACT.Copy).then_inc(hd_copied, 1)
            for k in range(2):
                n = 2 * call + k
                for c in range(NCH):
                    act.wait_ge(tail_lin, nth(n, NCH, c))
                    act.activation(chunk(hd_sq, c), PS[:, c, :], ACT.Square).then_inc(tail_sq, 1)
                for c in range(NCH):
                    act.wait_ge(tail_floor, nth(n, NCH, c))
                    act.activation(chunk(hd_rn, c), chunk(hd_rn, c), ACT.Ln, scale=float(C * 2 ** 24)).then_inc(tail_log, 1)
                    act.wait_ge(tail_log, nth(n, NCH, c))
                    act.activation(chunk(hd_rn, c), chunk(hd_rn, c), ACT.Exp, bias=eps[:, 1:2], scale=-0.5)\
                       .then_inc(tail_rn, 1)
            for c in range(NCH):
                act.wait_ge(tail_z, nth(2 * call + 1, NCH, c))
                act.activation(chunk(hd_y, c), chunk(hd_Z, c), ACT.Gelu).then_inc(tail_gelu, 1)

        def mask_vector(dve, g, source, which):
            dve.wait_ge(hd_projected, g * 3 + which)
            dve.wait_ge(hd_scores, g * PAIRS8)
            for v in range(HEADS_IN_GROUP):
                dve.tensor_scalar(hd_m[v], source, hd_only[:, v:v + 1], None, ALU.mult).then_inc(hd_masked, 1)

        def mix_vector(dve, run, call, n0):
            ln_vector(dve, n0, XO, XN)
            dve.memset(hd_vm, 0.0).then_inc(hd_zeroed, 1)
            wait_alone(dve, hd_loaded, 16 * 6 * (run + 1))
            wait_alone(dve, hd_zeroed, run + 1)
            with dve.Fori(0, B) as b:
                g = run * B + b + 1
                mask_vector(dve, g, hd_k, 2)

                def shift(u):
                    st = hd_st[u % 2]
                    dve.wait_ge(hd_scores, nth(g, PAIRS8, u))
                    dve.tensor_reduce(st[:, 0:4], PS[:, (u % 2) * 2:(u % 2) * 2 + 2, :]
                                      .rearrange("p h (t q) -> p (h t) q", t=2), AX_X, ALU.max).then_inc(hd_max, 1)
                    dve.wait_ge(hd_max, nth(g, PAIRS8, u))
                    dve.tensor_scalar(st[:, 4:8], st[:, 0:4], -MIX_SCALE, None, ALU.mult).then_inc(hd_bias, 1)

                def values(u):
                    st = hd_st[u % 2]
                    grp, v = divmod(2 * u, HEADS_IN_GROUP)
                    dve.wait_ge(hd_exp, nth(g, PAIRS8, u))
                    dve.reciprocal(st[:, 12:16], st[:, 8:12]).then_inc(hd_recip, 1)
                    dve.wait_ge(hd_recip, nth(g, PAIRS8, u))
                    if u == 0:
                        dve.wait_ge(hd_projected, (g + 1) * 3)
                    dve.wait_ge(hd_out, g * PAIRS8)
                    at = grp * VGROUP + v * 40
                    to = hd_vm[:, :, at:at + 80].rearrange("p t (h x) -> p t h x", h=2)[:, :, :, 0:8]
                    fr = hd_v[:, :, u * 16:(u + 1) * 16].rearrange("p t (h x) -> p t h x", h=2)
                    rc = st[:, 12:16].rearrange("p (h t o) -> p t h o", h=2, o=1).broadcast_to([P, 2, 2, 8])
                    dve.tensor_tensor(to, fr, rc, ALU.mult).then_inc(hd_v_ready, 1)
                shift(0)
                for u in range(PAIRS8):
                    if u + 1 < PAIRS8:
                        shift(u + 1)
                    values(u)
            for k in range(2):
                n = 2 * call + k
                for c in range(NCH):
                    dve.wait_ge(tail_sum, nth(n, NCH, c))
                    dve.tensor_scalar(chunk(hd_rn, c), PS[:, 4 + c, :], 1e-24 / C, None, ALU.max).then_inc(tail_floor, 1)
                for c in range(NCH):
                    dve.wait_ge(tail_rn, nth(n, NCH, c))
                    dve.tensor_tensor(chunk(hd_Z, c), PS[:, c, :], chunk(hd_rn, c), ALU.mult).then_inc(tail_z, 1)
            for c in range(NCH):
                dve.wait_ge(tail_gelu, nth(call, NCH, c))
                dve.tensor_tensor(chunk(XO, c), chunk(XO, c), chunk(hd_y, c), ALU.add)

        b1 = Space(hd.at)
        b1_ks = b1.take(3 * P)
        b1_mask = b1.take(2 * P)
        BLOCKS = 3 * P
        b1_s = [b1.take(2 * BLOCKS).rearrange("p (h j) -> p h j", h=2) for _ in range(2)]
        b1_e = [b1.take(2 * BLOCKS).rearrange("p (h j) -> p h j", h=2) for _ in range(2)]
        b1_t = [b1.take(2 * BLOCKS).rearrange("p (h j) -> p h j", h=2) for _ in range(2)]
        b1_added = sem("b1_added")
        b1_max = sem("b1_max")
        b1_sum = sem("b1_sum")
        b1_probs = sem("b1_probs")
        b1_turned = sem("b1_turned")
        b1_copied = sem("b1_copied")
        b1_lin = sem("b1_lin")
        B1_SCALE = float(1.0 / np.sqrt(8.0))
        ROW_BLOCKS = ((0, P), (P, BLOCKS))

        def b1_sync(sp):
            for k, name in enumerate(("wq", "wk", "wv", "wo")):
                sp.dma_start(hd_w[k], d[f"b1_{name}"]).then_inc(hd_loaded, 16)
            sp.dma_start(hd_only, d["c_only"]).then_inc(hd_loaded, 16)
            sp.dma_start(b1_mask, d["c_causal"]).then_inc(hd_loaded, 16)

        def b1_tensor(pe, run, n0):
            ln_tensor(pe, n0, XO)
            wait_alone(pe, hd_loaded, 16 * 6 * (run + 1))
            with pe.Fori(0, B) as b:
                g = run * B + b + 1
                pe.wait_ge(hd_entered, g + 1)
                for k in range(2):
                    last = pe.matmul(PS[:, 7, k * T:(k + 1) * T], hd_w[k], hd_x, start=True, stop=True)
                last.then_inc(hd_proj, 1)

                def scores(u):
                    if u >= 2:
                        wait_alone(pe, b1_added, nth(b, 2 * PAIRS8, 2 * (u - 2) + 1))
                    for s in range(2):
                        grp, v = divmod(2 * u + s, HEADS_IN_GROUP)
                        rows = slice(grp * GROUP, (grp + 1) * GROUP)
                        bank = (u % 2) * 2 + s
                        pe.matmul(PS[:, bank, 0:P], hd_m[v][rows, 0:P], b1_ks[rows, 0:P], start=True, stop=True)
                        last = pe.matmul(PS[:, bank, P:BLOCKS], hd_m[v][rows, P:T], b1_ks[rows, P:BLOCKS],
                                         start=True, stop=True)
                    last.then_inc(hd_scores, 1)

                def turn(u):
                    if u >= 1:
                        pe.wait_ge(b1_copied, nth(b, PAIRS8, u - 1))
                    pe.wait_ge(b1_probs, nth(b, PAIRS8, u))
                    for s in range(2):
                        for k, at in enumerate((0, 2, 1)):
                            last = pe.transpose(PS[:, 4 + s, at * P:(at + 1) * P],
                                                b1_e[u % 2][:, s, k * P:(k + 1) * P], ident[:])
                    last.then_inc(b1_turned, 1)

                def heads(u):
                    pe.wait_ge(b1_copied, nth(b, PAIRS8, u))
                    if u == 0:
                        pe.wait_ge(hd_v_ready, (g + 1) * PAIRS8)
                    for s in range(2):
                        grp, v = divmod(2 * u + s, HEADS_IN_GROUP)
                        rows = slice(grp * GROUP, (grp + 1) * GROUP)
                        at = grp * VGROUP + v * GROUP
                        turned_probs = b1_t[u % 2][:, s, :]
                        pe.matmul(PS[rows, 6, 0:T], hd_vm[:, 0, at:at + GROUP], turned_probs[:, 0:T],
                                  start=(v == 0), stop=False, skip_group_check=True)
                        last = pe.matmul(PS[rows, 6, P:T], hd_vm[:, 1, at:at + GROUP], turned_probs[:, T:BLOCKS],
                                         start=False, stop=(v == HEADS_IN_GROUP - 1), skip_group_check=True)
                    last.then_inc(hd_out, 1)
                wait_alone(pe, hd_masked, (g + 1) * HEADS_IN_GROUP)
                wait_alone(pe, hd_projected, g * 3 + 2)
                for t in range(2):
                    last = pe.matmul(PS[:, 7, t * C:(t + 1) * C], hd_x[:, t * P:(t + 1) * P], hd_w[2], start=True, stop=True)
                last.then_inc(hd_proj, 1)
                scores(0)
                scores(1)
                for u in range(PAIRS8):
                    turn(u)
                    if u > 0:
                        heads(u - 1)
                    if u + 2 < PAIRS8:
                        scores(u + 2)
                heads(PAIRS8 - 1)
            pe.wait_ge(hd_copied, (run + 1) * B + 1)
            for c in range(NCH):
                pe.matmul(PS[:, c, :], hd_w[3], chunk(hd_Z, c), start=True, stop=True).then_inc(b1_lin, 1)

        def b1_scalar(act, run, n0):
            ln_scalar(act, n0)
            wait_alone(act, ln_scaled, (n0 + 1) * NCH)
            with act.Fori(0, B) as b:
                g = run * B + b + 1
                act.wait_ge(hd_proj, g * 2)
                act.activation(hd_x, XN[:, ds(b * T, T)], ACT.Copy).then_inc(hd_entered, 1)
                act.wait_ge(hd_proj, g * 2 + 1)
                act.wait_ge(hd_scores, g * PAIRS8)
                act.activation(b1_ks[:, 0:T], PS[:, 7, T:2 * T], ACT.Copy)
                act.activation(b1_ks[:, T:T + P], PS[:, 7, T:T + P], ACT.Copy).then_inc(hd_projected, 1)
                act.wait_ge(hd_masked, g * HEADS_IN_GROUP)
                act.activation(hd_q, PS[:, 7, 0:T], ACT.Copy).then_inc(hd_projected, 1)
                act.wait_ge(hd_proj, g * 2 + 2)
                act.wait_ge(hd_v_ready, g * PAIRS8)
                act.activation(hd_v, PS[:, 7, 0:2 * C].rearrange("p (t n) -> p t n", t=2), ACT.Copy)\
                   .then_inc(hd_projected, 1)

                def copy(u):
                    act.wait_ge(b1_turned, nth(b, PAIRS8, u))
                    if u >= 2:
                        act.wait_ge(hd_out, nth(g, PAIRS8, u - 2))
                    act.activation(b1_t[u % 2], PS[:, 4:6, 0:BLOCKS], ACT.Copy).then_inc(b1_copied, 1)
                for u in range(PAIRS8):
                    act.wait_ge(hd_bias, nth(g, PAIRS8, u))
                    if u >= 2:
                        act.wait_ge(b1_turned, nth(b, PAIRS8, u - 2))
                    for s in range(2):
                        for t, (lo, hi) in enumerate(ROW_BLOCKS):
                            st = hd_st[u % 2]
                            last = act.activation(b1_e[u % 2][:, s, lo:hi], b1_s[u % 2][:, s, lo:hi], ACT.Exp,
                                                  bias=st[:, 4 + 2 * t + s:5 + 2 * t + s], scale=B1_SCALE,
                                                  accum_out=st[:, 8 + 2 * t + s:9 + 2 * t + s])
                    last.then_inc(hd_exp, 1)
                    if u > 0:
                        copy(u - 1)
                copy(PAIRS8 - 1)
                act.wait_ge(hd_out, (g + 1) * PAIRS8)
                act.activation(hd_Z[:, ds(b * T, T)], PS[:, 6, 0:T], ACT.Copy).then_inc(hd_copied, 1)

        def b1_vector(dve, run, n0):
            ln_vector(dve, n0, XO, XN)
            dve.memset(hd_vm, 0.0).then_inc(hd_zeroed, 1)
            wait_alone(dve, hd_loaded, 16 * 6 * (run + 1))
            wait_alone(dve, hd_zeroed, run + 1)
            with dve.Fori(0, B) as b:
                g = run * B + b + 1
                dve.wait_ge(hd_projected, g * 3 + 2)
                dve.wait_ge(hd_scores, g * PAIRS8)
                for v in range(HEADS_IN_GROUP):
                    dve.tensor_scalar(hd_m[v], hd_q, hd_only[:, v:v + 1], None, ALU.mult).then_inc(hd_masked, 1)
                dve.wait_ge(hd_projected, g * 3 + 3)
                dve.wait_ge(hd_out, g * PAIRS8)
                for t in range(2):
                    to = hd_vm[:, t, :].rearrange("p (h x) -> p h x", x=40)[:, :, 0:8]
                    last = dve.tensor_copy(to, hd_v[:, t, :].rearrange("p (h x) -> p h x", x=8))
                last.then_inc(hd_v_ready, PAIRS8)

                def shift(u):
                    st, S = hd_st[u % 2], b1_s[u % 2]
                    dve.wait_ge(hd_scores, nth(g, PAIRS8, u))
                    if u >= 2:
                        dve.wait_ge(hd_exp, nth(g, PAIRS8, u - 2))
                    banks = PS[:, (u % 2) * 2:(u % 2) * 2 + 2, :]
                    mask = b1_mask.rearrange("p (o j) -> p o j", o=1).broadcast_to([P, 2, 2 * P])
                    dve.tensor_copy(S[:, :, 2 * P:BLOCKS], banks[:, :, 2 * P:BLOCKS]).then_inc(b1_added, 1)
                    dve.tensor_tensor(S[:, :, 0:2 * P], banks[:, :, 0:2 * P], mask, ALU.add).then_inc(b1_added, 1)
                    dve.wait_ge(b1_added, nth(b, 2 * PAIRS8, 2 * u + 1))
                    for t, (lo, hi) in enumerate(ROW_BLOCKS):
                        dve.tensor_reduce(st[:, 2 * t:2 * t + 2], S[:, :, lo:hi], AX_X, ALU.max)\
                           .then_inc(hd_max if t else b1_max, 1)
                    dve.wait_ge(b1_max, nth(b, PAIRS8, u))
                    dve.wait_ge(hd_max, nth(g, PAIRS8, u))
                    dve.tensor_scalar(st[:, 4:8], st[:, 0:4], -B1_SCALE, None, ALU.mult).then_inc(hd_bias, 1)

                def normalise(u):
                    st, e = hd_st[u % 2], b1_e[u % 2]
                    dve.wait_ge(hd_exp, nth(g, PAIRS8, u))
                    dve.tensor_scalar(st[:, 12:16], st[:, 8:12], 1e-8, None, ALU.add).then_inc(b1_sum, 1)
                    dve.wait_ge(b1_sum, nth(b, PAIRS8, u))
                    dve.reciprocal(st[:, 12:16], st[:, 12:16]).then_inc(hd_recip, 1)
                    dve.wait_ge(hd_recip, nth(g, PAIRS8, u))
                    for s in range(2):
                        for t, (lo, hi) in enumerate(ROW_BLOCKS):
                            last = dve.tensor_scalar(e[:, s, lo:hi], e[:, s, lo:hi], st[:, 12 + 2 * t + s:13 + 2 * t + s],
                                                     None, ALU.mult)
                    last.then_inc(b1_probs, 1)
                shift(0)
                for u in range(PAIRS8):
                    if u + 1 < PAIRS8:
                        shift(u + 1)
                    normalise(u)
            for c in range(NCH):
                dve.wait_ge(b1_lin, c + 1)
                dve.tensor_tensor(chunk(XO, c), chunk(XO, c), PS[:, c, :], ALU.add)

        BR, BH = 4, 16
        UNITS = BH
        IN_GROUP = 4
        NGROUPS = UNITS // IN_GROUP
        SIG = float(np.pi / np.sqrt(3.0))
        b0 = Space(0)
        b0_wq = b0.take(2 * BR * C)
        b0_wk = b0.take(2 * C)
        b0_wv = b0.take(BR * C)
        b0_wo = b0.take(C)
        b0_vec = b0.take(16)
        b0_bv = b0.take(BR * C)
        b0_ones8 = b0.take(P)
        b0_only = b0.take(BH)
        b0_tab = b0.take(2 * T).rearrange("p (k t) -> p k t", k=2)
        b0_tri = b0.take(P)
        b0_sink = b0.take(2 * BR * BH)
        b0_null = b0.take(BR * C)
        b0_Q = b0.take(BR * N).rearrange("p (r t) -> p r t", r=BR)
        b0_K = b0.take(N)
        b0_V = b0.take(2 * B * BR * BH * 9).rearrange("p (t h e) -> p t h e", h=BR * BH, e=9)
        b0_KM = [b0.take(T) for _ in range(2 * IN_GROUP)]
        b0_m = [b0.take(3 * CH) for _ in range(2)]
        b0_w = b0.take(2 * IN_GROUP * 3 * CH).rearrange("p (r u j) -> p r u j", r=2, u=IN_GROUP)
        b0_sg = [b0.take(3 * CH) for _ in range(2)]
        b0_den = b0.take(2 * IN_GROUP * BR)
        b0_ctx = b0.take(2 * IN_GROUP * BR * 8)
        b0_tmp = b0_sg[0]
        b0_rk = b0_w.rearrange("p r u j -> p (r u j)")[:, 0:N]
        b0_sq = b0_w.rearrange("p r u j -> p (r u j)")[:, N:2 * N]
        b0_ct = b0_Q.rearrange("p r t -> p (r t)")[:, 0:N]
        CT = XN[:].rearrange("p (t f) -> p t f", f=C)
        b0_loaded = sem("b0_loaded")
        b0_ones = sem("b0_ones")
        b0_tanh = sem("b0_tanh")
        b0_sinks = sem("b0_sinks")
        b0_proj = sem("b0_proj")
        b0_freed = sem("b0_freed")
        b0_roped = sem("b0_roped")
        b0_ksq = sem("b0_ksq")
        b0_self = sem("b0_self")
        b0_floor = sem("b0_floor")
        b0_log = sem("b0_log")
        b0_rk_ready = sem("b0_rk_ready")
        b0_kn = sem("b0_kn")
        b0_km = sem("b0_km")
        b0_scores = sem("b0_scores")
        b0_min = sem("b0_min")
        b0_e = sem("b0_e")
        b0_l = sem("b0_l")
        b0_soft = sem("b0_soft")
        b0_sigm = sem("b0_sigm")
        b0_masked = sem("b0_masked")
        b0_weight = sem("b0_weight")
        b0_out = sem("b0_out")
        b0_ctx_step = sem("b0_ctx_step")
        b0_done = sem("b0_done")
        b0_ct_turned = sem("b0_ct_turned")
        b0_ct_copied = sem("b0_ct_copied")
        b0_lin = sem("b0_lin")
        b0_x = sem("b0_x")
        PAIRS_QK = BR + 1
        ITEMS = 2 * PAIRS_QK + 4

        def b0_sync(sp):
            loads = [(b0_wq, "b0_Wq"), (b0_wk, "b0_Wk"), (b0_wv, "b0_Wv"), (b0_wo, "L0_attn_b_Wo"),
                     (b0_vec, "b0_vectors"), (b0_ones8, "c_ones8"), (b0_only, "c_only16"), (b0_tri, "c_tri"),
                     (b0_tab.rearrange("p k t -> p (k t)"), "c_rope")]
            for to, name in loads:
                sp.dma_start(to, d[name]).then_inc(b0_loaded, 16)
            for to, name in ((b0_bv, "b0_bv"), (b0_sink[:, 0:BR * BH], "b0_sinks"), (b0_null, "b0_nulls")):
                sp.dma_start(to, d[name].broadcast_to([P, to.shape[1]])).then_inc(b0_loaded, 16)
        B0_LOADS = 16 * 12

        def b0_tensor(pe, n0):
            ln_tensor(pe, n0, XO)
            pe.wait_ge(b0_loaded, B0_LOADS)
            pe.wait_ge(ln_scaled, (n0 + 1) * NCH)
            for c in range(NCH):
                for i in range(ITEMS):
                    n = ITEMS * c + i
                    if n >= 8:
                        pe.wait_ge(b0_freed, n - 7)
                    if i < 2 * PAIRS_QK:
                        w = b0_wq[:, i * C:(i + 1) * C] if i < 2 * BR else b0_wk[:, (i - 2 * BR) * C:(i - 2 * BR + 1) * C]
                        pe.matmul(PS[:, n % 8, :], w, chunk(XN, c), start=True, stop=True).then_inc(b0_proj, 1)
                    else:
                        t = 4 * c + i - 2 * PAIRS_QK
                        pe.matmul(PS[:, n % 8, :], XN[:, t * P:(t + 1) * P], b0_wv, start=True, stop=True)\
                          .then_inc(b0_proj, 1)
            pe.wait_ge(b0_freed, ITEMS * NCH)
            for c in range(NCH):
                pe.wait_ge(b0_ksq, c + 1)
                pe.matmul(PS[:, c, :], b0_ones8, chunk(b0_sq, c), start=True, stop=True).then_inc(b0_self, 1)
            wait_alone(pe, b0_kn, NCH)

            def scores(b, group):
                wait_alone(pe, b0_km, nth(b, NGROUPS, group))
                at = b * T + (group // NGROUPS) * T
                for v in range(IN_GROUP):
                    u = group * IN_GROUP + v
                    wait_alone(pe, b0_soft, nth(b, UNITS, u - 2) + 2)
                    for k, (kt, qt) in enumerate(((0, 0), (1, 1), (0, 1))):
                        last = pe.matmul(PS[:, (u % 2) * 3 + k, :], b0_KM[u % (2 * IN_GROUP)][:, kt * P:(kt + 1) * P],
                                         b0_Q[:, :, ds(at + qt * P, P)], start=True, stop=True)
                    last.then_inc(b0_scores, 1)

            def heads(b, group):
                wait_alone(pe, b0_done, nth(b, NGROUPS, group - 2) + 2)
                for v in range(IN_GROUP):
                    pe.wait_ge(b0_weight, nth(b, UNITS, group * IN_GROUP + v) + 2)
                    w = b0_w[:, group % 2, v, :]
                    for r in range(BR):
                        h = (group * IN_GROUP + v) * BR + r
                        block = lambda k: w[:, k * CH + r * P:k * CH + (r + 1) * P]
                        o = lambda qt: PS[:, 6 + group % 2, ((qt * IN_GROUP + v) * BR + r) * 9:
                                          ((qt * IN_GROUP + v) * BR + r) * 9 + 9]
                        value = lambda kt: b0_V[:, ds(b * 2 + kt, 1), h, :].rearrange("p o e -> p (o e)")
                        pe.matmul(o(0), block(0), value(0), start=True, stop=True)
                        pe.matmul(o(1), block(2), value(0), start=True, stop=False)
                        last = pe.matmul(o(1), block(1), value(1), start=False, stop=True)
                last.then_inc(b0_out, 1)

            def batch(b, final):
                for n in range(NGROUPS):
                    if not (final and n == NGROUPS - 1):
                        scores(b, n + 1)
                    heads(b, n)
            scores(0, 0)
            with pe.Fori(0, B - 1) as b:
                batch(b, False)
            batch(B - 1, True)
            pe.wait_ge(b0_done, NGROUPS * B + 2)
            for c in range(NCH):
                for j in range(4):
                    last = pe.transpose(PS[:, c, j * P:(j + 1) * P], CT[:, 4 * c + j, :], ident[:])
                last.then_inc(b0_ct_turned, 1)
            for c in range(NCH):
                pe.wait_ge(b0_ct_copied, c + 1)
                pe.matmul(PS[:, 4 + c, :], b0_wo, chunk(b0_ct, c), start=True, stop=True).then_inc(b0_lin, 1)

        def b0_scalar(act, n0):
            ln_scalar(act, n0)
            act.wait_ge(b0_loaded, B0_LOADS)
            act.activation(b0_sink[:, 0:BR * BH], b0_sink[:, 0:BR * BH], ACT.Tanh).then_inc(b0_tanh, 1)
            log_exp_tables(act)
            for c in range(NCH):
                act.wait_ge(b0_roped, PAIRS_QK * (c + 1))
                act.activation(chunk(b0_sq, c), chunk(b0_K, c), ACT.Square).then_inc(b0_ksq, 1)
            for c in range(NCH):
                act.wait_ge(b0_floor, c + 1)
                act.activation(chunk(b0_rk, c), chunk(b0_rk, c), ACT.Ln).then_inc(b0_log, 1)
                act.wait_ge(b0_log, c + 1)
                act.activation(chunk(b0_rk, c), chunk(b0_rk, c), ACT.Exp, scale=-0.5).then_inc(b0_rk_ready, 1)

            def soft(b, group):
                log_exp_tables(act)
                for v in range(IN_GROUP):
                    u = group * IN_GROUP + v
                    act.wait_ge(b0_min, nth(b, UNITS, u))
                    act.activation(b0_m[u % 2], b0_m[u % 2], ACT.Exp).then_inc(b0_e, 1)
                    act.wait_ge(b0_e, nth(b, UNITS, u))
                    act.activation(b0_m[u % 2], b0_m[u % 2], ACT.Ln, bias=1.0).then_inc(b0_l, 1)

            def sigmoid(b, group):
                for v in range(IN_GROUP):
                    u = group * IN_GROUP + v
                    act.wait_ge(b0_soft, nth(b, UNITS, u) + 2)
                    act.wait_ge(b0_weight, nth(b, UNITS, u - 2) + 2)
                    act.activation(b0_sg[u % 2], b0_w[:, group % 2, v, :], ACT.Sigmoid, scale=SIG)\
                       .then_inc(b0_sigm, 1)

            def batch(b, final):
                for n in range(NGROUPS):
                    if not (final and n == NGROUPS - 1):
                        soft(b, n + 1)
                    sigmoid(b, n)
            soft(0, 0)
            with act.Fori(0, B - 1) as b:
                batch(b, False)
            batch(B - 1, True)
            for c in range(NCH):
                act.wait_ge(b0_ct_turned, c + 1)
                act.activation(chunk(b0_ct, c), PS[:, c, :], ACT.Copy).then_inc(b0_ct_copied, 1)

        def b0_vector(dve, n0):
            ln_vector(dve, n0, XO, XN)
            dve.wait_ge(b0_tanh, 1)
            dve.tensor_scalar(b0_sink[:, 0:BR * BH], b0_sink[:, 0:BR * BH], 1e-6, None, ALU.add).then_inc(b0_sinks, 1)
            dve.wait_ge(b0_sinks, 1)
            dve.tensor_scalar(b0_sink[:, BR * BH:], b0_sink[:, 0:BR * BH], 1e-6, None, ALU.add).then_inc(b0_sinks, 1)
            null3 = b0_null.rearrange("p (h e) -> p h e", e=8)
            sink3 = b0_sink[:, 0:BR * BH].rearrange("p (h o) -> p h o", o=1)
            dve.tensor_tensor(null3, null3, sink3.broadcast_to([P, BR * BH, 8]), ALU.mult).then_inc(b0_sinks, 1)
            for c in range(NCH):
                for j in range(PAIRS_QK):
                    n = ITEMS * c + 2 * j
                    to = chunk(b0_Q[:, j, :], c) if j < BR else chunk(b0_K, c)
                    tmp = b0_tmp[:, 0:CH]
                    m = PAIRS_QK * c + j
                    for k, half in enumerate((to, tmp)):
                        dve.wait_ge(b0_proj, n + k + 1)
                        if k == 1 and m > 0:
                            dve.wait_ge(b0_roped, m)
                        h3 = lambda a: a.rearrange("p (b t) -> p b t", t=T)
                        dve.scalar_tensor_tensor(h3(half), h3(PS[:, (n + k) % 8, :]), b0_vec[:, 2 * j + k:2 * j + k + 1],
                                                 b0_tab[:, k:k + 1, :].broadcast_to([P, CH // T, T]),
                                                 ALU.add, ALU.mult).then_inc(b0_freed, 1)
                    dve.wait_ge(b0_freed, n + 2)
                    dve.tensor_tensor(to, to, tmp, ALU.add).then_inc(b0_roped, 1)
                for j in range(4):
                    n = ITEMS * c + 2 * PAIRS_QK + j
                    dve.wait_ge(b0_proj, n + 1)
                    if n == 2 * PAIRS_QK:
                        dve.wait_ge(b0_ones, 1)
                    dve.tensor_tensor(b0_V[:, 4 * c + j, :, 0:8], PS[:, n % 8, :].rearrange("p (h e) -> p h e", e=8),
                                      b0_bv.rearrange("p (h e) -> p h e", e=8), ALU.add).then_inc(b0_freed, 1)
            for c in range(NCH):
                dve.wait_ge(b0_self, c + 1)
                dve.tensor_scalar(chunk(b0_rk, c), PS[:, c, :], 1e-6, None, ALU.max).then_inc(b0_floor, 1)
            for c in range(NCH):
                dve.wait_ge(b0_rk_ready, c + 1)
                dve.scalar_tensor_tensor(chunk(b0_K, c), chunk(b0_K, c), float(8 ** -0.5), chunk(b0_rk, c),
                                         ALU.mult, ALU.mult).then_inc(b0_kn, 1)
            wait_alone(dve, b0_kn, NCH)

            def masked_keys(b, group):
                at = b * T + (group // NGROUPS) * T
                dve.wait_ge(b0_scores, nth(b, UNITS, (group - 1) * IN_GROUP - 1) + UNITS)
                for v in range(IN_GROUP):
                    u = group * IN_GROUP + v
                    last = dve.tensor_scalar(b0_KM[u % (2 * IN_GROUP)], b0_K[:, ds(at, T)],
                                             b0_only[:, u % UNITS:u % UNITS + 1], None, ALU.mult)
                last.then_inc(b0_km, 1)

            def clamp(b, u):
                S = PS[:, (u % 2) * 3:(u % 2) * 3 + 3, :].rearrange("p k j -> p (k j)")
                dve.wait_ge(b0_scores, nth(b, UNITS, u) + UNITS)
                dve.wait_ge(b0_soft, nth(b, UNITS, u - 2) + 2)
                dve.tensor_scalar(b0_m[u % 2], S, 40.0, None, ALU.min).then_inc(b0_min, 1)

            def larger(b, group, v):
                u = group * IN_GROUP + v
                S = PS[:, (u % 2) * 3:(u % 2) * 3 + 3, :].rearrange("p k j -> p (k j)")
                dve.wait_ge(b0_l, nth(b, UNITS, u))
                dve.wait_ge(b0_out, nth(b, NGROUPS, group - 2) + 2)
                dve.tensor_tensor(b0_w[:, group % 2, v, :], b0_m[u % 2], S, ALU.max).then_inc(b0_soft, 1)

            def soft(b, group):
                masked_keys(b, group)
                clamp(b, group * IN_GROUP)
                for v in range(IN_GROUP):
                    if v + 1 < IN_GROUP:
                        clamp(b, group * IN_GROUP + v + 1)
                    larger(b, group, v)

            def weigh(b, group):
                for v in range(IN_GROUP):
                    u = group * IN_GROUP + v
                    w = b0_w[:, group % 2, v, :]
                    dve.wait_ge(b0_masked, nth(b, UNITS, u))
                    dve.tensor_tensor(w, w, b0_sg[u % 2], ALU.mult).then_inc(b0_weight, 1)

            def context(b, group):
                n = nth(b, NGROUPS, group)
                step = nth(b, 5 * NGROUPS, 5 * group)
                dve.wait_ge(b0_out, n + 2)
                O = PS[:, 6 + group % 2, 0:2 * IN_GROUP * BR * 9].rearrange("p (q h e) -> p q h e", q=2, e=9)
                heads_of = slice(group * IN_GROUP * BR, (group + 1) * IN_GROUP * BR)
                HB = IN_GROUP * BR
                den = b0_den.rearrange("p (q h) -> p q h", q=2)
                sinks = b0_sink[:, BR * BH:][:, heads_of].rearrange("p (o h) -> p o h", o=1).broadcast_to([P, 2, HB])
                dve.tensor_tensor(den, O[:, :, :, 8:9].rearrange("p q h o -> p q (h o)"), sinks, ALU.add)\
                   .then_inc(b0_ctx_step, 1)
                nulls = b0_null[:, group * HB * 8:(group + 1) * HB * 8]
                X = b0_ctx.rearrange("p (q h e) -> p q h e", q=2, e=8)
                for q in range(2):
                    dve.tensor_tensor(X[:, q, :, :], O[:, q, :, 0:8], nulls.rearrange("p (h e) -> p h e", e=8), ALU.add)\
                       .then_inc(b0_ctx_step, 1)
                dve.wait_ge(b0_ctx_step, step)
                dve.reciprocal(b0_den, b0_den).then_inc(b0_ctx_step, 1)
                dve.wait_ge(b0_ctx_step, step + 3)
                X2 = b0_ctx.rearrange("p (h e) -> p h e", e=8)
                alpha = b0_den.rearrange("p (h o) -> p h o", o=1).broadcast_to([P, 2 * HB, 8])
                dve.tensor_tensor(X2, X2, alpha, ALU.mult).then_inc(b0_ctx_step, 1)
                dve.wait_ge(b0_ctx_step, step + 4)
                for q in range(2):
                    to = CT[:, ds(b * 2 + q, 1), group * 32:(group + 1) * 32].rearrange("p o f -> p (o f)")
                    fr = b0_ctx[:, q * HB * 8:(q + 1) * HB * 8].rearrange("p (h r e) -> p h e r", r=BR, e=8)
                    last = dve.tensor_reduce(to.rearrange("p (h e) -> p h e", e=8), fr, AX_X, ALU.add)
                last.then_inc(b0_done, 1)

            def batch(b, final):
                for n in range(NGROUPS):
                    if not (final and n == NGROUPS - 1):
                        soft(b, n + 1)
                    weigh(b, n)
                    context(b, n)
            soft(0, 0)
            with dve.Fori(0, B - 1) as b:
                batch(b, False)
            batch(B - 1, True)
            for c in range(NCH):
                dve.tensor_scalar(chunk(XO, c), chunk(XO, c), b0_vec[:, 10:11], None, ALU.add).then_inc(b0_x, 1)
            for c in range(NCH):
                dve.wait_ge(b0_lin, c + 1)
                dve.wait_ge(b0_x, c + 1)
                dve.scalar_tensor_tensor(chunk(XO, c), PS[:, 4 + c, :], 1.0 / BR, chunk(XO, c), ALU.mult, ALU.add)

        def b0_gpsimd(pool):
            pool.memset(b0_V, 1.0).then_inc(b0_ones, 1)
            wait_alone(pool, b0_loaded, B0_LOADS)

            def mask(b, group):
                for v in range(IN_GROUP):
                    u = group * IN_GROUP + v
                    wait_alone(pool, b0_sigm, nth(b, UNITS, u))
                    s3 = b0_sg[u % 2][:, 0:2 * CH].rearrange("p (r j) -> p r j", j=P)
                    tri = b0_tri.rearrange("p (o j) -> p o j", o=1).broadcast_to([P, 2 * BR, P])
                    pool.tensor_tensor(s3, s3, tri, ALU.mult).then_inc(b0_masked, 1)
            with pool.Fori(0, B) as b:
                for n in range(NGROUPS):
                    mask(b, n)

        block = ctx.enter_context(nc.Block())

        K, n0, run, plan, calls = 1, 0, 0, [], {"ffn": 0, "mix": 0}
        for part in parts:
            kind = part[:-1]
            plan.append((kind + part[-1] if kind in ("attn_a", "attn_b") else kind, K, n0, calls.get(kind, 0), run))
            run += part in ("mix0", "mix1", "attn_b1")
            if kind in calls:
                calls[kind] += 1
            K += 2 + 2 * DEPTH if kind == "ffn" else 1
            n0 += 1 + DEPTH if kind == "ffn" else 1

        @block.sync
        def _(sp):
            load_sync(sp)
            for part, K, n0, call, run in plan:
                sp.wait_ge(phase_end, 4 * K)
                if part == "attn_a0":
                    a0_sync(sp)
                if part == "ffn":
                    ffn_sync(sp, call, K)
                if part == "attn_b0":
                    b0_sync(sp)
                if part == "attn_a1":
                    a1_sync(sp)
                if part == "mix":
                    mix_sync(sp)
                if part == "attn_b1":
                    b1_sync(sp)
            store_sync(sp)

        @block.tensor
        def _(pe):
            load_tensor(pe)
            meet(pe, 1)
            for part, K, n0, call, run in plan:
                if part == "attn_a0":
                    a0_tensor(pe, n0)
                if part == "ffn":
                    ffn_tensor(pe, call, K, n0)
                    K += 1 + 2 * DEPTH
                if part == "attn_b0":
                    b0_tensor(pe, n0)
                if part == "attn_a1":
                    a1_tensor(pe, n0)
                if part == "mix":
                    mix_tensor(pe, run, call, n0)
                if part == "attn_b1":
                    b1_tensor(pe, run, n0)
                meet(pe, K + 1)
            store_tensor(pe)

        @block.scalar
        def _(act):
            act.sem_inc(qkv_copied, 2)
            act.sem_inc(turned_copied, 2)
            act.sem_inc(o_copied, 2)
            act.sem_inc(b0_scores, UNITS)
            act.sem_inc(b0_out, 2)
            act.sem_inc(scan_norm, 3)
            for semaphore, of_batch in ((hd_entered, 1), (hd_proj, 2), (hd_projected, 3), (hd_scores, PAIRS8),
                                        (hd_exp, PAIRS8), (hd_out, PAIRS8), (hd_copied, 1)):
                act.sem_inc(semaphore, of_batch)
            load_scalar(act)
            meet(act, 1)
            for part, K, n0, call, run in plan:
                if part == "attn_a0":
                    a0_scalar(act, n0)
                if part == "ffn":
                    ffn_scalar(act, call, K, n0)
                    K += 1 + 2 * DEPTH
                if part == "attn_b0":
                    b0_scalar(act, n0)
                if part == "attn_a1":
                    a1_scalar(act, n0)
                if part == "mix":
                    mix_scalar(act, run, call, n0)
                if part == "attn_b1":
                    b1_scalar(act, run, n0)
                meet(act, K + 1)
            store_scalar(act)

        @block.vector
        def _(dve):
            dve.sem_inc(scores_read, 2)
            dve.sem_inc(b0_soft, 2)
            dve.sem_inc(b0_weight, 2)
            dve.sem_inc(b0_done, 2)
            dve.sem_inc(t1_ready, 1)
            dve.sem_inc(t2_ready, 1)
            for semaphore, of_batch in ((hd_masked, HEADS_IN_GROUP), (hd_max, PAIRS8), (hd_bias, PAIRS8),
                                        (hd_recip, PAIRS8), (hd_v_ready, PAIRS8)):
                dve.sem_inc(semaphore, of_batch)
            dve.sem_inc(stream_added, 1)
            meet(dve, 1)
            for part, K, n0, call, run in plan:
                if part == "attn_a0":
                    a0_vector(dve, n0)
                if part == "ffn":
                    ffn_vector(dve, call, K, n0)
                    K += 1 + 2 * DEPTH
                if part == "attn_b0":
                    b0_vector(dve, n0)
                if part == "attn_a1":
                    a1_vector(dve, n0)
                if part == "mix":
                    mix_vector(dve, run, call, n0)
                if part == "attn_b1":
                    b1_vector(dve, run, n0)
                meet(dve, K + 1)

        @block.gpsimd
        def _(pool):
            meet(pool, 1)
            for part, K, n0, call, run in plan:
                if part == "ffn":
                    ffn_gpsimd(pool, call, K, n0)
                    K += 1 + 2 * DEPTH
                if part == "attn_b0":
                    b0_gpsimd(pool)
                meet(pool, K + 1)


def laid_out(inputs):
    a = {k: np.asarray(v) for k, v in inputs.items()}
    d = {k: a[k] for k in ("L0_attn_a_x", "L0_ffn_Wqkv", "L0_ffn_Wo", "L0_ffn_W1", "L0_ffn_W2")}
    b1 = a["L0_ffn_b1"]
    vectors = np.zeros((DEPTH, P, 9), np.float32)
    vectors[:, :, 0] = a["L0_ffn_ln_g"]
    vectors[:, :, 1] = a["L0_ffn_ln_b"]
    vectors[:, :, 2] = a["L0_ffn_b2"]
    for m, rows in enumerate(DIM):
        vectors[:, :rows, 3 + m] = b1[:, DI + P * m:DI + P * m + rows]
        vectors[:, :rows, 6 + m] = b1[:, P * m:P * m + rows]
    d["ffn_vectors"] = vectors
    q, k = a["L0_ffn_q_scale"], a["L0_ffn_k_scale"]
    d["ffn_scales"] = np.concatenate([q, k, np.roll(q, FD // 2, 1), np.roll(k, FD // 2, 1)], 1)
    for name in "rkvgo":
        d[f"a0_W_{name}"] = a[f"L0_attn_a_W_{name}"].T
    v = np.zeros((P, 16), np.float32)
    for k, name in enumerate("rkvg"):
        v[:, k] = a[f"L0_attn_a_time_mix_{name}"].reshape(C)
        v[:, 4 + k] = a[f"L0_attn_a_b_{name}"]
    v[:, 8], v[:, 9], v[:, 10] = a["L0_attn_a_b_o"], a["L0_attn_a_gn_weight"], a["L0_attn_a_gn_bias"]
    d["a0_vectors"] = v
    d["a0_heads"] = np.stack([np.tile(a[f"L0_attn_a_{n}"].reshape(-1), B) for n in ("decay", "eta")], 1)
    for name in ("za", "z", "ya", "y"):
        d[f"a1_W_{name}"] = a[f"L1_attn_a_W{name}"].T
    v = np.zeros((P, 8), np.float32)
    for k, name in enumerate(("bza", "bz", "bya", "by", "norm_w", "lc_re", "lc_im")):
        v[:, k] = a[f"L1_attn_a_{name}"]
    d["a1_vectors"] = v
    for name in ("Wq", "Wk", "Wv", "Wo", "Wff"):
        d[f"L1_ffn_{name}"] = a[f"L1_ffn_{name}"]
    for name in ("wq", "wk", "wv", "wo"):
        d[f"b1_{name}"] = a[f"L1_attn_b_{name}"].T
    order = np.arange(C).reshape(16, 4, 2).transpose(0, 2, 1).reshape(-1)
    swapped = order.reshape(16, 2, 4)[:, ::-1].reshape(-1)
    Wq, bq = a["L0_attn_b_Wq"].reshape(C, 4, C), a["L0_attn_b_bq"].reshape(4, C)
    d["b0_Wq"] = np.stack([Wq[:, :, order], Wq[:, :, swapped]], 2).reshape(C, 8 * C)
    Wk, bk = a["L0_attn_b_Wk"], a["L0_attn_b_bk"]
    d["b0_Wk"] = np.concatenate([Wk[:, order], Wk[:, swapped]], 1)
    v = np.zeros((P, 16), np.float32)
    v[:, 0:8] = np.stack([bq[:, order], bq[:, swapped]], 1).reshape(8, C).T
    v[:, 8], v[:, 9], v[:, 10] = bk[order], bk[swapped], a["L0_attn_b_bo"]
    d["b0_vectors"] = v
    by_head = lambda m: m.reshape(-1, 4, 16, 8).transpose(0, 2, 1, 3).reshape(-1, 4 * C)
    d["b0_Wv"], d["b0_bv"], d["b0_nulls"] = by_head(a["L0_attn_b_Wv"]), by_head(a["L0_attn_b_bv"]), by_head(a["L0_attn_b_v_nulls"])
    d["b0_sinks"] = a["L0_attn_b_sink_scalars"].reshape(4, 16).T.reshape(1, 64)
    d["L0_attn_b_Wo"] = a["L0_attn_b_Wo"]
    d.update(shape_constants())
    return {k: np.ascontiguousarray(v) for k, v in d.items()}


def kernel(**inputs):
    from concourse import bacc
    from concourse.bass_utils import run_bass_kernel_spmd

    nc = bacc.Bacc("TRN2", target_bir_lowering=False, num_devices=1)
    arrays = {f"in_{k}": v for k, v in laid_out(inputs).items()}
    d = {k[3:]: nc.dram_tensor(k, v.shape, mybir.dt.from_np(v.dtype), kind="ExternalInput").ap()
         for k, v in arrays.items()}
    out = nc.dram_tensor("out_x", (B, T, C), F32, kind="ExternalOutput").ap()
    program(nc, d, out)
    return run_bass_kernel_spmd(nc, [arrays], core_ids=[0]).results[0]["out_x"]
```

```python
from contextlib import ExitStack

import numpy as np

import concourse.bass as bass
from concourse import mybir

F32 = mybir.dt.float32
ALU = mybir.AluOpType
ACT = mybir.ActivationFunctionType
AX_X = mybir.AxisListType.X
ds = bass.ds

P = 128
B, T, C = 8, 256, 128
N = B * T
CH = 512
NCH = N // CH

DEPTH, FH, FD = 6, 16, 64
WIN = 32
INNER = FH * FD
PAIRS = FH // 2
DI = int(C * 4 * 2 / 3)
DIM = [min(P, DI - P * m) for m in range(-(-DI // P))]
UNITS_IN_BODY = 2
TILES = 2 * UNITS_IN_BODY
BODIES = B // UNITS_IN_BODY
NEG = -1.0e30

INPUTS = {}


def nth(turn, per_turn, j):
    return turn * per_turn + j + 1


def rotary_constants():
    half = np.arange(0, FD, 2, dtype=np.float32)
    inv_freq = (np.float32(1.0) / np.float32(10000.0) ** (half / np.float32(FD))).astype(np.float32)
    t = np.arange(T, dtype=np.float32)
    freqs = (t[:, None] * inv_freq[None, :]).astype(np.float32).astype(np.float64)
    freqs = np.concatenate([freqs, freqs], -1)
    base = ((half + np.float32(0.4 * FD)) / np.float32(1.4 * FD)).astype(np.float64)
    power = (t.astype(np.float64) - T // 2) / (WIN // 2)
    scale = base[None, :] ** power[:, None]
    scale = np.concatenate([scale, scale], -1)
    sign = np.where(np.arange(FD) < FD // 2, -1.0, 1.0)
    qk_scale = 8.0
    kinds = [qk_scale * np.cos(freqs) * scale, np.cos(freqs) / scale,
             qk_scale * sign * np.sin(freqs) * scale, sign * np.sin(freqs) / scale]
    a = np.stack(kinds).reshape(4, 2, P, FD).transpose(2, 0, 1, 3)
    return np.ascontiguousarray(a, dtype=np.float32).reshape(P, 4 * 2 * FD)


def window_masks():
    i = np.arange(WIN)[:, None]
    previous = np.where(np.arange(WIN)[None, :] >= i, 0.0, NEG)
    own = np.where(np.arange(WIN)[None, :] <= i, 0.0, NEG)
    m = np.tile(np.concatenate([previous, own], 1), (4, 1))
    first = m.copy()
    first[:WIN, :WIN] = NEG
    return np.ascontiguousarray(np.concatenate([first, m], 1), dtype=np.float32)


def phazor_tables():
    w = np.power(np.float32(0.001), np.linspace(0.0, 1.0, C, dtype=np.float32)).astype(np.float64)[:, None]
    t = np.arange(T, dtype=np.float64)[None, :]
    a = 1e-5
    kinds = [np.exp(-a * t) * np.cos(w * t), np.exp(-a * t) * np.sin(w * t),
             np.exp(a * t) * np.cos(w * t), np.exp(a * t) * np.sin(w * t),
             np.exp(a * (t + 1)) * np.cos(w * (t + 1)), -np.exp(a * (t + 1)) * np.sin(w * (t + 1))]
    return np.stack(kinds, 1).reshape(P, 6 * T).astype(np.float32)


def rope_tables():
    inv_freq = np.float32(1.0) / np.float32(10000.0) ** (np.arange(0, 8, 2, dtype=np.float32) / np.float32(8))
    freqs = (np.arange(T, dtype=np.float32)[:, None] * inv_freq[None, :].astype(np.float32)).astype(np.float64).T
    cos = np.tile(np.cos(freqs), (P // 4, 1))
    sin = np.tile(np.concatenate([-np.sin(freqs), np.sin(freqs)]), (P // 8, 1))
    return np.concatenate([cos, sin], 1).astype(np.float32)


def shape_constants():
    ones = np.ones((P, P), np.float32)
    return {
        "c_identity": np.eye(P, dtype=np.float32),
        "c_mean": ones / np.float32(C),
        "c_rotary": rotary_constants(),
        "c_masks": window_masks(),
        "c_phazor": phazor_tables(),
        "c_rope": rope_tables(),
        "c_only16": (np.arange(P)[:, None] // 8 == np.arange(16)[None, :]).astype(np.float32),
        "c_ones8": np.kron(np.eye(16), np.ones((8, 8))).astype(np.float32),
        "c_tri": np.triu(np.ones((P, P), np.float32)),
        "c_causal": np.tile(np.triu(np.full((P, P), NEG, np.float32), 1), (1, 2)),
        "c_only": ((np.arange(P)[:, None] % 32) // 8 == np.arange(4)[None, :]).astype(np.float32),
        "c_eps": np.tile(np.array([[1e-5, 12 * np.log(2.0), 1e-6, 1e-12]], np.float32), (P, 1)),
    }


ALL = ("attn_a0", "ffn0", "attn_b0", "ffn1", "attn_a1", "mix0", "attn_b1", "mix1")


def program(nc, d, out, parts=ALL):
    ctx = ExitStack()
    with ctx:
        def sem(name):
            return ctx.enter_context(nc.semaphore(name))

        def sb(name, cols):
            return ctx.enter_context(nc.sbuf_tensor(name, [P, cols], F32))

        arena_cols = 44400
        arena = sb("arena", arena_cols)

        class Space:
            def __init__(self, start):
                self.at = start

            def take(self, cols):
                got = arena[:, self.at:self.at + cols]
                self.at += cols
                assert self.at <= arena_cols, self.at
                return got

        XO = sb("XO", N)
        XN = sb("XN", N)
        ident = sb("ident", P)
        mean_w = sb("mean_w", P)
        eps = sb("eps", 4)
        PS = ctx.enter_context(nc.psum_tensor("PS", [P, 8, CH], F32))
        lnc = sb("lnc", N)
        lns = sb("lns", N)

        ffn = Space(0)
        XT = ffn.take(N)
        Wqkv = ffn.take(3 * INNER)
        Wo = ffn.take(PAIRS * C).rearrange("p (m n) -> p m n", m=PAIRS)
        W1 = ffn.take(2 * DI)
        W2 = ffn.take(len(DIM) * C).rearrange("p (m n) -> p m n", m=len(DIM))
        fvec = ffn.take(16)
        qks = ffn.take(4 * FD).rearrange("p (k e) -> p k e", k=4)
        rotary = ffn.take(8 * FD).rearrange("p (k t e) -> p k t e", k=4, t=2)
        table = ffn.take(8 * FD).rearrange("p (k t e) -> p k t e", k=4, t=2)
        masks = ffn.take(2 * 2 * WIN).rearrange("p (t j) -> p t j", t=2)
        attn = Space(ffn.at)
        xs = [attn.take(T) for _ in range(UNITS_IN_BODY)]
        raw_at = attn.at
        raws = [attn.take(2 * INNER) for _ in range(2)]
        sq = attn.take(2 * INNER)
        t1 = attn.take(2 * INNER)
        t2 = attn.take(2 * INNER)
        nrm = attn.take(4 * 2 * FH).rearrange("p (a h) -> p a h", a=4)
        qT = attn.take(PAIRS * P).rearrange("p (m t) -> p m t", m=PAIRS)
        KT = [attn.take(PAIRS * (WIN + T)).rearrange("p (m t) -> p m t", m=PAIRS) for _ in range(UNITS_IN_BODY)]
        V = [attn.take(INNER) for _ in range(TILES)]
        sm = attn.take(INNER)
        E = attn.take(INNER)
        sst = attn.take(4 * FH).rearrange("p (a h) -> p a h", a=4)
        EP = attn.take(FH * P).rearrange("p (h j) -> p h j", h=FH)
        EPv = attn.take(FH * P).rearrange("p (h j) -> p h j", h=FH)
        PT = attn.take(FH * P).rearrange("p (h i) -> p h i", h=FH)
        PTv = attn.take(FH * WIN).rearrange("p (h i) -> p h i", h=FH)
        AT = [attn.take(PAIRS * T).rearrange("p (m t) -> p m t", m=PAIRS) for _ in range(UNITS_IN_BODY)]
        ysb = attn.take(T)
        mlp = Space(raw_at)
        gl = mlp.take(2 * len(DIM) * CH).rearrange("p (r m n) -> p r m n", r=2, m=len(DIM))
        hh = mlp.take(2 * len(DIM) * CH).rearrange("p (r m n) -> p r m n", r=2, m=len(DIM))
        assert mlp.at - raw_at <= 10 * INNER

        phase_end = sem("phase_end")
        const_loaded = sem("const_loaded")
        x_loaded = sem("x_loaded")
        x_turned = sem("x_turned")
        x_copied = sem("x_copied")
        out_turned = sem("out_turned")
        out_copied = sem("out_copied")
        out_stored = sem("out_stored")
        ln_mean = sem("ln_mean")
        ln_centred = sem("ln_centred")
        ln_squared = sem("ln_squared")
        ln_var = sem("ln_var")
        ln_log = sem("ln_log")
        ln_rstd = sem("ln_rstd")
        ln_scaled = sem("ln_scaled")
        ln_out = sem("ln_out")
        attn_w_loaded = sem("attn_w_loaded")
        mlp_w_loaded = sem("mlp_w_loaded")
        tables_ready = sem("tables_ready")
        xs_ready = sem("xs_ready")
        qkv_ready = sem("qkv_ready")
        qkv_copied = sem("qkv_copied")
        norm2_ready = sem("norm2_ready")
        norm2_own = sem("norm2_own")
        rnorm_log = sem("rnorm_log")
        rnorm_ready = sem("rnorm_ready")
        u_ready = sem("u_ready")
        t1_ready = sem("t1_ready")
        t2_ready = sem("t2_ready")
        turned = sem("turned")
        turned_copied = sem("turned_copied")
        scores_ready = sem("scores_ready")
        scores_read = sem("scores_read")
        max_ready = sem("max_ready")
        shifted_ready = sem("shifted_ready")
        exp_ready = sem("exp_ready")
        sum_ready = sem("sum_ready")
        recip_ready = sem("recip_ready")
        padded_ready = sem("padded_ready")
        o_ready = sem("o_ready")
        o_copied = sem("o_copied")
        stream_added = sem("stream_added")
        up_ready = sem("up_ready")
        gelu_ready = sem("gelu_ready")
        h_ready = sem("h_ready")
        down_ready = sem("down_ready")
        down_added = sem("down_added")
        low_shifted = sem("low_shifted")
        high_shifted = sem("high_shifted")
        edge_zeroed = sem("edge_zeroed")
        ffn_const_loaded = sem("ffn_const_loaded")

        consts = [(ident, "c_identity"), (mean_w, "c_mean"), (eps, "c_eps")]

        def wait_alone(eng, semaphore, count):
            if not isinstance(count, int):
                count = eng.compute_val(count)
            eng.wait_ge(phase_end, 0)
            eng.wait_ge(semaphore, count)

        def meet(eng, n):
            eng.drain().then_inc(phase_end, 1)
            wait_alone(eng, phase_end, n * 4)

        def chunk(a, c):
            return a[:, c * CH:(c + 1) * CH]

        x_dram = d["L0_attn_a_x"].rearrange("b (u p) c -> p (b u) c", p=P)
        out_dram = out.rearrange("b (u p) c -> p (b u) c", p=P)
        xtok = arena[:, 0:N].rearrange("p (t c) -> p t c", c=C)
        otok = arena[:, 0:N].rearrange("p (t c) -> p t c", c=C)

        def load_sync(sp):
            for tile, name in consts:
                sp.dma_start(tile[:], d[name]).then_inc(const_loaded, 16)
            sp.dma_start(xtok, x_dram).then_inc(x_loaded, 16)

        def load_tensor(pe):
            pe.wait_ge(const_loaded, 16 * len(consts))
            pe.wait_ge(x_loaded, 16)
            for c in range(NCH):
                for j in range(4):
                    last = pe.transpose(PS[:, c, j * P:(j + 1) * P], xtok[:, 4 * c + j, :], ident[:])
                last.then_inc(x_turned, 1)

        def load_scalar(act):
            for c in range(NCH):
                act.wait_ge(x_turned, c + 1)
                act.activation(chunk(XO, c), PS[:, c, :], ACT.Copy).then_inc(x_copied, 1)

        def store_tensor(pe):
            for c in range(NCH):
                for j in range(4):
                    last = pe.transpose(PS[:, c, j * P:(j + 1) * P], XO[:, (4 * c + j) * P:(4 * c + j + 1) * P], ident[:])
                last.then_inc(out_turned, 1)

        def store_scalar(act):
            for c in range(NCH):
                act.wait_ge(out_turned, c + 1)
                act.activation(otok[:, 4 * c:4 * c + 4, :], PS[:, c, :], ACT.Copy).then_inc(out_copied, 1)

        def store_sync(sp):
            for c in range(NCH):
                sp.wait_ge(out_copied, c + 1)
                sp.dma_start(out_dram[:, 4 * c:4 * c + 4, :], otok[:, 4 * c:4 * c + 4, :]).then_inc(out_stored, 16)
            sp.wait_ge(out_stored, 16 * NCH)

        def ln_tensor(pe, n, src):
            def var(c):
                pe.wait_ge(ln_squared, nth(n, NCH, c))
                pe.matmul(PS[:, 4 + c, :], mean_w[:], chunk(lns, c), start=True, stop=True).then_inc(ln_var, 1)
            for c in range(NCH):
                pe.matmul(PS[:, c, :], mean_w[:], chunk(src, c), start=True, stop=True).then_inc(ln_mean, 1)
            for c in range(NCH):
                var(c)

        def log_exp_tables(act):
            act.preload_act_table_set("natural_log_exp_and_others")

        def ln_scalar(act, n):
            log_exp_tables(act)
            for c in range(NCH):
                act.wait_ge(ln_centred, nth(n, NCH, c))
                act.activation(chunk(lns, c), chunk(lnc, c), ACT.Square).then_inc(ln_squared, 1)
            for c in range(NCH):
                act.wait_ge(ln_var, nth(n, NCH, c))
                act.activation(chunk(lns, c), PS[:, 4 + c, :], ACT.Ln, bias=eps[:, 0:1]).then_inc(ln_log, 1)
                act.wait_ge(ln_log, nth(n, NCH, c))
                act.activation(chunk(lns, c), chunk(lns, c), ACT.Exp, scale=-0.5).then_inc(ln_rstd, 1)

        def ln_vector(dve, n, src, dst, gain=None):
            def centre(c):
                dve.wait_ge(ln_mean, nth(n, NCH, c))
                dve.tensor_tensor(chunk(lnc, c), chunk(src, c), PS[:, c, :], ALU.subtract).then_inc(ln_centred, 1)

            def scale(c):
                dve.wait_ge(ln_rstd, nth(n, NCH, c))
                dve.tensor_tensor(chunk(dst, c), chunk(lnc, c), chunk(lns, c), ALU.mult).then_inc(ln_scaled, 1)
                dve.wait_ge(ln_scaled, nth(n, NCH, c))
                if gain is not None:
                    dve.tensor_scalar(chunk(dst, c), chunk(dst, c), gain[0], gain[1], ALU.mult, ALU.add)\
                       .then_inc(ln_out, 1)
            for c in range(NCH):
                centre(c)
            for c in range(NCH):
                scale(c)

        QKV, TURN, SCORE, HEAD = 0, 2, 4, 6
        QKV_PER, TURN_PER, SCORE_PER, HEAD_PER = 6 * TILES, 17 * UNITS_IN_BODY, 2 * TILES, 5 * UNITS_IN_BODY

        def turned_from(tt):
            return 4 + 17 * (tt // 2) + 8 * (tt % 2)

        def place_qk(tt, j):
            return turned_from(tt - 1) + j if tt > 0 else j

        def place_probs(tt, j, final):
            return turned_from(tt) + (0 if final and tt == TILES - 1 else 4) + j

        def head_index(tt, j):
            uu, par = divmod(tt, 2)
            return uu * 5 + par * 2 + j

        def fa_tensor(pe, run):
            def qkv(g, tt, half=None):
                uu, par = divmod(tt, 2)
                if par == 0 and half != 1:
                    pe.wait_ge(xs_ready, nth(g, UNITS_IN_BODY, uu))
                for c in range(6) if half is None else range(3 * half, 3 * half + 3):
                    n = 6 * tt + c
                    pe.wait_ge(qkv_copied, nth(g, QKV_PER, n))
                    pe.matmul(PS[:, QKV + n % 2, :], xs[uu % 2][:, par * P:(par + 1) * P], chunk(Wqkv, c),
                              start=True, stop=True).then_inc(qkv_ready, 1)

            def turn_qk(g, tt):
                for c in range(4):
                    n = place_qk(tt, c)
                    pe.wait_ge(turned_copied, nth(g, TURN_PER, n))
                    if c % 2 == 0:
                        pe.wait_ge(t2_ready, nth(g, 2 * TILES, 2 * tt + c // 2) + 3)
                        pe.wait_ge(t1_ready, nth(g, 2 * TILES, 2 * tt + c // 2) + 3)
                    for j in range(4):
                        o = PS[:, TURN + n % 2, j * P:(j + 1) * P]
                        cols = slice((4 * c + j) * P, (4 * c + j + 1) * P)
                        pe.matmul(o, t1[:, cols], ident[:], start=True, stop=False, is_transpose=True)
                        last = pe.matmul(o, t2[:, cols], ident[:], start=False, stop=True, is_transpose=True)
                    last.then_inc(turned, 1)

            def scores(g, tt, s):
                uu, par = divmod(tt, 2)
                if s == 0:
                    wait_alone(pe, turned_copied, nth(g, TURN_PER, place_qk(tt, 3)) + 2)
                wait_alone(pe, scores_read, nth(g, SCORE_PER, 2 * tt + s))
                for m in range(PAIRS):
                    for w in range(4):
                        at = par * P + w * WIN
                        last = pe.matmul(PS[w * WIN:(w + 1) * WIN, SCORE + s, m * FD:(m + 1) * FD],
                                         qT[s * FD:(s + 1) * FD, m, w * WIN:(w + 1) * WIN],
                                         KT[uu % 2][s * FD:(s + 1) * FD, m, at:at + 2 * WIN],
                                         start=True, stop=True)
                last.then_inc(scores_ready, 1)

            def turn_probs(g, tt, final):
                pe.wait_ge(padded_ready, nth(g, TILES, tt))
                for c in range(4):
                    n = place_probs(tt, c, final)
                    pe.wait_ge(turned_copied, nth(g, TURN_PER, n))
                    for j in range(4):
                        last = pe.transpose(PS[:, TURN + n % 2, j * P:(j + 1) * P], EP[:, 4 * c + j, :], ident[:])
                    last.then_inc(turned, 1)
                if tt % 2 == 1:
                    n = place_probs(tt, 4, final)
                    wait_alone(pe, turned_copied, nth(g, TURN_PER, n))
                    for h in range(FH):
                        last = pe.transpose(PS[:, TURN + n % 2, h * WIN:(h + 1) * WIN], EPv[0:WIN, h, :],
                                            ident[0:WIN, 0:WIN])
                    last.then_inc(turned, 1)

            def heads(g, tt, final):
                par = tt % 2
                pe.wait_ge(turned_copied, nth(g, TURN_PER, place_probs(tt, 3 + par, final)) + 2)
                for j in range(2):
                    n = head_index(tt, j)
                    pe.wait_ge(o_copied, nth(g, HEAD_PER, n))
                    for m in range(4):
                        for s in range(2):
                            slot = s * PAIRS + 4 * j + m
                            h = 2 * (4 * j + m) + s
                            rows = slice(s * FD, (s + 1) * FD)
                            last = pe.matmul(PS[rows, HEAD + n % 2, m * P:(m + 1) * P],
                                             V[tt][:, h * FD:(h + 1) * FD], PT[:, slot, :],
                                             start=True, stop=True)
                            if par == 1:
                                last = pe.matmul(PS[rows, HEAD + n % 2, m * P:m * P + WIN],
                                                 V[tt - 1][:, h * FD:(h + 1) * FD], PTv[:, slot, :],
                                                 start=False, stop=True, skip_group_check=True)
                    last.then_inc(o_ready, 1)

            def project(g, uu):
                n = 5 * uu + 4
                pe.wait_ge(o_copied, nth(g, HEAD_PER, n))
                for m in range(PAIRS):
                    if m == PAIRS // 2:
                        pe.wait_ge(o_copied, nth(g, HEAD_PER, n - 1) + 2)
                    last = pe.matmul(PS[:, HEAD + n % 2, 0:T], Wo[:, m, :], AT[uu][:, m, :],
                                     start=(m == 0), stop=(m == PAIRS - 1))
                last.then_inc(o_ready, 1)

            def body(g, final):
                for tt in range(TILES):
                    ahead = not (final and tt + 1 >= TILES)
                    further = not (final and tt + 2 >= TILES)
                    if further:
                        qkv(g, tt + 2, 0)
                    if ahead:
                        turn_qk(g, tt + 1)
                    if further:
                        qkv(g, tt + 2, 1)
                    if ahead:
                        scores(g, tt + 1, 0)
                    if ahead:
                        scores(g, tt + 1, 1)
                    turn_probs(g, tt, final)
                    heads(g, tt, final)
                    if tt % 2 == 1:
                        project(g, tt // 2)
            wait_alone(pe, attn_w_loaded, (run + 1) * ATTN_LOADS)
            qkv(run * BODIES, 0)
            qkv(run * BODIES, 1)
            turn_qk(run * BODIES, 0)
            scores(run * BODIES, 0, 0)
            scores(run * BODIES, 0, 1)
            with pe.Fori(0, BODIES - 1) as it:
                body(run * BODIES + it, False)
            body(run * BODIES + BODIES - 1, True)

        def fa_scalar(act, run):
            def enter(unit, uu):
                act.activation(xs[uu][0:64, :], XT[0:64, ds(unit * T, T)], ACT.Copy)
                act.activation(xs[uu][64:128, 1:T], XT[64:128, ds(unit * T, T - 1)], ACT.Copy).then_inc(xs_ready, 1)

            def copy_qkv(g, tt, half=None):
                act.wait_ge(norm2_own, g * TILES + tt + 1)
                act.wait_ge(t1_ready, g * 2 * TILES + 2 * tt + 1)
                act.wait_ge(t2_ready, g * 2 * TILES + 2 * tt + 1)
                for c in range(6) if half is None else range(3 * half, 3 * half + 3):
                    n = 6 * tt + c
                    act.wait_ge(qkv_ready, nth(g, QKV_PER, n))
                    bank = PS[:, QKV + n % 2, :]
                    if c < 4:
                        act.activation(chunk(raws[tt % 2], c), bank, ACT.Copy)
                        act.activation(chunk(sq, c), bank, ACT.Square).then_inc(qkv_copied, 1)
                    else:
                        act.activation(V[tt % TILES][:, (c - 4) * CH:(c - 3) * CH], bank, ACT.Copy)\
                           .then_inc(qkv_copied, 1)

            def rnorm(g, tt):
                act.wait_ge(norm2_ready, nth(g, TILES, tt))
                act.activation(nrm[:, 1, :], nrm[:, 0, :], ACT.Ln, scale=float(2 ** 24)).then_inc(rnorm_log, 1)
                act.wait_ge(rnorm_log, nth(g, TILES, tt))
                act.activation(nrm[:, 2, :], nrm[:, 1, :], ACT.Exp, bias=eps[:, 1:2], scale=-0.5)\
                   .then_inc(rnorm_ready, 1)

            def copy_turned(g, tt):
                uu, par = divmod(tt, 2)
                for c in range(4):
                    n = place_qk(tt, c)
                    act.wait_ge(turned, nth(g, TURN_PER, n))
                    m = slice(4 * (c % 2), 4 * (c % 2) + 4)
                    to = qT[:, m, :] if c < 2 else KT[uu % 2][:, m, WIN + par * P:WIN + (par + 1) * P]
                    act.activation(to, PS[:, TURN + n % 2, :].rearrange("p (m t) -> p m t", m=4), ACT.Copy)\
                       .then_inc(turned_copied, 1)

            def exps(g, tt):
                act.wait_ge(shifted_ready, nth(g, TILES, tt))
                act.activation(E, sm, ACT.Exp).then_inc(exp_ready, 1)

            def copy_probs(g, tt, final):
                for c in range(4):
                    n = place_probs(tt, c, final)
                    act.wait_ge(turned, nth(g, TURN_PER, n))
                    act.activation(PT[:, 4 * c:4 * c + 4, :],
                                   PS[:, TURN + n % 2, :].rearrange("p (m t) -> p m t", m=4), ACT.Copy)\
                       .then_inc(turned_copied, 1)
                if tt % 2 == 1:
                    n = place_probs(tt, 4, final)
                    act.wait_ge(turned, nth(g, TURN_PER, n))
                    act.activation(PTv, PS[:, TURN + n % 2, :].rearrange("p (m t) -> p m t", m=FH), ACT.Copy)\
                       .then_inc(turned_copied, 1)

            def copy_heads(g, tt, j):
                uu, par = divmod(tt, 2)
                n = head_index(tt, j)
                act.wait_ge(o_ready, nth(g, HEAD_PER, n))
                act.activation(AT[uu][:, 4 * j:4 * j + 4, par * P:(par + 1) * P],
                               PS[:, HEAD + n % 2, :].rearrange("p (m t) -> p m t", m=4), ACT.Copy)\
                   .then_inc(o_copied, 1)

            def copy_projected(g, uu):
                n = 5 * uu + 4
                act.wait_ge(o_ready, nth(g, HEAD_PER, n))
                act.wait_ge(stream_added, nth(g, UNITS_IN_BODY, uu))
                act.activation(ysb, PS[:, HEAD + n % 2, 0:T], ACT.Copy).then_inc(o_copied, 1)

            def body(g, it, final):
                for tt in range(TILES):
                    further = not (final and tt + 2 >= TILES)
                    if further:
                        copy_qkv(g, tt + 2, 0)
                    if not (final and tt + 1 >= TILES):
                        copy_turned(g, tt + 1)
                    if further:
                        copy_qkv(g, tt + 2, 1)
                        rnorm(g, tt + 2)
                    if tt % 2 == 1 and not (final and tt + 3 >= TILES):
                        enter(it * UNITS_IN_BODY + (tt + 3) // 2, (tt + 3) // 2 % 2)
                    copy_probs(g, tt, final)
                    copy_heads(g, tt, 0)
                    if not (final and tt + 1 >= TILES):
                        exps(g, tt + 1)
                    copy_heads(g, tt, 1)
                    if tt % 2 == 1:
                        copy_projected(g, tt // 2)
            first = run * BODIES
            enter(0, 0)
            enter(1, 1)
            copy_qkv(first, 0)
            rnorm(first, 0)
            copy_qkv(first, 1)
            copy_turned(first, 0)
            rnorm(first, 1)
            exps(first, 0)
            with act.Fori(0, BODIES - 1) as it:
                body(first + it, it, False)
            body(first + BODIES - 1, BODIES - 1, True)

        def fa_vector(dve, run):
            h3 = lambda a: a.rearrange("p (h e) -> p h e", e=FD)

            def softmax_shift(g, tt):
                mask = masks[:, tt % 2:tt % 2 + 1, :].broadcast_to([P, PAIRS, 2 * WIN])
                for s in range(2):
                    dve.wait_ge(scores_ready, nth(g, SCORE_PER, 2 * tt + s))
                    last = dve.tensor_tensor(h3(chunk(sm, s)), h3(PS[:, SCORE + s, :]), mask, ALU.add)
                    last.then_inc(scores_read, 1)
                dve.wait_ge(scores_read, nth(g, SCORE_PER, 2 * tt + 1) + 2)
                dve.tensor_reduce(sst[:, 0, :], h3(sm), AX_X, ALU.max).then_inc(max_ready, 1)
                dve.wait_ge(max_ready, nth(g, TILES, tt))
                mx = sst[:, 0, :].rearrange("p (h o) -> p h o", o=1).broadcast_to([P, FH, FD])
                dve.tensor_tensor(h3(sm), h3(sm), mx, ALU.subtract).then_inc(shifted_ready, 1)

            def softmax_norm(g, tt, probs_turned):
                dve.wait_ge(exp_ready, nth(g, TILES, tt))
                dve.tensor_reduce(sst[:, 1, :], h3(E), AX_X, ALU.add).then_inc(sum_ready, 1)
                dve.wait_ge(sum_ready, nth(g, TILES, tt))
                dve.reciprocal(sst[:, 2, :], sst[:, 1, :]).then_inc(recip_ready, 1)
                dve.wait_ge(recip_ready, nth(g, TILES, tt))
                if probs_turned is not None:
                    dve.wait_ge(turned, probs_turned)

                def place(to, w, keys):
                    rows = slice(w * WIN, (w + 1) * WIN)
                    rc = sst[rows, 2, :].rearrange("p (h o) -> p h o", o=1).broadcast_to([WIN, FH, to.shape[2]])
                    return dve.tensor_tensor(to, h3(E)[rows, :, keys], rc, ALU.mult)
                if tt % 2 == 1:
                    place(EPv[0:WIN, :, 3 * WIN:4 * WIN], 0, slice(0, WIN))
                place(EP[0:WIN, :, 0:WIN], 0, slice(WIN, 2 * WIN))
                for w in range(1, 4):
                    last = place(EP[w * WIN:(w + 1) * WIN, :, (w - 1) * WIN:(w + 1) * WIN], w, slice(0, 2 * WIN))
                last.then_inc(padded_ready, 1)

            def norms(g, tt):
                dve.wait_ge(qkv_copied, nth(g, QKV_PER, 6 * tt + 3) + 2)
                dve.tensor_reduce(nrm[:, 3, :], h3(sq), AX_X, ALU.add).then_inc(norm2_own, 1)
                dve.wait_ge(norm2_own, nth(g, TILES, tt) + 1)
                dve.tensor_scalar(nrm[:, 0, :], nrm[:, 3, :], 1e-24, None, ALU.max).then_inc(norm2_ready, 1)

            def unit_length(g, tt):
                raw = raws[tt % 2]
                dve.wait_ge(rnorm_ready, nth(g, TILES, tt))
                for k in range(2):
                    part = slice(k * INNER, (k + 1) * INNER)
                    rn = nrm[:, 2, k * FH:(k + 1) * FH].rearrange("p (h o) -> p h o", o=1)\
                        .broadcast_to([P, FH, FD])
                    dve.tensor_tensor(h3(raw[:, part]), h3(raw[:, part]), rn, ALU.mult).then_inc(u_ready, 1)

            def add_stream(g, it, uu):
                at = ds((it * UNITS_IN_BODY + uu) * T, T)
                dve.wait_ge(o_copied, nth(g, HEAD_PER, 5 * uu + 4) + 2)
                dve.tensor_tensor(XT[:, at], XT[:, at], ysb, ALU.add).then_inc(stream_added, 1)

            def body(g, it, final):
                for tt in range(TILES):
                    if not (final and tt + 2 >= TILES):
                        norms(g, tt + 2)
                        unit_length(g, tt + 2)
                    if not (final and tt + 1 >= TILES):
                        softmax_shift(g, tt + 1)
                        softmax_norm(g, tt + 1, nth(g, TURN_PER, place_probs(tt, 3 + tt % 2, final)))
                    if tt % 2 == 1:
                        add_stream(g, it, tt // 2)
            wait_alone(dve, tables_ready, run + 1)
            first = run * BODIES
            norms(first, 0)
            unit_length(first, 0)
            norms(first, 1)
            unit_length(first, 1)
            softmax_shift(first, 0)
            softmax_norm(first, 0, None)
            with dve.Fori(0, BODIES - 1) as it:
                body(first + it, it, False)
            body(first + BODIES - 1, BODIES - 1, True)

        def fa_gpsimd(pool, run):
            pool.wait_ge(attn_w_loaded, (run + 1) * ATTN_LOADS)
            for k in range(4):
                last = pool.tensor_tensor(table[:, k, :, :], rotary[:, k, :, :],
                                          qks[:, k:k + 1, :].broadcast_to([P, 2, FD]), ALU.mult)
            last.then_inc(tables_ready, 1)
            wait_alone(pool, tables_ready, run + 1)

            def rotate(g, tt, qk_turned):
                par = tt % 2
                for k in range(2):
                    part = slice(k * INNER, (k + 1) * INNER)
                    heads = lambda a: a[:, part].rearrange("p (h e) -> p h e", e=FD)
                    if k == 0 and qk_turned is not None:
                        wait_alone(pool, turned, qk_turned)
                    wait_alone(pool, u_ready, nth(g, 2 * TILES, 2 * tt + k))
                    for half in range(2):
                        a, b = half * 32, 32 - half * 32
                        sine = table[:, 2 + k, par:par + 1, a:a + 32].broadcast_to([P, FH, 32])
                        last = pool.tensor_tensor(heads(t2)[:, :, a:a + 32], heads(raws[par])[:, :, b:b + 32], sine,
                                                  ALU.mult)
                    last.then_inc(t2_ready, 1)
                    cosine = table[:, k, par:par + 1, :].broadcast_to([P, FH, FD])
                    pool.tensor_tensor(heads(t1), heads(raws[par]), cosine, ALU.mult).then_inc(t1_ready, 1)
            rotate(run * BODIES, 0, None)
            with pool.Fori(0, BODIES - 1) as it:
                for tt in range(1, TILES + 1):
                    g = run * BODIES + it
                    rotate(g, tt, nth(g, TURN_PER, place_qk(tt - 1, 3)))
            for tt in range(1, TILES):
                g = run * BODIES + BODIES - 1
                rotate(g, tt, nth(g, TURN_PER, place_qk(tt - 1, 3)))

        ATTN_LOADS, MLP_LOADS = 16 * 3, 16 * 4

        def ff_shift_vector(dve, run):
            dve.memset(XN[64:128, :].rearrange("p (b t) -> p b t", t=T)[:, :, 0:1], 0.0).then_inc(edge_zeroed, 1)
            for c in range(NCH):
                dve.tensor_copy(XN[0:64, c * CH:(c + 1) * CH], XT[0:64, c * CH:(c + 1) * CH]).then_inc(low_shifted, 1)

        def ff_shift_scalar(act, run):
            for c in range(NCH):
                to = XN[64:128, c * CH:(c + 1) * CH].rearrange("p (b t) -> p b t", t=T)
                fr = XT[64:128, c * CH:(c + 1) * CH].rearrange("p (b t) -> p b t", t=T)
                act.activation(to[:, :, 1:T], fr[:, :, 0:T - 1], ACT.Copy).then_inc(high_shifted, 1)

        def ff_tensor(pe, run, n):
            pe.wait_ge(edge_zeroed, run + 1)
            pe.wait_ge(low_shifted, nth(run, NCH, NCH - 1))
            pe.wait_ge(high_shifted, nth(run, NCH, NCH - 1))
            ln_tensor(pe, n, XN)
            M = len(DIM)

            def up(c):
                if c == 0:
                    pe.wait_ge(mlp_w_loaded, (run + 1) * MLP_LOADS)
                pe.wait_ge(ln_out, nth(run, NCH, NCH - 1))
                for m in range(M):
                    if c > 0:
                        pe.wait_ge(h_ready, nth(run, M * NCH, M * (c - 1) + m))
                    for k, first in ((0, DI), (1, 0)):
                        pe.matmul(PS[0:DIM[m], 2 * m + k, :], W1[:, first + P * m:first + P * m + DIM[m]],
                                  chunk(XN, c), start=True, stop=True).then_inc(up_ready, 1)

            def down(c):
                if c >= 2:
                    pe.wait_ge(down_added, nth(run, NCH, c - 2))
                for m in range(M):
                    pe.wait_ge(h_ready, nth(run, M * NCH, M * c + m))
                    last = pe.matmul(PS[:, 6 + c % 2, :], W2[0:DIM[m], m, :], hh[0:DIM[m], c % 2, m, :],
                                     start=(m == 0), stop=(m == M - 1))
                last.then_inc(down_ready, 1)
            up(0)
            for c in range(NCH):
                if c + 1 < NCH:
                    up(c + 1)
                down(c)

        def ff_scalar(act, run, n):
            M = len(DIM)
            ff_shift_scalar(act, run)
            ln_scalar(act, n)
            for c in range(NCH):
                for m in range(M):
                    act.wait_ge(up_ready, nth(run, 2 * M * NCH, 2 * (M * c + m)))
                    act.activation(gl[0:DIM[m], c % 2, m, :], PS[0:DIM[m], 2 * m, :], ACT.Gelu,
                                   bias=fvec[0:DIM[m], 3 + m:4 + m]).then_inc(gelu_ready, 1)

        def ff_vector(dve, run, n):
            M = len(DIM)
            ff_shift_vector(dve, run)
            dve.wait_ge(edge_zeroed, run + 1)
            dve.wait_ge(low_shifted, nth(run, NCH, NCH - 1))
            dve.wait_ge(high_shifted, nth(run, NCH, NCH - 1))
            dve.wait_ge(mlp_w_loaded, (run + 1) * MLP_LOADS)
            ln_vector(dve, n, XN, XN, gain=(fvec[:, 0:1], fvec[:, 1:2]))

            def gated(c):
                for m in range(M):
                    dve.wait_ge(gelu_ready, nth(run, M * NCH, M * c + m))
                    dve.wait_ge(up_ready, nth(run, 2 * M * NCH, 2 * (M * c + m) + 1))
                    rows = slice(0, DIM[m])
                    dve.scalar_tensor_tensor(hh[rows, c % 2, m, :], PS[rows, 2 * m + 1, :], fvec[rows, 6 + m:7 + m],
                                             gl[rows, c % 2, m, :], ALU.add, ALU.mult).then_inc(h_ready, 1)
            gated(0)
            for c in range(NCH):
                if c + 1 < NCH:
                    gated(c + 1)
                dve.wait_ge(down_ready, nth(run, NCH, c))
                dve.scalar_tensor_tensor(chunk(XT, c), PS[:, 6 + c % 2, :], fvec[:, 2:3], chunk(XT, c),
                                         ALU.add, ALU.add).then_inc(down_added, 1)

        def ffn_tensor(pe, call, K, n0):
            ln_tensor(pe, n0, XO)
            meet(pe, K + 1)
            with pe.Fori(0, DEPTH) as l:
                fa_tensor(pe, l + call * DEPTH)
                meet(pe, l * 2 + K + 2)
                ff_tensor(pe, l + call * DEPTH, l + n0 + 1)
                meet(pe, l * 2 + K + 3)

        def ffn_scalar(act, call, K, n0):
            ln_scalar(act, n0)
            meet(act, K + 1)
            with act.Fori(0, DEPTH) as l:
                log_exp_tables(act)
                fa_scalar(act, l + call * DEPTH)
                meet(act, l * 2 + K + 2)
                ff_scalar(act, l + call * DEPTH, l + n0 + 1)
                meet(act, l * 2 + K + 3)

        def ffn_vector(dve, call, K, n0):
            ln_vector(dve, n0, XO, XT)
            meet(dve, K + 1)
            with dve.Fori(0, DEPTH) as l:
                fa_vector(dve, l + call * DEPTH)
                meet(dve, l * 2 + K + 2)
                ff_vector(dve, l + call * DEPTH, l + n0 + 1)
                meet(dve, l * 2 + K + 3)
            for c in range(NCH):
                last = dve.tensor_tensor(chunk(XO, c), chunk(XO, c), chunk(XT, c), ALU.add)

        def ffn_gpsimd(pool, call, K, n0):
            for uu in range(UNITS_IN_BODY):
                pool.memset(xs[uu][:, 0:1], 0.0)
                pool.memset(KT[uu][:, :, 0:WIN], 0.0)
            pool.memset(EP, 0.0)
            pool.memset(EPv, 0.0)
            meet(pool, K + 1)
            wait_alone(pool, ffn_const_loaded, 32 * (call + 1))
            with pool.Fori(0, DEPTH) as l:
                fa_gpsimd(pool, l + call * DEPTH)
                meet(pool, l * 2 + K + 2)
                meet(pool, l * 2 + K + 3)

        def ffn_sync(sp, call, K):
            def attention(layer):
                sp.dma_start(Wqkv, d["L0_ffn_Wqkv"][layer, :, :].rearrange("o p n -> (o p) n")).then_inc(attn_w_loaded, 16)
                sp.dma_start(Wo, d["L0_ffn_Wo"][layer, :, :].rearrange("o (m p) n -> p (o m) n", p=P)).then_inc(attn_w_loaded, 16)
                sp.dma_start(qks, d["ffn_scales"][layer, :].rearrange("o (k e) -> o k e", k=4)
                             .broadcast_to([P, 4, FD])).then_inc(attn_w_loaded, 16)

            def feed_forward(layer):
                sp.dma_start(W1, d["L0_ffn_W1"][layer, :, :].rearrange("o p n -> (o p) n")).then_inc(mlp_w_loaded, 16)
                full = 2 * P
                w2 = d["L0_ffn_W2"]
                sp.dma_start(W2[:, 0:2, :], w2[layer, 0:full, :].rearrange("o (m p) n -> p (o m) n", p=P)).then_inc(mlp_w_loaded, 16)
                sp.dma_start(W2[0:DIM[2], 2, :], w2[layer, full:DI, :].rearrange("o p n -> (o p) n")).then_inc(mlp_w_loaded, 16)
                sp.dma_start(fvec[:, 0:9], d["ffn_vectors"][layer, :, :].rearrange("o p n -> (o p) n")).then_inc(mlp_w_loaded, 16)
            if K > 0:
                sp.wait_ge(phase_end, 4 * K)
            attention(slice(0, 1))
            feed_forward(slice(0, 1))
            sp.dma_start(rotary, d["c_rotary"].rearrange("p (k t e) -> p k t e", k=4, t=2)).then_inc(ffn_const_loaded, 16)
            sp.dma_start(masks, d["c_masks"].rearrange("p (t j) -> p t j", t=2)).then_inc(ffn_const_loaded, 16)
            with sp.Fori(0, DEPTH - 1) as l:
                sp.wait_ge(phase_end, (l * 2 + K + 2) * 4)
                attention(ds(l + 1, 1))
                sp.wait_ge(phase_end, (l * 2 + K + 3) * 4)
                feed_forward(ds(l + 1, 1))

        HD8 = 8
        MAX_NORM2 = float(HD8) * 4.0
        a0 = Space(0)
        a0_w = [a0.take(C) for _ in range(5)]
        a0_vec = a0.take(16)
        a0_rest = a0.take(4)
        a0_head = a0.take(8)
        a0_G = a0.take(N)
        a0_sh = a0.take(N)
        a0_R = a0.take(N)
        a0_K = a0.take(N)
        a0_V = a0.take(N)
        a0_F = a0.take(T + 1)
        a0_DF = a0.take(T + 1)
        a0_small = a0.take(64)
        a0_rn = a0.take(2 * T)
        a0_step = a0.take(256)
        a0_H = a0.take((T + 1) * HD8 * HD8)
        a0_mix = a0_H[:, 0:4 * N]
        a0_out = a0_H[:, 4 * N:7 * N]
        a0_tmp = a0_sh
        scratch = nc.dram_tensor("scratch", (4, B, C, T), F32, kind="Internal").ap()
        s_mix = sem("s_mix")
        s_sh = sem("s_sh")
        s_rest = sem("s_rest")
        s_part = sem("s_part")
        s_proj = sem("s_proj")
        s_act = sem("s_act")
        s_gate = sem("s_gate")
        s_a0w = sem("s_a0w")
        s_out = [sem(f"s_out{i}") for i in range(3)]
        s_in = sem("s_in")
        s_sq = sem("s_sq")
        s_n2 = sem("s_n2")
        s_rn = sem("s_rn")
        s_unit = sem("s_unit")
        scan_step = sem("scan_step")
        scan_norm = sem("scan_norm")
        s_wkv = sem("s_wkv")
        s_stat = sem("s_stat")
        s_rstd = sem("s_rstd")
        s_back = sem("s_back")
        s_backed = sem("s_backed")
        s_gn = sem("s_gn")
        s_o = sem("s_o")
        s_x = sem("s_x")
        r3 = lambda a: a.rearrange("p (d t) -> p d t", t=T)
        H3 = a0_H.rearrange("p (t e) -> p t e", e=HD8 * HD8)
        STEPS = 4

        def a0_sync(sp):
            for k, name in enumerate(("r", "k", "v", "g", "o")):
                sp.dma_start(a0_w[k], d[f"a0_W_{name}"]).then_inc(s_a0w, 16)
            sp.dma_start(a0_vec, d["a0_vectors"]).then_inc(s_a0w, 16)
            sp.dma_start(a0_head[:, 0:2], d["a0_heads"]).then_inc(s_a0w, 16)
            for k in range(3):
                sp.wait_ge(s_act, (k + 1) * NCH)
                sp.dma_start(scratch[k].rearrange("b c t -> c b t"),
                             a0_out[:, k * N:(k + 1) * N].rearrange("p (b t) -> p b t", b=B)).then_inc(s_out[k], 16)
            for k, to in enumerate((a0_R, a0_K, a0_V)):
                sp.wait_ge(s_out[k], 16)
                sp.dma_start(to, scratch[k].rearrange("b (h d) t -> (b h) (d t)", d=HD8)).then_inc(s_in, 16)
            sp.wait_ge(s_wkv, 6)
            sp.dma_start(scratch[3].rearrange("b (h d) t -> (b h) (d t)", d=HD8), a0_tmp).then_inc(s_back, 16)
            sp.wait_ge(s_back, 16)
            sp.dma_start(a0_R.rearrange("p (b t) -> p b t", b=B), scratch[3].rearrange("b c t -> c b t"))\
              .then_inc(s_backed, 16)

        def a0_vector(dve, n0):
            ln_vector(dve, n0, XO, XN)
            dve.memset(a0_sh.rearrange("p (b t) -> p b t", t=T)[:, :, 0:1], 0.0).then_inc(s_rest, 1)
            dve.wait_ge(s_a0w, 16 * 7)
            dve.tensor_scalar(a0_rest, a0_vec[:, 0:4], -1.0, 1.0, ALU.mult, ALU.add).then_inc(s_rest, 1)
            dve.wait_ge(s_rest, 2)
            dve.wait_ge(ln_scaled, (n0 + 1) * NCH)
            dve.tensor_copy(a0_sh.rearrange("p (b t) -> p b t", t=T)[:, :, 1:T],
                            XN[:].rearrange("p (b t) -> p b t", t=T)[:, :, 0:T - 1]).then_inc(s_sh, 1)
            dve.wait_ge(s_sh, 1)
            for k in range(4):
                dve.wait_ge(s_part, k + 1)
                m = a0_mix[:, k * N:(k + 1) * N]
                dve.scalar_tensor_tensor(m, a0_sh, a0_rest[:, k:k + 1], m, ALU.mult, ALU.add).then_inc(s_mix, 1)
            for c in range(NCH):
                dve.wait_ge(s_act, 4 * NCH - NCH + c + 1)
                dve.scalar_tensor_tensor(chunk(a0_G, c), PS[:, 4 + c, :], a0_vec[:, 7:8], chunk(a0_G, c),
                                         ALU.add, ALU.mult).then_inc(s_gate, 1)
            dve.wait_ge(s_unit, 1)
            dve.tensor_scalar(a0_head[:, 3:4], a0_head[:, 3:4], -1.0, None, ALU.mult).then_inc(s_unit, 1)
            dve.wait_ge(s_in, 48)
            for k, a in enumerate((a0_K, a0_V)):
                if k:
                    dve.wait_ge(s_n2, 1)
                dve.tensor_tensor(a0_tmp, a, a, ALU.mult).then_inc(s_sq, 1)
                dve.wait_ge(s_sq, k + 1)
                rn = a0_rn[:, k * T:(k + 1) * T]
                dve.tensor_reduce(rn, a0_tmp.rearrange("p (d t) -> p t d", t=T), AX_X, ALU.add).then_inc(s_n2, 1)
            dve.wait_ge(s_n2, 2)
            dve.tensor_scalar(a0_rn, a0_rn, 1e-24, None, ALU.max).then_inc(s_n2, 1)
            dve.wait_ge(s_rn, 2)
            for k, a in enumerate((a0_K, a0_V)):
                rn = a0_rn[:, k * T:(k + 1) * T].rearrange("p (o t) -> p o t", o=1).broadcast_to([P, HD8, T])
                dve.tensor_tensor(r3(a), r3(a), rn, ALU.mult).then_inc(s_sq, 1)
            dve.wait_ge(s_sq, 4)
            dve.tensor_scalar(a0_KEs, a0_K, a0_head[:, 3:4], None, ALU.mult).then_inc(s_unit, 1)
            dve.memset(a0_H[:, 0:HD8 * HD8], 0.0).then_inc(s_unit, 1)
            dve.memset(a0_F[:, 0:1], 1.0).then_inc(s_unit, 1)
            dve.wait_ge(s_unit, 5)
            prod = a0_step[:, 0:64].rearrange("p (i j) -> p i j", j=HD8)
            outer = a0_step[:, 64:128].rearrange("p (i j) -> p i j", j=HD8)
            pred = a0_step[:, 128:136]
            err = a0_step[:, 136:144]
            with dve.Fori(0, T // STEPS) as turn:
                for q in range(STEPS):
                    g = turn * STEPS + q
                    n = turn * STEPS * 6 + 6 * q
                    col = ds(g, 1)
                    kj = r3(a0_K)[:, :, col].rearrange("p j o -> p o j").broadcast_to([P, HD8, HD8])
                    ke = r3(a0_KEs)[:, :, col].rearrange("p j o -> p o j").broadcast_to([P, HD8, HD8])
                    before = a0_H[:, ds(g * 64, 64)]
                    after = a0_H[:, ds(g * 64 + 64, 64)]
                    dve.tensor_tensor(prod, before.rearrange("p (i j) -> p i j", j=HD8), kj, ALU.mult)\
                       .then_inc(scan_step, 1)
                    dve.wait_ge(scan_step, n + 1)
                    dve.tensor_reduce(pred, prod, AX_X, ALU.add).then_inc(scan_step, 1)
                    dve.wait_ge(scan_norm, turn * STEPS * 4 + 4 * q + 4)
                    dve.wait_ge(scan_step, n + 2)
                    dve.scalar_tensor_tensor(err, pred, a0_F[:, col], r3(a0_V)[:, :, col].rearrange("p i o -> p (i o)"),
                                             ALU.mult, ALU.subtract).then_inc(scan_step, 1)
                    dve.tensor_scalar(a0_DF[:, col], a0_F[:, col], a0_head[:, 2:3], None, ALU.mult)\
                       .then_inc(scan_step, 1)
                    dve.wait_ge(scan_step, n + 3)
                    dve.tensor_tensor(outer, err.rearrange("p (i o) -> p i o", o=1).broadcast_to([P, HD8, HD8]),
                                      ke, ALU.mult).then_inc(scan_step, 1)
                    dve.wait_ge(scan_step, n + 5)
                    dve.scalar_tensor_tensor(after, before, a0_DF[:, col], a0_step[:, 64:128],
                                             ALU.mult, ALU.add).then_inc(scan_step, 1)
                    dve.wait_ge(scan_step, n + 6)
            dve.wait_ge(scan_norm, 4 * T + 4)
            W3 = r3(a0_tmp)
            part = T // 4
            prod4 = a0_big.rearrange("p (t i j) -> p t i j", i=HD8, j=HD8)
            for c in range(4):
                dve.tensor_tensor(
                    a0_big.rearrange("p (t i j) -> p t i j", i=HD8, j=HD8),
                    H3[:, 1 + c * part:1 + (c + 1) * part, :].rearrange("p t (i j) -> p t i j", j=HD8),
                    a0_R.rearrange("p (j o t) -> p t o j", t=T, o=1)[:, c * part:(c + 1) * part, :, :]
                    .broadcast_to([P, part, HD8, HD8]), ALU.mult).then_inc(s_stat, 1)
                dve.wait_ge(s_stat, 2 * c + 1)
                dve.tensor_reduce(W3.rearrange("p i t -> p t i")[:, c * part:(c + 1) * part, :], prod4, AX_X,
                                  ALU.add).then_inc(s_stat, 1)
                dve.wait_ge(s_stat, 2 * c + 2)
            fb = a0_F[:, 1:T + 1].rearrange("p (o t) -> p o t", o=1).broadcast_to([P, HD8, T])
            dve.tensor_tensor(W3, W3, fb, ALU.mult).then_inc(s_wkv, 1)
            dve.wait_ge(s_wkv, 1)
            for c in range(NCH):
                dve.bn_stats(a0_small[:, 8 + 6 * c:14 + 6 * c], chunk(a0_tmp, c)).then_inc(s_wkv, 1)
            dve.wait_ge(s_wkv, 5)
            dve.bn_aggr(a0_small[:, 40:42], a0_small[:, 8:8 + 6 * NCH].rearrange("p (c s) -> p c s", s=6))\
               .then_inc(s_stat, 1)
            dve.wait_ge(s_rstd, 2)
            dve.tensor_scalar(a0_tmp, a0_tmp, a0_small[:, 40:41], a0_small[:, 43:44], ALU.subtract, ALU.mult)\
               .then_inc(s_wkv, 1)
            dve.wait_ge(s_backed, 16)
            dve.tensor_scalar(a0_R, a0_R, a0_vec[:, 9:10], a0_vec[:, 10:11], ALU.mult, ALU.add).then_inc(s_gn, 1)
            for c in range(NCH):
                dve.wait_ge(s_o, c + 1)
                dve.scalar_tensor_tensor(chunk(a0_G, c), PS[:, c, :], a0_vec[:, 8:9], chunk(a0_G, c),
                                         ALU.add, ALU.mult).then_inc(s_x, 1)
                dve.wait_ge(s_x, c + 1)
                dve.tensor_tensor(chunk(XO, c), chunk(XO, c), chunk(a0_G, c), ALU.add)

        a0_KEs = a0.take(N)
        a0_big = arena[:, a0.at:a0.at + (T // 4) * 64]
        a0.take((T // 4) * 64)

        def a0_scalar(act, n0):
            ln_scalar(act, n0)
            act.wait_ge(s_a0w, 16 * 7)
            act.wait_ge(ln_scaled, (n0 + 1) * NCH)
            for k in range(4):
                act.activation(a0_mix[:, k * N:(k + 1) * N], XN[:], ACT.Identity, scale=a0_vec[:, k:k + 1])\
                   .then_inc(s_part, 1)
            act.activation(a0_head[:, 2:4], a0_head[:, 0:2], ACT.Sigmoid).then_inc(s_unit, 1)
            for k in range(4):
                for c in range(NCH):
                    act.wait_ge(s_proj, k * NCH + c + 1)
                    bank = PS[:, (k % 2) * 4 + c, :]
                    to = chunk(a0_out[:, k * N:(k + 1) * N], c) if k < 3 else chunk(a0_G, c)
                    act.activation(to, bank, ACT.Sigmoid if k in (0, 3) else ACT.Identity,
                                   bias=a0_vec[:, 4 + k:5 + k]).then_inc(s_act, 1)
            log_exp_tables(act)
            act.wait_ge(s_n2, 3)
            act.activation(a0_rn, a0_rn, ACT.Ln, scale=float(2 ** 24)).then_inc(s_rn, 1)
            act.wait_ge(s_rn, 1)
            act.activation(a0_rn, a0_rn, ACT.Exp, bias=eps[:, 1:2], scale=-0.5).then_inc(s_rn, 1)
            act.wait_ge(s_unit, 5)
            with act.Fori(0, T // STEPS) as turn:
                for q in range(STEPS):
                    g = turn * STEPS + q
                    n = turn * STEPS * 4 + 4 * q + 4
                    act.wait_ge(scan_step, turn * STEPS * 6 + 6 * q + 6)
                    after = a0_H[:, ds(g * 64 + 64, 64)]
                    act.activation(a0_step[:, 192:256], after, ACT.Square, accum_out=a0_small[:, 0:1])\
                       .then_inc(scan_norm, 1)
                    act.wait_ge(scan_norm, n + 1)
                    act.activation(a0_small[:, 1:2], a0_small[:, 0:1], ACT.Ln, bias=eps[:, 3:4],
                                   scale=1.0 / MAX_NORM2).then_inc(scan_norm, 1)
                    act.wait_ge(scan_norm, n + 2)
                    act.activation(a0_small[:, 2:3], a0_small[:, 1:2], ACT.Relu).then_inc(scan_norm, 1)
                    act.wait_ge(scan_norm, n + 3)
                    act.activation(a0_F[:, ds(g + 1, 1)], a0_small[:, 2:3], ACT.Exp, scale=-0.5).then_inc(scan_norm, 1)
            act.wait_ge(s_stat, 9)
            act.activation(a0_small[:, 42:43], a0_small[:, 41:42], ACT.Ln, bias=eps[:, 0:1]).then_inc(s_rstd, 1)
            act.wait_ge(s_rstd, 1)
            act.activation(a0_small[:, 43:44], a0_small[:, 42:43], ACT.Exp, scale=-0.5).then_inc(s_rstd, 1)

        def a0_tensor(pe, n0):
            ln_tensor(pe, n0, XO)
            for k in range(4):
                pe.wait_ge(s_mix, k + 1)
                for c in range(NCH):
                    if k >= 2:
                        pe.wait_ge(s_act, (k - 2) * NCH + c + 1)
                    if k == 0 and c == 0:
                        pe.wait_ge(ln_scaled, (n0 + 1) * NCH)
                    pe.matmul(PS[:, (k % 2) * 4 + c, :], a0_w[k], chunk(a0_mix[:, k * N:(k + 1) * N], c),
                              start=True, stop=True).then_inc(s_proj, 1)
            pe.wait_ge(s_gn, 1)
            for c in range(NCH):
                pe.matmul(PS[:, c, :], a0_w[4], chunk(a0_R, c), start=True, stop=True).then_inc(s_o, 1)

        a1 = Space(0)
        a1_w = [a1.take(C) for _ in range(4)]
        a1_vec = a1.take(8)
        a1_tab = a1.take(6 * T).rearrange("p (k t) -> p k t", k=6)
        a1_cross = a1.take(T)
        a1_keep = a1.take(N)
        a1_S = a1.take(N)
        a1_Z = a1.take(N)
        a1_D = [a1.take(N) for _ in range(2)]
        a1_GY = a1.take(N)
        a1_sq = a1.take(N)
        a1_loaded = sem("a1_loaded")
        a1_proj = sem("a1_proj")
        a1_sigmoid = sem("a1_sigmoid")
        a1_gate = sem("a1_gate")
        a1_z = sem("a1_z")
        a1_keep_ready = sem("a1_keep_ready")
        a1_down = sem("a1_down")
        a1_run = sem("a1_run")
        a1_up = sem("a1_up")
        a1_cross_ready = sem("a1_cross_ready")
        a1_h = sem("a1_h")
        a1_squared = sem("a1_squared")
        a1_mean = sem("a1_mean")
        a1_log = sem("a1_log")
        a1_rms = sem("a1_rms")
        a1_normed = sem("a1_normed")
        a1_y = sem("a1_y")
        bt = lambda a: a.rearrange("p (b t) -> p b t", t=T)

        def a1_sync(sp):
            for k, name in enumerate(("za", "z", "ya", "y")):
                sp.dma_start(a1_w[k], d[f"a1_W_{name}"]).then_inc(a1_loaded, 16)
            sp.dma_start(a1_vec, d["a1_vectors"]).then_inc(a1_loaded, 16)
            sp.dma_start(a1_tab, d["c_phazor"].rearrange("p (k t) -> p k t", k=6)).then_inc(a1_loaded, 16)

        def a1_tensor(pe, n0):
            ln_tensor(pe, n0, XO)
            pe.wait_ge(a1_loaded, 16 * 6)
            pe.wait_ge(ln_scaled, (n0 + 1) * NCH)
            for k in range(3):
                for c in range(NCH):
                    if k == 2:
                        pe.wait_ge(a1_gate, c + 1)
                    pe.matmul(PS[:, (k % 2) * 4 + c, :], a1_w[k], chunk(XN, c), start=True, stop=True)\
                      .then_inc(a1_proj, 1)
            for c in range(NCH):
                pe.wait_ge(a1_squared, c + 1)
                pe.matmul(PS[:, 4 + c, :], mean_w[:], chunk(a1_sq, c), start=True, stop=True).then_inc(a1_mean, 1)
            for c in range(NCH):
                pe.wait_ge(a1_normed, c + 1)
                pe.matmul(PS[:, c, :], a1_w[3], chunk(a1_Z, c), start=True, stop=True).then_inc(a1_proj, 1)

        def a1_scalar(act, n0):
            ln_scalar(act, n0)
            for k, of in ((0, 0), (1, 2)):
                for c in range(NCH):
                    act.wait_ge(a1_proj, of * NCH + c + 1)
                    if k == 1:
                        act.wait_ge(a1_gate, c + 1)
                    act.activation(chunk(a1_S, c), PS[:, c, :], ACT.Sigmoid, bias=a1_vec[:, of:of + 1])\
                       .then_inc(a1_sigmoid, 1)
            log_exp_tables(act)
            for c in range(NCH):
                act.wait_ge(a1_h, c + 1)
                act.activation(chunk(a1_sq, c), chunk(a1_D[0], c), ACT.Square).then_inc(a1_squared, 1)
                act.wait_ge(a1_mean, c + 1)
                act.wait_ge(a1_gate, NCH + c + 1)
                act.activation(chunk(a1_S, c), PS[:, 4 + c, :], ACT.Ln, bias=eps[:, 2:3]).then_inc(a1_log, 1)
                act.wait_ge(a1_log, c + 1)
                act.activation(chunk(a1_S, c), chunk(a1_S, c), ACT.Exp, scale=-0.5).then_inc(a1_rms, 1)

        def a1_vector(dve, n0):
            ln_vector(dve, n0, XO, XN)
            dve.memset(a1_keep, 1.0).then_inc(a1_keep_ready, 1)
            dve.wait_ge(a1_keep_ready, 1)
            dve.memset(bt(a1_keep)[:, :, 0:1], 0.0).then_inc(a1_keep_ready, 1)
            dve.wait_ge(a1_loaded, 16 * 6)
            dve.tensor_scalar(a1_cross, a1_tab[:, 4, :], a1_vec[:, 5:6], None, ALU.mult).then_inc(a1_cross_ready, 1)
            dve.wait_ge(a1_cross_ready, 1)
            dve.scalar_tensor_tensor(a1_cross, a1_tab[:, 5, :], a1_vec[:, 6:7], a1_cross, ALU.mult, ALU.add)\
               .then_inc(a1_cross_ready, 1)
            for c in range(NCH):
                dve.wait_ge(a1_sigmoid, c + 1)
                dve.scalar_tensor_tensor(chunk(a1_Z, c), PS[:, c, :], a1_vec[:, 0:1], chunk(a1_S, c),
                                         ALU.add, ALU.mult).then_inc(a1_gate, 1)
                dve.wait_ge(a1_gate, c + 1)
                dve.wait_ge(a1_proj, NCH + c + 1)
                dve.scalar_tensor_tensor(chunk(a1_Z, c), PS[:, 4 + c, :], a1_vec[:, 1:2], chunk(a1_Z, c),
                                         ALU.add, ALU.mult).then_inc(a1_z, 1)
            dve.wait_ge(a1_z, NCH)
            dve.wait_ge(a1_keep_ready, 2)
            for k in range(2):
                table_of = lambda j: a1_tab[:, j:j + 1, :].broadcast_to([P, B, T])
                D = a1_D[k]
                dve.tensor_tensor(bt(D), bt(a1_Z), table_of(k), ALU.mult).then_inc(a1_down, 1)
                dve.wait_ge(a1_down, k + 1)
                dve.tensor_tensor_scan(D, a1_keep, D, 0.0, ALU.mult, ALU.add).then_inc(a1_run, 1)
                dve.wait_ge(a1_run, k + 1)
                dve.tensor_tensor(bt(D), bt(D), table_of(2 + k), ALU.mult).then_inc(a1_up, 1)
                dve.wait_ge(a1_up, k + 1)
            dve.wait_ge(a1_cross_ready, 2)
            cross = a1_cross.rearrange("p (o t) -> p o t", o=1).broadcast_to([P, CH // T, T])
            for c in range(NCH):
                dve.tensor_tensor(bt(chunk(a1_D[1], c)), bt(chunk(a1_D[1], c)), cross, ALU.add).then_inc(a1_up, 1)
                dve.wait_ge(a1_up, 3 + c)
                dve.tensor_tensor(chunk(a1_D[0], c), chunk(a1_D[0], c), chunk(a1_D[1], c), ALU.add).then_inc(a1_h, 1)
            for c in range(NCH):
                dve.wait_ge(a1_sigmoid, NCH + c + 1)
                dve.scalar_tensor_tensor(chunk(a1_GY, c), PS[:, c, :], a1_vec[:, 2:3], chunk(a1_S, c),
                                         ALU.add, ALU.mult).then_inc(a1_gate, 1)
            for c in range(NCH):
                dve.wait_ge(a1_rms, c + 1)
                dve.scalar_tensor_tensor(chunk(a1_Z, c), chunk(a1_D[0], c), a1_vec[:, 4:5], chunk(a1_S, c),
                                         ALU.mult, ALU.mult).then_inc(a1_normed, 1)
            for c in range(NCH):
                dve.wait_ge(a1_proj, 3 * NCH + c + 1)
                dve.scalar_tensor_tensor(chunk(a1_GY, c), PS[:, c, :], a1_vec[:, 3:4], chunk(a1_GY, c),
                                         ALU.add, ALU.mult).then_inc(a1_y, 1)
                dve.wait_ge(a1_y, c + 1)
                dve.tensor_tensor(chunk(XO, c), chunk(XO, c), chunk(a1_GY, c), ALU.add)

        SMALL = 16
        GROUPS, HEADS_IN_GROUP, GROUP = 4, 4, 32
        PAIRS8 = SMALL // 2
        hd = Space(0)
        hd_w = [hd.take(C) for _ in range(5)]
        hd_only = hd.take(HEADS_IN_GROUP)
        hd_x = hd.take(T)
        hd_q = hd.take(T)
        hd_k = hd.take(T)
        hd_m = [hd.take(T) for _ in range(HEADS_IN_GROUP)]
        hd_v = hd.take(2 * C).rearrange("p (t n) -> p t n", t=2)
        VGROUP = HEADS_IN_GROUP * 40
        hd_vm = hd.take(2 * GROUPS * VGROUP).rearrange("p (t n) -> p t n", t=2)
        hd_e = [hd.take(4 * T).rearrange("p (h t q) -> p h t q", h=2, t=2) for _ in range(2)]
        hd_st = [hd.take(16) for _ in range(2)]
        hd_Z = hd.take(N)
        hd_sq = hd.take(N)
        hd_rn = hd.take(N)
        hd_y = hd.take(N)
        hd_loaded = sem("hd_loaded")
        hd_zeroed = sem("hd_zeroed")
        hd_entered = sem("hd_entered")
        hd_proj = sem("hd_proj")
        hd_projected = sem("hd_projected")
        hd_masked = sem("hd_masked")
        hd_scores = sem("hd_scores")
        hd_max = sem("hd_max")
        hd_bias = sem("hd_bias")
        hd_exp = sem("hd_exp")
        hd_recip = sem("hd_recip")
        hd_v_ready = sem("hd_v_ready")
        hd_out = sem("hd_out")
        hd_copied = sem("hd_copied")
        tail_lin = sem("tail_lin")
        tail_sq = sem("tail_sq")
        tail_sum = sem("tail_sum")
        tail_floor = sem("tail_floor")
        tail_log = sem("tail_log")
        tail_rn = sem("tail_rn")
        tail_z = sem("tail_z")
        tail_gelu = sem("tail_gelu")
        MIX_SCALE = float(1.0 / np.sqrt(np.float32(C)))

        def mix_sync(sp):
            for k, name in enumerate(("Wq", "Wk", "Wv", "Wo", "Wff")):
                sp.dma_start(hd_w[k], d[f"L1_ffn_{name}"]).then_inc(hd_loaded, 16)
            sp.dma_start(hd_only, d["c_only"]).then_inc(hd_loaded, 16)

        def project_tensor(pe, g):
            pe.wait_ge(hd_entered, g + 1)
            for k in range(2):
                last = pe.matmul(PS[:, 5, k * T:(k + 1) * T], hd_w[k], hd_x, start=True, stop=True)
            last.then_inc(hd_proj, 1)
            for t in range(2):
                last = pe.matmul(PS[:, 6, t * C:(t + 1) * C], hd_x[:, t * P:(t + 1) * P], hd_w[2], start=True, stop=True)
            last.then_inc(hd_proj, 1)

        def mix_tensor(pe, run, call, n0):
            ln_tensor(pe, n0, XO)
            wait_alone(pe, hd_loaded, 16 * 6 * (run + 1))
            def batch(g, final):

                def scores(u):
                    if u >= 2:
                        wait_alone(pe, hd_exp, nth(g, PAIRS8, u - 2))
                    for s in range(2):
                        grp, v = divmod(2 * u + s, HEADS_IN_GROUP)
                        rows = slice(grp * GROUP, (grp + 1) * GROUP)
                        for t in range(2):
                            last = pe.matmul(PS[:, (u % 2) * 2 + s, t * T:(t + 1) * T],
                                             hd_m[v][rows, t * P:(t + 1) * P], hd_q[rows, :], start=True, stop=True)
                    last.then_inc(hd_scores, 1)

                def heads(u):
                    pe.wait_ge(hd_v_ready, nth(g, PAIRS8, u))
                    for s in range(2):
                        grp, v = divmod(2 * u + s, HEADS_IN_GROUP)
                        at = grp * VGROUP + v * GROUP
                        for t in range(2):
                            last = pe.matmul(PS[grp * GROUP:(grp + 1) * GROUP, 4, 0:T], hd_vm[:, t, at:at + GROUP],
                                             hd_e[u % 2][:, s, t, :], start=(v == 0 and t == 0),
                                             stop=(v == HEADS_IN_GROUP - 1 and t == 1), skip_group_check=True)
                    last.then_inc(hd_out, 1)
                wait_alone(pe, hd_masked, (g + 1) * HEADS_IN_GROUP)
                wait_alone(pe, hd_projected, (g + 1) * 3)
                scores(0)
                scores(1)
                for u in range(PAIRS8):
                    if u + 2 < PAIRS8:
                        scores(u + 2)
                    heads(u)
                    if u == PAIRS8 - 3 and not final:
                        project_tensor(pe, g + 1)
            project_tensor(pe, run * B + 1)
            with pe.Fori(0, B - 1) as b:
                batch(run * B + b + 1, False)
            batch(run * B + B, True)
            for k in range(2):
                n = 2 * call + k
                for c in range(NCH):
                    if k == 0 and c == 0:
                        pe.wait_ge(hd_copied, (run + 1) * B + 1)
                    if k == 1:
                        pe.wait_ge(tail_z, nth(n - 1, NCH, c))
                    pe.matmul(PS[:, c, :], hd_w[3 + k], chunk(hd_Z, c), start=True, stop=True).then_inc(tail_lin, 1)
                for c in range(NCH):
                    pe.wait_ge(tail_sq, nth(n, NCH, c))
                    pe.matmul(PS[:, 4 + c, :], mean_w[:], chunk(hd_sq, c), start=True, stop=True).then_inc(tail_sum, 1)

        def project_scalar(act, g, b):
            act.wait_ge(hd_proj, g * 2)
            act.activation(hd_x, XN[:, ds(b * T, T)], ACT.Copy).then_inc(hd_entered, 1)

        def mix_scalar(act, run, call, n0):
            ln_scalar(act, n0)
            wait_alone(act, ln_scaled, (n0 + 1) * NCH)
            def copy_projected(g):
                act.wait_ge(hd_proj, g * 2 + 1)
                act.wait_ge(hd_scores, g * PAIRS8)
                act.activation(hd_q, PS[:, 5, 0:T], ACT.Copy).then_inc(hd_projected, 1)
                act.wait_ge(hd_masked, g * HEADS_IN_GROUP)
                act.activation(hd_k, PS[:, 5, T:2 * T], ACT.Copy).then_inc(hd_projected, 1)
                act.wait_ge(hd_proj, g * 2 + 2)
                act.wait_ge(hd_v_ready, g * PAIRS8)
                act.activation(hd_v, PS[:, 6, 0:2 * C].rearrange("p (t n) -> p t n", t=2), ACT.Copy)\
                   .then_inc(hd_projected, 1)

            def batch(g, b, final):
                if not final:
                    project_scalar(act, g + 1, b + 1)
                for u in range(PAIRS8):
                    act.wait_ge(hd_bias, nth(g, PAIRS8, u))
                    if u >= 2:
                        act.wait_ge(hd_out, nth(g, PAIRS8, u - 2))
                    for s in range(2):
                        for t in range(2):
                            st = hd_st[u % 2]
                            last = act.activation(hd_e[u % 2][:, s, t, :], PS[:, (u % 2) * 2 + s, t * T:(t + 1) * T],
                                                  ACT.Exp, bias=st[:, 4 + 2 * s + t:5 + 2 * s + t], scale=MIX_SCALE,
                                                  accum_out=st[:, 8 + 2 * s + t:9 + 2 * s + t])
                    last.then_inc(hd_exp, 1)
                if not final:
                    copy_projected(g + 1)
                act.wait_ge(hd_out, (g + 1) * PAIRS8)
                act.activation(hd_Z[:, ds(b * T, T)], PS[:, 4, 0:T], ACT.Copy).then_inc(hd_copied, 1)
            project_scalar(act, run * B + 1, 0)
            copy_projected(run * B + 1)
            with act.Fori(0, B - 1) as b:
                batch(run * B + b + 1, b, False)
            batch(run * B + B, B - 1, True)
            for k in range(2):
                n = 2 * call + k
                for c in range(NCH):
                    act.wait_ge(tail_lin, nth(n, NCH, c))
                    act.activation(chunk(hd_sq, c), PS[:, c, :], ACT.Square).then_inc(tail_sq, 1)
                for c in range(NCH):
                    act.wait_ge(tail_floor, nth(n, NCH, c))
                    act.activation(chunk(hd_rn, c), chunk(hd_rn, c), ACT.Ln, scale=float(C * 2 ** 24)).then_inc(tail_log, 1)
                    act.wait_ge(tail_log, nth(n, NCH, c))
                    act.activation(chunk(hd_rn, c), chunk(hd_rn, c), ACT.Exp, bias=eps[:, 1:2], scale=-0.5)\
                       .then_inc(tail_rn, 1)
            for c in range(NCH):
                act.wait_ge(tail_z, nth(2 * call + 1, NCH, c))
                act.activation(chunk(hd_y, c), chunk(hd_Z, c), ACT.Gelu).then_inc(tail_gelu, 1)

        def mask_vector(dve, g, source, which):
            dve.wait_ge(hd_projected, g * 3 + which)
            dve.wait_ge(hd_scores, g * PAIRS8)
            for v in range(HEADS_IN_GROUP):
                dve.tensor_scalar(hd_m[v], source, hd_only[:, v:v + 1], None, ALU.mult).then_inc(hd_masked, 1)

        def mix_vector(dve, run, call, n0):
            ln_vector(dve, n0, XO, XN)
            dve.memset(hd_vm, 0.0).then_inc(hd_zeroed, 1)
            wait_alone(dve, hd_loaded, 16 * 6 * (run + 1))
            wait_alone(dve, hd_zeroed, run + 1)
            def batch(g, final):
                def shift(u):
                    st = hd_st[u % 2]
                    dve.wait_ge(hd_scores, nth(g, PAIRS8, u))
                    dve.tensor_reduce(st[:, 0:4], PS[:, (u % 2) * 2:(u % 2) * 2 + 2, :]
                                      .rearrange("p h (t q) -> p (h t) q", t=2), AX_X, ALU.max).then_inc(hd_max, 1)
                    dve.wait_ge(hd_max, nth(g, PAIRS8, u))
                    dve.tensor_scalar(st[:, 4:8], st[:, 0:4], -MIX_SCALE, None, ALU.mult).then_inc(hd_bias, 1)

                def values(u):
                    st = hd_st[u % 2]
                    grp, v = divmod(2 * u, HEADS_IN_GROUP)
                    dve.wait_ge(hd_exp, nth(g, PAIRS8, u))
                    dve.reciprocal(st[:, 12:16], st[:, 8:12]).then_inc(hd_recip, 1)
                    dve.wait_ge(hd_recip, nth(g, PAIRS8, u))
                    if u == 0:
                        dve.wait_ge(hd_projected, (g + 1) * 3)
                    dve.wait_ge(hd_out, g * PAIRS8)
                    at = grp * VGROUP + v * 40
                    to = hd_vm[:, :, at:at + 80].rearrange("p t (h x) -> p t h x", h=2)[:, :, :, 0:8]
                    fr = hd_v[:, :, u * 16:(u + 1) * 16].rearrange("p t (h x) -> p t h x", h=2)
                    rc = st[:, 12:16].rearrange("p (h t o) -> p t h o", h=2, o=1).broadcast_to([P, 2, 2, 8])
                    dve.tensor_tensor(to, fr, rc, ALU.mult).then_inc(hd_v_ready, 1)
                shift(0)
                for u in range(PAIRS8):
                    if u + 1 < PAIRS8:
                        shift(u + 1)
                    values(u)
                if not final:
                    mask_vector(dve, g + 1, hd_k, 2)
            mask_vector(dve, run * B + 1, hd_k, 2)
            with dve.Fori(0, B - 1) as b:
                batch(run * B + b + 1, False)
            batch(run * B + B, True)
            for k in range(2):
                n = 2 * call + k
                for c in range(NCH):
                    dve.wait_ge(tail_sum, nth(n, NCH, c))
                    dve.tensor_scalar(chunk(hd_rn, c), PS[:, 4 + c, :], 1e-24 / C, None, ALU.max).then_inc(tail_floor, 1)
                for c in range(NCH):
                    dve.wait_ge(tail_rn, nth(n, NCH, c))
                    dve.tensor_tensor(chunk(hd_Z, c), PS[:, c, :], chunk(hd_rn, c), ALU.mult).then_inc(tail_z, 1)
            for c in range(NCH):
                dve.wait_ge(tail_gelu, nth(call, NCH, c))
                dve.tensor_tensor(chunk(XO, c), chunk(XO, c), chunk(hd_y, c), ALU.add)

        b1 = Space(hd.at)
        b1_ks = b1.take(3 * P)
        b1_mask = b1.take(2 * P)
        BLOCKS = 3 * P
        b1_s = [b1.take(2 * BLOCKS).rearrange("p (h j) -> p h j", h=2) for _ in range(2)]
        b1_e = [b1.take(2 * BLOCKS).rearrange("p (h j) -> p h j", h=2) for _ in range(2)]
        b1_t = [b1.take(2 * BLOCKS).rearrange("p (h j) -> p h j", h=2) for _ in range(2)]
        b1_added = sem("b1_added")
        b1_max = sem("b1_max")
        b1_sum = sem("b1_sum")
        b1_probs = sem("b1_probs")
        b1_turned = sem("b1_turned")
        b1_copied = sem("b1_copied")
        b1_lin = sem("b1_lin")
        B1_SCALE = float(1.0 / np.sqrt(8.0))
        ROW_BLOCKS = ((0, P), (P, BLOCKS))

        def b1_sync(sp):
            for k, name in enumerate(("wq", "wk", "wv", "wo")):
                sp.dma_start(hd_w[k], d[f"b1_{name}"]).then_inc(hd_loaded, 16)
            sp.dma_start(hd_only, d["c_only"]).then_inc(hd_loaded, 16)
            sp.dma_start(b1_mask, d["c_causal"]).then_inc(hd_loaded, 16)

        def b1_tensor(pe, run, n0):
            ln_tensor(pe, n0, XO)
            wait_alone(pe, hd_loaded, 16 * 6 * (run + 1))
            def project(g):
                pe.wait_ge(hd_entered, g + 1)
                for k in range(2):
                    last = pe.matmul(PS[:, 7, k * T:(k + 1) * T], hd_w[k], hd_x, start=True, stop=True)
                last.then_inc(hd_proj, 1)

            def batch(g, b, final):
                def scores(u):
                    if u >= 2:
                        wait_alone(pe, b1_added, nth(b, 2 * PAIRS8, 2 * (u - 2) + 1))
                    for s in range(2):
                        grp, v = divmod(2 * u + s, HEADS_IN_GROUP)
                        rows = slice(grp * GROUP, (grp + 1) * GROUP)
                        bank = (u % 2) * 2 + s
                        pe.matmul(PS[:, bank, 0:P], hd_m[v][rows, 0:P], b1_ks[rows, 0:P], start=True, stop=True)
                        last = pe.matmul(PS[:, bank, P:BLOCKS], hd_m[v][rows, P:T], b1_ks[rows, P:BLOCKS],
                                         start=True, stop=True)
                    last.then_inc(hd_scores, 1)

                def turn(u):
                    if u >= 1:
                        pe.wait_ge(b1_copied, nth(b, PAIRS8, u - 1))
                    pe.wait_ge(b1_probs, nth(b, PAIRS8, u))
                    for s in range(2):
                        for k, at in enumerate((0, 2, 1)):
                            last = pe.transpose(PS[:, 4 + s, at * P:(at + 1) * P],
                                                b1_e[u % 2][:, s, k * P:(k + 1) * P], ident[:])
                    last.then_inc(b1_turned, 1)

                def heads(u):
                    pe.wait_ge(b1_copied, nth(b, PAIRS8, u))
                    if u == 0:
                        pe.wait_ge(hd_v_ready, (g + 1) * PAIRS8)
                    for s in range(2):
                        grp, v = divmod(2 * u + s, HEADS_IN_GROUP)
                        rows = slice(grp * GROUP, (grp + 1) * GROUP)
                        at = grp * VGROUP + v * GROUP
                        turned_probs = b1_t[u % 2][:, s, :]
                        pe.matmul(PS[rows, 6, 0:T], hd_vm[:, 0, at:at + GROUP], turned_probs[:, 0:T],
                                  start=(v == 0), stop=False, skip_group_check=True)
                        last = pe.matmul(PS[rows, 6, P:T], hd_vm[:, 1, at:at + GROUP], turned_probs[:, T:BLOCKS],
                                         start=False, stop=(v == HEADS_IN_GROUP - 1), skip_group_check=True)
                    last.then_inc(hd_out, 1)
                wait_alone(pe, hd_masked, (g + 1) * HEADS_IN_GROUP)
                wait_alone(pe, hd_projected, g * 3 + 2)
                for t in range(2):
                    last = pe.matmul(PS[:, 7, t * C:(t + 1) * C], hd_x[:, t * P:(t + 1) * P], hd_w[2], start=True, stop=True)
                last.then_inc(hd_proj, 1)
                scores(0)
                scores(1)
                for u in range(PAIRS8):
                    if u + 2 < PAIRS8:
                        scores(u + 2)
                    turn(u)
                    if u > 0:
                        heads(u - 1)
                    if u == PAIRS8 - 3 and not final:
                        project(g + 1)
                heads(PAIRS8 - 1)
            project(run * B + 1)
            with pe.Fori(0, B - 1) as b:
                batch(run * B + b + 1, b, False)
            batch(run * B + B, B - 1, True)
            pe.wait_ge(hd_copied, (run + 1) * B + 1)
            for c in range(NCH):
                pe.matmul(PS[:, c, :], hd_w[3], chunk(hd_Z, c), start=True, stop=True).then_inc(b1_lin, 1)

        def b1_scalar(act, run, n0):
            ln_scalar(act, n0)
            wait_alone(act, ln_scaled, (n0 + 1) * NCH)
            def enter(g, b):
                act.wait_ge(hd_proj, g * 2)
                act.activation(hd_x, XN[:, ds(b * T, T)], ACT.Copy).then_inc(hd_entered, 1)

            def copy_projected(g):
                act.wait_ge(hd_proj, g * 2 + 1)
                act.wait_ge(hd_scores, g * PAIRS8)
                act.activation(b1_ks[:, 0:T], PS[:, 7, T:2 * T], ACT.Copy)
                act.activation(b1_ks[:, T:T + P], PS[:, 7, T:T + P], ACT.Copy).then_inc(hd_projected, 1)
                act.wait_ge(hd_masked, g * HEADS_IN_GROUP)
                act.activation(hd_q, PS[:, 7, 0:T], ACT.Copy).then_inc(hd_projected, 1)

            def batch(g, b, final):
                act.wait_ge(hd_proj, g * 2 + 2)
                act.wait_ge(hd_v_ready, g * PAIRS8)
                act.activation(hd_v, PS[:, 7, 0:2 * C].rearrange("p (t n) -> p t n", t=2), ACT.Copy)\
                   .then_inc(hd_projected, 1)
                if not final:
                    enter(g + 1, b + 1)

                def copy(u):
                    act.wait_ge(b1_turned, nth(b, PAIRS8, u))
                    if u >= 2:
                        act.wait_ge(hd_out, nth(g, PAIRS8, u - 2))
                    act.activation(b1_t[u % 2], PS[:, 4:6, 0:BLOCKS], ACT.Copy).then_inc(b1_copied, 1)
                for u in range(PAIRS8):
                    act.wait_ge(hd_bias, nth(g, PAIRS8, u))
                    if u >= 2:
                        act.wait_ge(b1_turned, nth(b, PAIRS8, u - 2))
                    for s in range(2):
                        for t, (lo, hi) in enumerate(ROW_BLOCKS):
                            st = hd_st[u % 2]
                            last = act.activation(b1_e[u % 2][:, s, lo:hi], b1_s[u % 2][:, s, lo:hi], ACT.Exp,
                                                  bias=st[:, 4 + 2 * t + s:5 + 2 * t + s], scale=B1_SCALE,
                                                  accum_out=st[:, 8 + 2 * t + s:9 + 2 * t + s])
                    last.then_inc(hd_exp, 1)
                    if u > 0:
                        copy(u - 1)
                if not final:
                    copy_projected(g + 1)
                copy(PAIRS8 - 1)
                act.wait_ge(hd_out, (g + 1) * PAIRS8)
                act.activation(hd_Z[:, ds(b * T, T)], PS[:, 6, 0:T], ACT.Copy).then_inc(hd_copied, 1)
            enter(run * B + 1, 0)
            copy_projected(run * B + 1)
            with act.Fori(0, B - 1) as b:
                batch(run * B + b + 1, b, False)
            batch(run * B + B, B - 1, True)

        def b1_vector(dve, run, n0):
            ln_vector(dve, n0, XO, XN)
            dve.memset(hd_vm, 0.0).then_inc(hd_zeroed, 1)
            wait_alone(dve, hd_loaded, 16 * 6 * (run + 1))
            wait_alone(dve, hd_zeroed, run + 1)
            def mask(g):
                dve.wait_ge(hd_projected, g * 3 + 2)
                dve.wait_ge(hd_scores, g * PAIRS8)
                for v in range(HEADS_IN_GROUP):
                    dve.tensor_scalar(hd_m[v], hd_q, hd_only[:, v:v + 1], None, ALU.mult).then_inc(hd_masked, 1)

            def batch(g, b, final):
                dve.wait_ge(hd_projected, g * 3 + 3)
                dve.wait_ge(hd_out, g * PAIRS8)
                for t in range(2):
                    to = hd_vm[:, t, :].rearrange("p (h x) -> p h x", x=40)[:, :, 0:8]
                    last = dve.tensor_copy(to, hd_v[:, t, :].rearrange("p (h x) -> p h x", x=8))
                last.then_inc(hd_v_ready, PAIRS8)

                def shift(u):
                    st, S = hd_st[u % 2], b1_s[u % 2]
                    dve.wait_ge(hd_scores, nth(g, PAIRS8, u))
                    if u >= 2:
                        dve.wait_ge(hd_exp, nth(g, PAIRS8, u - 2))
                    banks = PS[:, (u % 2) * 2:(u % 2) * 2 + 2, :]
                    mask = b1_mask.rearrange("p (o j) -> p o j", o=1).broadcast_to([P, 2, 2 * P])
                    dve.tensor_copy(S[:, :, 2 * P:BLOCKS], banks[:, :, 2 * P:BLOCKS]).then_inc(b1_added, 1)
                    dve.tensor_tensor(S[:, :, 0:2 * P], banks[:, :, 0:2 * P], mask, ALU.add).then_inc(b1_added, 1)
                    dve.wait_ge(b1_added, nth(b, 2 * PAIRS8, 2 * u + 1))
                    for t, (lo, hi) in enumerate(ROW_BLOCKS):
                        dve.tensor_reduce(st[:, 2 * t:2 * t + 2], S[:, :, lo:hi], AX_X, ALU.max)\
                           .then_inc(hd_max if t else b1_max, 1)
                    dve.wait_ge(b1_max, nth(b, PAIRS8, u))
                    dve.wait_ge(hd_max, nth(g, PAIRS8, u))
                    dve.tensor_scalar(st[:, 4:8], st[:, 0:4], -B1_SCALE, None, ALU.mult).then_inc(hd_bias, 1)

                def normalise(u):
                    st, e = hd_st[u % 2], b1_e[u % 2]
                    dve.wait_ge(hd_exp, nth(g, PAIRS8, u))
                    dve.tensor_scalar(st[:, 12:16], st[:, 8:12], 1e-8, None, ALU.add).then_inc(b1_sum, 1)
                    dve.wait_ge(b1_sum, nth(b, PAIRS8, u))
                    dve.reciprocal(st[:, 12:16], st[:, 12:16]).then_inc(hd_recip, 1)
                    dve.wait_ge(hd_recip, nth(g, PAIRS8, u))
                    for s in range(2):
                        for t, (lo, hi) in enumerate(ROW_BLOCKS):
                            last = dve.tensor_scalar(e[:, s, lo:hi], e[:, s, lo:hi], st[:, 12 + 2 * t + s:13 + 2 * t + s],
                                                     None, ALU.mult)
                    last.then_inc(b1_probs, 1)
                shift(0)
                for u in range(PAIRS8):
                    if u + 1 < PAIRS8:
                        shift(u + 1)
                    normalise(u)
                if not final:
                    mask(g + 1)
            mask(run * B + 1)
            with dve.Fori(0, B - 1) as b:
                batch(run * B + b + 1, b, False)
            batch(run * B + B, B - 1, True)
            for c in range(NCH):
                dve.wait_ge(b1_lin, c + 1)
                dve.tensor_tensor(chunk(XO, c), chunk(XO, c), PS[:, c, :], ALU.add)

        BR, BH = 4, 16
        UNITS = BH
        QUAD = 4
        QUADS = UNITS // QUAD
        STAGES = UNITS // 2
        SIG = float(np.pi / np.sqrt(3.0))
        b0 = Space(0)
        b0_wq = b0.take(2 * BR * C)
        b0_wk = b0.take(2 * C)
        b0_wv = b0.take(BR * C)
        b0_wo = b0.take(C)
        b0_vec = b0.take(16)
        b0_bv = b0.take(BR * C)
        b0_ones8 = b0.take(P)
        b0_only = b0.take(BH)
        b0_tab = b0.take(2 * T).rearrange("p (k t) -> p k t", k=2)
        b0_tri = b0.take(P)
        b0_sink = b0.take(2 * BR * BH)
        b0_null = b0.take(BR * C)
        b0_Q = b0.take(BR * N).rearrange("p (r t) -> p r t", r=BR)
        b0_K = b0.take(N)
        b0_V = b0.take(2 * B * BR * BH * 9).rearrange("p (t h e) -> p t h e", h=BR * BH, e=9)
        b0_KM = [b0.take(T) for _ in range(2 * QUAD)]
        b0_m = [b0.take(3 * CH) for _ in range(2)]
        b0_w = b0.take(8 * 3 * CH).rearrange("p (u j) -> p u j", u=8)
        b0_sg = [b0.take(3 * CH) for _ in range(2)]
        b0_den = b0.take(2 * QUAD * BR)
        b0_ctx = b0.take(2 * QUAD * BR * 8)
        b0_tmp = b0_sg[0]
        b0_rk = b0_w.rearrange("p u j -> p (u j)")[:, 0:N]
        b0_sq = b0_w.rearrange("p u j -> p (u j)")[:, N:2 * N]
        b0_ct = b0_Q.rearrange("p r t -> p (r t)")[:, 0:N]
        CT = XN[:].rearrange("p (t f) -> p t f", f=C)
        b0_loaded = sem("b0_loaded")
        b0_ones = sem("b0_ones")
        b0_tanh = sem("b0_tanh")
        b0_sinks = sem("b0_sinks")
        b0_proj = sem("b0_proj")
        b0_freed = sem("b0_freed")
        b0_roped = sem("b0_roped")
        b0_ksq = sem("b0_ksq")
        b0_self = sem("b0_self")
        b0_floor = sem("b0_floor")
        b0_log = sem("b0_log")
        b0_rk_ready = sem("b0_rk_ready")
        b0_kn = sem("b0_kn")
        b0_km = sem("b0_km")
        b0_scores = sem("b0_scores")
        b0_min = sem("b0_min")
        b0_e = sem("b0_e")
        b0_l = sem("b0_l")
        b0_soft = sem("b0_soft")
        b0_sigm = sem("b0_sigm")
        b0_masked = sem("b0_masked")
        b0_weight = sem("b0_weight")
        b0_out = sem("b0_out")
        b0_ctx_step = sem("b0_ctx_step")
        b0_done = sem("b0_done")
        b0_ct_turned = sem("b0_ct_turned")
        b0_ct_copied = sem("b0_ct_copied")
        b0_lin = sem("b0_lin")
        b0_x = sem("b0_x")
        PAIRS_QK = BR + 1
        ITEMS = 2 * PAIRS_QK + 4

        def b0_sync(sp):
            loads = [(b0_wq, "b0_Wq"), (b0_wk, "b0_Wk"), (b0_wv, "b0_Wv"), (b0_wo, "L0_attn_b_Wo"),
                     (b0_vec, "b0_vectors"), (b0_ones8, "c_ones8"), (b0_only, "c_only16"), (b0_tri, "c_tri"),
                     (b0_tab.rearrange("p k t -> p (k t)"), "c_rope")]
            for to, name in loads:
                sp.dma_start(to, d[name]).then_inc(b0_loaded, 16)
            for to, name in ((b0_bv, "b0_bv"), (b0_sink[:, 0:BR * BH], "b0_sinks"), (b0_null, "b0_nulls")):
                sp.dma_start(to, d[name].broadcast_to([P, to.shape[1]])).then_inc(b0_loaded, 16)
        B0_LOADS = 16 * 12

        def b0_tensor(pe, n0):
            ln_tensor(pe, n0, XO)
            pe.wait_ge(b0_loaded, B0_LOADS)
            pe.wait_ge(ln_scaled, (n0 + 1) * NCH)
            for c in range(NCH):
                for i in range(ITEMS):
                    n = ITEMS * c + i
                    if n >= 8:
                        pe.wait_ge(b0_freed, n - 7)
                    if i < 2 * PAIRS_QK:
                        w = b0_wq[:, i * C:(i + 1) * C] if i < 2 * BR else b0_wk[:, (i - 2 * BR) * C:(i - 2 * BR + 1) * C]
                        pe.matmul(PS[:, n % 8, :], w, chunk(XN, c), start=True, stop=True).then_inc(b0_proj, 1)
                    else:
                        t = 4 * c + i - 2 * PAIRS_QK
                        pe.matmul(PS[:, n % 8, :], XN[:, t * P:(t + 1) * P], b0_wv, start=True, stop=True)\
                          .then_inc(b0_proj, 1)
            pe.wait_ge(b0_freed, ITEMS * NCH)
            for c in range(NCH):
                pe.wait_ge(b0_ksq, c + 1)
                pe.matmul(PS[:, c, :], b0_ones8, chunk(b0_sq, c), start=True, stop=True).then_inc(b0_self, 1)
            wait_alone(pe, b0_kn, NCH)

            def scores(b, u):
                if u % QUAD == 0:
                    wait_alone(pe, b0_km, nth(b, QUADS, u // QUAD))
                at = b * T + (u // UNITS) * T
                wait_alone(pe, b0_soft, nth(b, UNITS, u - 2) + 2)
                for k, (kt, qt) in enumerate(((0, 0), (1, 1), (0, 1))):
                    last = pe.matmul(PS[:, (u % 2) * 3 + k, :], b0_KM[u % (2 * QUAD)][:, kt * P:(kt + 1) * P],
                                     b0_Q[:, :, ds(at + qt * P, P)], start=True, stop=True)
                last.then_inc(b0_scores, 1)

            def heads(b, u):
                quad, v = divmod(u, QUAD)
                if v == 0:
                    wait_alone(pe, b0_done, nth(b, QUADS, quad - 2) + 2)
                pe.wait_ge(b0_weight, nth(b, UNITS, u) + 2)
                w = b0_w[:, u % 8, :]
                for r in range(BR):
                    h = u * BR + r
                    block = lambda k: w[:, k * CH + r * P:k * CH + (r + 1) * P]
                    o = lambda qt: PS[:, 6 + quad % 2, ((qt * QUAD + v) * BR + r) * 9:
                                      ((qt * QUAD + v) * BR + r) * 9 + 9]
                    value = lambda kt: b0_V[:, ds(b * 2 + kt, 1), h, :].rearrange("p o e -> p (o e)")
                    pe.matmul(o(0), block(0), value(0), start=True, stop=True)
                    pe.matmul(o(1), block(2), value(0), start=True, stop=False)
                    last = pe.matmul(o(1), block(1), value(1), start=False, stop=True)
                last.then_inc(b0_out, 1)

            def batch(b, final):
                for n in range(STAGES):
                    if not (final and n + 2 >= STAGES):
                        scores(b, 2 * n + 4)
                        scores(b, 2 * n + 5)
                    heads(b, 2 * n)
                    heads(b, 2 * n + 1)
            for u in range(4):
                scores(0, u)
            with pe.Fori(0, B - 1) as b:
                batch(b, False)
            batch(B - 1, True)
            pe.wait_ge(b0_done, QUADS * B + 2)
            for c in range(NCH):
                for j in range(4):
                    last = pe.transpose(PS[:, c, j * P:(j + 1) * P], CT[:, 4 * c + j, :], ident[:])
                last.then_inc(b0_ct_turned, 1)
            for c in range(NCH):
                pe.wait_ge(b0_ct_copied, c + 1)
                pe.matmul(PS[:, 4 + c, :], b0_wo, chunk(b0_ct, c), start=True, stop=True).then_inc(b0_lin, 1)

        def b0_scalar(act, n0):
            ln_scalar(act, n0)
            act.wait_ge(b0_loaded, B0_LOADS)
            act.activation(b0_sink[:, 0:BR * BH], b0_sink[:, 0:BR * BH], ACT.Tanh).then_inc(b0_tanh, 1)
            log_exp_tables(act)
            for c in range(NCH):
                act.wait_ge(b0_roped, PAIRS_QK * (c + 1))
                act.activation(chunk(b0_sq, c), chunk(b0_K, c), ACT.Square).then_inc(b0_ksq, 1)
            for c in range(NCH):
                act.wait_ge(b0_floor, c + 1)
                act.activation(chunk(b0_rk, c), chunk(b0_rk, c), ACT.Ln).then_inc(b0_log, 1)
                act.wait_ge(b0_log, c + 1)
                act.activation(chunk(b0_rk, c), chunk(b0_rk, c), ACT.Exp, scale=-0.5).then_inc(b0_rk_ready, 1)

            def soft(b, n):
                log_exp_tables(act)
                for u in (2 * n, 2 * n + 1):
                    act.wait_ge(b0_min, nth(b, UNITS, u))
                    act.activation(b0_m[u % 2], b0_m[u % 2], ACT.Exp).then_inc(b0_e, 1)
                    act.wait_ge(b0_e, nth(b, UNITS, u))
                    act.activation(b0_m[u % 2], b0_m[u % 2], ACT.Ln, bias=1.0).then_inc(b0_l, 1)

            def sigmoid(b, n):
                for u in (2 * n, 2 * n + 1):
                    act.wait_ge(b0_soft, nth(b, UNITS, u) + 2)
                    act.wait_ge(b0_weight, nth(b, UNITS, u - 2) + 2)
                    act.activation(b0_sg[u % 2], b0_w[:, u % 8, :], ACT.Sigmoid, scale=SIG).then_inc(b0_sigm, 1)

            def batch(b, final):
                for n in range(STAGES):
                    if not (final and n + 1 >= STAGES):
                        sigmoid(b, n + 1)
                    if not (final and n + 2 >= STAGES):
                        soft(b, n + 2)
            soft(0, 0)
            sigmoid(0, 0)
            soft(0, 1)
            with act.Fori(0, B - 1) as b:
                batch(b, False)
            batch(B - 1, True)
            for c in range(NCH):
                act.wait_ge(b0_ct_turned, c + 1)
                act.activation(chunk(b0_ct, c), PS[:, c, :], ACT.Copy).then_inc(b0_ct_copied, 1)

        def b0_vector(dve, n0):
            ln_vector(dve, n0, XO, XN)
            dve.wait_ge(b0_tanh, 1)
            dve.tensor_scalar(b0_sink[:, 0:BR * BH], b0_sink[:, 0:BR * BH], 1e-6, None, ALU.add).then_inc(b0_sinks, 1)
            dve.wait_ge(b0_sinks, 1)
            dve.tensor_scalar(b0_sink[:, BR * BH:], b0_sink[:, 0:BR * BH], 1e-6, None, ALU.add).then_inc(b0_sinks, 1)
            null3 = b0_null.rearrange("p (h e) -> p h e", e=8)
            sink3 = b0_sink[:, 0:BR * BH].rearrange("p (h o) -> p h o", o=1)
            dve.tensor_tensor(null3, null3, sink3.broadcast_to([P, BR * BH, 8]), ALU.mult).then_inc(b0_sinks, 1)
            for c in range(NCH):
                for j in range(PAIRS_QK):
                    n = ITEMS * c + 2 * j
                    to = chunk(b0_Q[:, j, :], c) if j < BR else chunk(b0_K, c)
                    tmp = b0_tmp[:, 0:CH]
                    m = PAIRS_QK * c + j
                    for k, half in enumerate((to, tmp)):
                        dve.wait_ge(b0_proj, n + k + 1)
                        if k == 1 and m > 0:
                            dve.wait_ge(b0_roped, m)
                        h3 = lambda a: a.rearrange("p (b t) -> p b t", t=T)
                        dve.scalar_tensor_tensor(h3(half), h3(PS[:, (n + k) % 8, :]), b0_vec[:, 2 * j + k:2 * j + k + 1],
                                                 b0_tab[:, k:k + 1, :].broadcast_to([P, CH // T, T]),
                                                 ALU.add, ALU.mult).then_inc(b0_freed, 1)
                    dve.wait_ge(b0_freed, n + 2)
                    dve.tensor_tensor(to, to, tmp, ALU.add).then_inc(b0_roped, 1)
                for j in range(4):
                    n = ITEMS * c + 2 * PAIRS_QK + j
                    dve.wait_ge(b0_proj, n + 1)
                    if n == 2 * PAIRS_QK:
                        dve.wait_ge(b0_ones, 1)
                    dve.tensor_tensor(b0_V[:, 4 * c + j, :, 0:8], PS[:, n % 8, :].rearrange("p (h e) -> p h e", e=8),
                                      b0_bv.rearrange("p (h e) -> p h e", e=8), ALU.add).then_inc(b0_freed, 1)
            for c in range(NCH):
                dve.wait_ge(b0_self, c + 1)
                dve.tensor_scalar(chunk(b0_rk, c), PS[:, c, :], 1e-6, None, ALU.max).then_inc(b0_floor, 1)
            for c in range(NCH):
                dve.wait_ge(b0_rk_ready, c + 1)
                dve.scalar_tensor_tensor(chunk(b0_K, c), chunk(b0_K, c), float(8 ** -0.5), chunk(b0_rk, c),
                                         ALU.mult, ALU.mult).then_inc(b0_kn, 1)
            wait_alone(dve, b0_kn, NCH)

            def masked_keys(b, quad):
                at = b * T + (quad // QUADS) * T
                dve.wait_ge(b0_scores, nth(b, UNITS, (quad - 1) * QUAD - 1) + UNITS)
                for v in range(QUAD):
                    u = quad * QUAD + v
                    last = dve.tensor_scalar(b0_KM[u % (2 * QUAD)], b0_K[:, ds(at, T)],
                                             b0_only[:, u % UNITS:u % UNITS + 1], None, ALU.mult)
                last.then_inc(b0_km, 1)

            def clamp(b, u):
                S = PS[:, (u % 2) * 3:(u % 2) * 3 + 3, :].rearrange("p k j -> p (k j)")
                dve.wait_ge(b0_scores, nth(b, UNITS, u) + UNITS)
                dve.wait_ge(b0_soft, nth(b, UNITS, u - 2) + 2)
                dve.tensor_scalar(b0_m[u % 2], S, 40.0, None, ALU.min).then_inc(b0_min, 1)

            def larger(b, u):
                S = PS[:, (u % 2) * 3:(u % 2) * 3 + 3, :].rearrange("p k j -> p (k j)")
                dve.wait_ge(b0_l, nth(b, UNITS, u))
                dve.wait_ge(b0_out, nth(b, UNITS, u - 8) + 8)
                dve.tensor_tensor(b0_w[:, u % 8, :], b0_m[u % 2], S, ALU.max).then_inc(b0_soft, 1)

            def weigh(b, u):
                w = b0_w[:, u % 8, :]
                dve.wait_ge(b0_masked, nth(b, UNITS, u))
                dve.tensor_tensor(w, w, b0_sg[u % 2], ALU.mult).then_inc(b0_weight, 1)

            def context(b, quad):
                step = nth(b, 5 * QUADS, 5 * quad)
                dve.wait_ge(b0_out, nth(b, UNITS, quad * QUAD + QUAD - 1) + 8)
                O = PS[:, 6 + quad % 2, 0:2 * QUAD * BR * 9].rearrange("p (q h e) -> p q h e", q=2, e=9)
                HB = QUAD * BR
                heads_of = slice(quad * HB, (quad + 1) * HB)
                den = b0_den.rearrange("p (q h) -> p q h", q=2)
                sinks = b0_sink[:, BR * BH:][:, heads_of].rearrange("p (o h) -> p o h", o=1).broadcast_to([P, 2, HB])
                dve.tensor_tensor(den, O[:, :, :, 8:9].rearrange("p q h o -> p q (h o)"), sinks, ALU.add)\
                   .then_inc(b0_ctx_step, 1)
                nulls = b0_null[:, quad * HB * 8:(quad + 1) * HB * 8]
                X = b0_ctx.rearrange("p (q h e) -> p q h e", q=2, e=8)
                for q in range(2):
                    dve.tensor_tensor(X[:, q, :, :], O[:, q, :, 0:8], nulls.rearrange("p (h e) -> p h e", e=8), ALU.add)\
                       .then_inc(b0_ctx_step, 1)
                dve.wait_ge(b0_ctx_step, step)
                dve.reciprocal(b0_den, b0_den).then_inc(b0_ctx_step, 1)
                dve.wait_ge(b0_ctx_step, step + 3)
                X2 = b0_ctx.rearrange("p (h e) -> p h e", e=8)
                alpha = b0_den.rearrange("p (h o) -> p h o", o=1).broadcast_to([P, 2 * HB, 8])
                dve.tensor_tensor(X2, X2, alpha, ALU.mult).then_inc(b0_ctx_step, 1)
                dve.wait_ge(b0_ctx_step, step + 4)
                for q in range(2):
                    to = CT[:, ds(b * 2 + q, 1), quad * 32:(quad + 1) * 32].rearrange("p o f -> p (o f)")
                    fr = b0_ctx[:, q * HB * 8:(q + 1) * HB * 8].rearrange("p (h r e) -> p h e r", r=BR, e=8)
                    last = dve.tensor_reduce(to.rearrange("p (h e) -> p h e", e=8), fr, AX_X, ALU.add)
                last.then_inc(b0_done, 1)

            def stage(b, n, ahead, keys=None, done=None):
                weigh(b, 2 * n)
                weigh(b, 2 * n + 1)
                if keys is not None:
                    masked_keys(b, keys)
                if done is not None:
                    context(b, done)
                if ahead:
                    clamp(b, 2 * n + 4)
                    clamp(b, 2 * n + 5)
                    larger(b, 2 * n + 4)
                    larger(b, 2 * n + 5)

            def batch(b, final):
                for n in range(1, STAGES if final else STAGES + 1):
                    stage(b, n, not (final and n + 2 >= STAGES), (n + 3) // 2 if n % 2 == 1 and not (final and n + 3 >= STAGES) else None,
                          n // 2 - 1 if n % 2 == 0 else None)
                if final:
                    context(b, QUADS - 1)
            masked_keys(0, 0)
            for u in range(4):
                clamp(0, u)
                larger(0, u)
            masked_keys(0, 1)
            stage(0, 0, True)
            with dve.Fori(0, B - 1) as b:
                batch(b, False)
            batch(B - 1, True)
            for c in range(NCH):
                dve.tensor_scalar(chunk(XO, c), chunk(XO, c), b0_vec[:, 10:11], None, ALU.add).then_inc(b0_x, 1)
            for c in range(NCH):
                dve.wait_ge(b0_lin, c + 1)
                dve.wait_ge(b0_x, c + 1)
                dve.scalar_tensor_tensor(chunk(XO, c), PS[:, 4 + c, :], 1.0 / BR, chunk(XO, c), ALU.mult, ALU.add)

        def b0_gpsimd(pool):
            pool.memset(b0_V, 1.0).then_inc(b0_ones, 1)
            wait_alone(pool, b0_loaded, B0_LOADS)

            def mask(b, u):
                wait_alone(pool, b0_sigm, nth(b, UNITS, u))
                s3 = b0_sg[u % 2][:, 0:2 * CH].rearrange("p (r j) -> p r j", j=P)
                tri = b0_tri.rearrange("p (o j) -> p o j", o=1).broadcast_to([P, 2 * BR, P])
                pool.tensor_tensor(s3, s3, tri, ALU.mult).then_inc(b0_masked, 1)
            with pool.Fori(0, B) as b:
                for u in range(UNITS):
                    mask(b, u)

        block = ctx.enter_context(nc.Block())

        K, n0, run, plan, calls = 1, 0, 0, [], {"ffn": 0, "mix": 0}
        for part in parts:
            kind = part[:-1]
            plan.append((kind + part[-1] if kind in ("attn_a", "attn_b") else kind, K, n0, calls.get(kind, 0), run))
            run += part in ("mix0", "mix1", "attn_b1")
            if kind in calls:
                calls[kind] += 1
            K += 2 + 2 * DEPTH if kind == "ffn" else 1
            n0 += 1 + DEPTH if kind == "ffn" else 1

        @block.sync
        def _(sp):
            load_sync(sp)
            for part, K, n0, call, run in plan:
                sp.wait_ge(phase_end, 4 * K)
                if part == "attn_a0":
                    a0_sync(sp)
                if part == "ffn":
                    ffn_sync(sp, call, K)
                if part == "attn_b0":
                    b0_sync(sp)
                if part == "attn_a1":
                    a1_sync(sp)
                if part == "mix":
                    mix_sync(sp)
                if part == "attn_b1":
                    b1_sync(sp)
            store_sync(sp)

        @block.tensor
        def _(pe):
            load_tensor(pe)
            meet(pe, 1)
            for part, K, n0, call, run in plan:
                if part == "attn_a0":
                    a0_tensor(pe, n0)
                if part == "ffn":
                    ffn_tensor(pe, call, K, n0)
                    K += 1 + 2 * DEPTH
                if part == "attn_b0":
                    b0_tensor(pe, n0)
                if part == "attn_a1":
                    a1_tensor(pe, n0)
                if part == "mix":
                    mix_tensor(pe, run, call, n0)
                if part == "attn_b1":
                    b1_tensor(pe, run, n0)
                meet(pe, K + 1)
            store_tensor(pe)

        @block.scalar
        def _(act):
            act.sem_inc(qkv_copied, 2)
            act.sem_inc(turned_copied, 2)
            act.sem_inc(o_copied, 2)
            act.sem_inc(b0_scores, UNITS)
            act.sem_inc(b0_out, 8)
            act.sem_inc(scan_norm, 4)
            for semaphore, of_batch in ((hd_entered, 1), (hd_proj, 2), (hd_projected, 3), (hd_scores, PAIRS8),
                                        (hd_exp, PAIRS8), (hd_out, PAIRS8), (hd_copied, 1)):
                act.sem_inc(semaphore, of_batch)
            load_scalar(act)
            meet(act, 1)
            for part, K, n0, call, run in plan:
                if part == "attn_a0":
                    a0_scalar(act, n0)
                if part == "ffn":
                    ffn_scalar(act, call, K, n0)
                    K += 1 + 2 * DEPTH
                if part == "attn_b0":
                    b0_scalar(act, n0)
                if part == "attn_a1":
                    a1_scalar(act, n0)
                if part == "mix":
                    mix_scalar(act, run, call, n0)
                if part == "attn_b1":
                    b1_scalar(act, run, n0)
                meet(act, K + 1)
            store_scalar(act)

        @block.vector
        def _(dve):
            dve.sem_inc(scores_read, 2)
            dve.sem_inc(b0_soft, 2)
            dve.sem_inc(b0_weight, 2)
            dve.sem_inc(b0_done, 2)
            dve.sem_inc(t1_ready, 3)
            dve.sem_inc(t2_ready, 3)
            dve.sem_inc(norm2_own, 1)
            for semaphore, of_batch in ((hd_masked, HEADS_IN_GROUP), (hd_max, PAIRS8), (hd_bias, PAIRS8),
                                        (hd_recip, PAIRS8), (hd_v_ready, PAIRS8)):
                dve.sem_inc(semaphore, of_batch)
            dve.sem_inc(stream_added, 1)
            meet(dve, 1)
            for part, K, n0, call, run in plan:
                if part == "attn_a0":
                    a0_vector(dve, n0)
                if part == "ffn":
                    ffn_vector(dve, call, K, n0)
                    K += 1 + 2 * DEPTH
                if part == "attn_b0":
                    b0_vector(dve, n0)
                if part == "attn_a1":
                    a1_vector(dve, n0)
                if part == "mix":
                    mix_vector(dve, run, call, n0)
                if part == "attn_b1":
                    b1_vector(dve, run, n0)
                meet(dve, K + 1)

        @block.gpsimd
        def _(pool):
            meet(pool, 1)
            for part, K, n0, call, run in plan:
                if part == "ffn":
                    ffn_gpsimd(pool, call, K, n0)
                    K += 1 + 2 * DEPTH
                if part == "attn_b0":
                    b0_gpsimd(pool)
                meet(pool, K + 1)


def laid_out(inputs):
    a = {k: np.asarray(v) for k, v in inputs.items()}
    d = {k: a[k] for k in ("L0_attn_a_x", "L0_ffn_Wqkv", "L0_ffn_Wo", "L0_ffn_W1", "L0_ffn_W2")}
    b1 = a["L0_ffn_b1"]
    vectors = np.zeros((DEPTH, P, 9), np.float32)
    vectors[:, :, 0] = a["L0_ffn_ln_g"]
    vectors[:, :, 1] = a["L0_ffn_ln_b"]
    vectors[:, :, 2] = a["L0_ffn_b2"]
    for m, rows in enumerate(DIM):
        vectors[:, :rows, 3 + m] = b1[:, DI + P * m:DI + P * m + rows]
        vectors[:, :rows, 6 + m] = b1[:, P * m:P * m + rows]
    d["ffn_vectors"] = vectors
    q, k = a["L0_ffn_q_scale"], a["L0_ffn_k_scale"]
    d["ffn_scales"] = np.concatenate([q, k, np.roll(q, FD // 2, 1), np.roll(k, FD // 2, 1)], 1)
    for name in "rkvgo":
        d[f"a0_W_{name}"] = a[f"L0_attn_a_W_{name}"].T
    v = np.zeros((P, 16), np.float32)
    for k, name in enumerate("rkvg"):
        v[:, k] = a[f"L0_attn_a_time_mix_{name}"].reshape(C)
        v[:, 4 + k] = a[f"L0_attn_a_b_{name}"]
    v[:, 8], v[:, 9], v[:, 10] = a["L0_attn_a_b_o"], a["L0_attn_a_gn_weight"], a["L0_attn_a_gn_bias"]
    d["a0_vectors"] = v
    d["a0_heads"] = np.stack([np.tile(a[f"L0_attn_a_{n}"].reshape(-1), B) for n in ("decay", "eta")], 1)
    for name in ("za", "z", "ya", "y"):
        d[f"a1_W_{name}"] = a[f"L1_attn_a_W{name}"].T
    v = np.zeros((P, 8), np.float32)
    for k, name in enumerate(("bza", "bz", "bya", "by", "norm_w", "lc_re", "lc_im")):
        v[:, k] = a[f"L1_attn_a_{name}"]
    d["a1_vectors"] = v
    for name in ("Wq", "Wk", "Wv", "Wo", "Wff"):
        d[f"L1_ffn_{name}"] = a[f"L1_ffn_{name}"]
    for name in ("wq", "wk", "wv", "wo"):
        d[f"b1_{name}"] = a[f"L1_attn_b_{name}"].T
    order = np.arange(C).reshape(16, 4, 2).transpose(0, 2, 1).reshape(-1)
    swapped = order.reshape(16, 2, 4)[:, ::-1].reshape(-1)
    Wq, bq = a["L0_attn_b_Wq"].reshape(C, 4, C), a["L0_attn_b_bq"].reshape(4, C)
    d["b0_Wq"] = np.stack([Wq[:, :, order], Wq[:, :, swapped]], 2).reshape(C, 8 * C)
    Wk, bk = a["L0_attn_b_Wk"], a["L0_attn_b_bk"]
    d["b0_Wk"] = np.concatenate([Wk[:, order], Wk[:, swapped]], 1)
    v = np.zeros((P, 16), np.float32)
    v[:, 0:8] = np.stack([bq[:, order], bq[:, swapped]], 1).reshape(8, C).T
    v[:, 8], v[:, 9], v[:, 10] = bk[order], bk[swapped], a["L0_attn_b_bo"]
    d["b0_vectors"] = v
    by_head = lambda m: m.reshape(-1, 4, 16, 8).transpose(0, 2, 1, 3).reshape(-1, 4 * C)
    d["b0_Wv"], d["b0_bv"], d["b0_nulls"] = by_head(a["L0_attn_b_Wv"]), by_head(a["L0_attn_b_bv"]), by_head(a["L0_attn_b_v_nulls"])
    d["b0_sinks"] = a["L0_attn_b_sink_scalars"].reshape(4, 16).T.reshape(1, 64)
    d["L0_attn_b_Wo"] = a["L0_attn_b_Wo"]
    d.update(shape_constants())
    return {k: np.ascontiguousarray(v) for k, v in d.items()}


def kernel(**inputs):
    from concourse import bacc
    from concourse.bass_utils import run_bass_kernel_spmd

    nc = bacc.Bacc("TRN2", target_bir_lowering=False, num_devices=1)
    arrays = {f"in_{k}": v for k, v in laid_out(inputs).items()}
    d = {k[3:]: nc.dram_tensor(k, v.shape, mybir.dt.from_np(v.dtype), kind="ExternalInput").ap()
         for k, v in arrays.items()}
    out = nc.dram_tensor("out_x", (B, T, C), F32, kind="ExternalOutput").ap()
    program(nc, d, out)
    return run_bass_kernel_spmd(nc, [arrays], core_ids=[0]).results[0]["out_x"]
```
